# Optimizing a Trainium2 kernel written in Bass

```python
import numpy as np
import jax
import jax.numpy as jnp

def _softmax(x, axis=-1):
    return jax.nn.softmax(x, axis=axis)

def _gelu(x):
    return jax.nn.gelu(x, approximate=True)

def _silu(x):
    return jax.nn.silu(x)

def _sigmoid(x):
    return jax.nn.sigmoid(x)

def _layernorm(x, axis=-1, eps=1e-05):
    m = jnp.mean(x, axis=axis, keepdims=True)
    v = jnp.var(x, axis=axis, keepdims=True)
    return (x - m) / jnp.sqrt(v + eps)

def _scatter_add(tgt, idx, src, axis=0):
    return tgt.at[idx].add(src)

def _segment_sum(src, seg, n):
    return jax.ops.segment_sum(src, seg, n)
kernel_name = 'mk_lm_tower_d1_tok_ids1024_r4_7cb979'

def setup_inputs(seed: int=0):
    np.random.seed(seed)
    _w = jnp.asarray

    def _rec_inputs():
        import jax
        import jax.numpy as jnp
        _rk = jax.random.key(seed)
        x = jax.random.randint(jax.random.fold_in(_rk, 1), (32, 128), 0, 200, jnp.int32)
        return x
    x = _rec_inputs()

    def _L0_tok_setup():
        import jax, jax.numpy as jnp
        import numpy as np
        NUM_LEVELS = 32
        SCALE = 0.15
        OPEN_TOKENS = jnp.array([40, 91, 123], dtype=jnp.int32)
        CLOSE_TOKENS = jnp.array([41, 93, 125], dtype=jnp.int32)

        def _compute_levels(token_ids, num_levels):
            is_open = (token_ids[..., None] == OPEN_TOKENS).any(-1)
            is_close = (token_ids[..., None] == CLOSE_TOKENS).any(-1)
            delta = is_open.astype(jnp.int32) - is_close.astype(jnp.int32)

            def step(lvl, d):
                lvl = jnp.clip(lvl + d, 0, num_levels - 1)
                return (lvl, lvl)
            init = jnp.zeros(token_ids.shape[0], dtype=jnp.int32)
            _, levels = jax.lax.scan(step, init, delta.T)
            return levels.T
        key = jax.random.key(seed)
        k1, k2 = jax.random.split(key)
        token_ids = jax.random.randint(k1, (8, 2048), 0, 200, dtype=jnp.int32)
        level_emb = jax.random.normal(k2, (NUM_LEVELS, 256), dtype=jnp.float32)
        return {'token_ids': token_ids, 'level_emb': level_emb}
    _L0_tok_all = _L0_tok_setup()
    _L0_tok_in = {k: v for k, v in _L0_tok_all.items() if k in ('level_emb',)}
    del _L0_tok_all

    def _L0_attn_setup():
        import jax, jax.numpy as jnp
        import numpy as np
        HIDDEN = 256
        STATE = 16
        BATCH = 4
        SEQ = 512
        LN_EPS = 1e-05

        def _selective_scan(x_ssm, dt, A, Bm, Cm):
            Bsz, L, D = x_ssm.shape
            N = A.shape[1]

            def step(h, inp):
                xt, dtt, bt, ct = inp
                dA = jnp.exp(A[None] * dtt[..., None])
                dB = dtt[..., None] * bt[:, None, :]
                h = dA * h + dB * xt[..., None]
                y = jnp.sum(h * ct[:, None, :], axis=-1)
                return (h, y)
            h0 = jnp.zeros((Bsz, D, N), x_ssm.dtype)
            xs = (jnp.swapaxes(x_ssm, 0, 1), jnp.swapaxes(dt, 0, 1), jnp.swapaxes(Bm, 0, 1), jnp.swapaxes(Cm, 0, 1))
            _, ys = jax.lax.scan(step, h0, xs)
            return jnp.swapaxes(ys, 0, 1)
        key = jax.random.key(seed)
        ks = jax.random.split(key, 16)
        D, N = (HIDDEN, STATE)
        s = 0.02
        return {'x': jax.random.normal(ks[0], (BATCH, SEQ, D), dtype=jnp.float32), 'w_in': jax.random.normal(ks[1], (2 * D, D), dtype=jnp.float32) * s, 'b_in': jnp.zeros((2 * D,), jnp.float32), 'w_dt': jax.random.normal(ks[2], (D, D), dtype=jnp.float32) * s, 'b_dt': jnp.zeros((D,), jnp.float32), 'A_log': jax.random.normal(ks[3], (D, N), dtype=jnp.float32), 'w_B': jax.random.normal(ks[4], (N, D), dtype=jnp.float32) * s, 'b_B': jnp.zeros((N,), jnp.float32), 'w_C': jax.random.normal(ks[5], (N, D), dtype=jnp.float32) * s, 'b_C': jnp.zeros((N,), jnp.float32), 'D': jnp.ones((D,), jnp.float32), 'w_out': jax.random.normal(ks[6], (D, D), dtype=jnp.float32) * s, 'b_out': jnp.zeros((D,), jnp.float32), 'gamma': jnp.ones((D,), jnp.float32), 'beta': jnp.zeros((D,), jnp.float32)}
    _L0_attn_all = _L0_attn_setup()
    _L0_attn_in = {k: v for k, v in _L0_attn_all.items() if k in ('w_in', 'b_in', 'w_dt', 'b_dt', 'A_log', 'w_B', 'b_B', 'w_C', 'b_C', 'D', 'w_out', 'b_out', 'gamma', 'beta')}
    del _L0_attn_all

    def _L0_ffn_setup():
        import jax, jax.numpy as jnp
        import numpy as np
        HID, FFN, E, K = (256, 1024, 8, 2)
        CAP_FACTOR = 1.25
        key = jax.random.key(seed)
        k1, k2, k3, k4 = jax.random.split(key, 4)
        B, T = (4, 512)
        x = jax.random.normal(k1, (B, T, HID), dtype=jnp.float32)
        router_w = jax.random.normal(k2, (E, HID), dtype=jnp.float32) * 0.02
        w1 = jax.random.normal(k3, (E, HID, FFN), dtype=jnp.float32) * 0.02
        w2 = jax.random.normal(k4, (E, FFN, HID), dtype=jnp.float32) * 0.02
        return {'x': x, 'router_w': router_w, 'w1': w1, 'w2': w2}
    _L0_ffn_all = _L0_ffn_setup()
    _L0_ffn_in = {k: v for k, v in _L0_ffn_all.items() if k in ('router_w', 'w1', 'w2')}
    del _L0_ffn_all
    return {'x': x, 'L0_tok_level_emb': _L0_tok_in['level_emb'], 'L0_attn_w_in': _L0_attn_in['w_in'], 'L0_attn_b_in': _L0_attn_in['b_in'], 'L0_attn_w_dt': _L0_attn_in['w_dt'], 'L0_attn_b_dt': _L0_attn_in['b_dt'], 'L0_attn_A_log': _L0_attn_in['A_log'], 'L0_attn_w_B': _L0_attn_in['w_B'], 'L0_attn_b_B': _L0_attn_in['b_B'], 'L0_attn_w_C': _L0_attn_in['w_C'], 'L0_attn_b_C': _L0_attn_in['b_C'], 'L0_attn_D': _L0_attn_in['D'], 'L0_attn_w_out': _L0_attn_in['w_out'], 'L0_attn_b_out': _L0_attn_in['b_out'], 'L0_attn_gamma': _L0_attn_in['gamma'], 'L0_attn_beta': _L0_attn_in['beta'], 'L0_ffn_router_w': _L0_ffn_in['router_w'], 'L0_ffn_w1': _L0_ffn_in['w1'], 'L0_ffn_w2': _L0_ffn_in['w2']}

def reference(x, L0_tok_level_emb, L0_attn_w_in, L0_attn_b_in, L0_attn_w_dt, L0_attn_b_dt, L0_attn_A_log, L0_attn_w_B, L0_attn_b_B, L0_attn_w_C, L0_attn_b_C, L0_attn_D, L0_attn_w_out, L0_attn_b_out, L0_attn_gamma, L0_attn_beta, L0_ffn_router_w, L0_ffn_w1, L0_ffn_w2):
    import jax
    import jax.numpy as jnp

    def _L0_tok_ref(token_ids, level_emb):
        import jax, jax.numpy as jnp
        import numpy as np
        NUM_LEVELS = 32
        SCALE = 0.15
        OPEN_TOKENS = jnp.array([40, 91, 123], dtype=jnp.int32)
        CLOSE_TOKENS = jnp.array([41, 93, 125], dtype=jnp.int32)

        def _compute_levels(token_ids, num_levels):
            is_open = (token_ids[..., None] == OPEN_TOKENS).any(-1)
            is_close = (token_ids[..., None] == CLOSE_TOKENS).any(-1)
            delta = is_open.astype(jnp.int32) - is_close.astype(jnp.int32)

            def step(lvl, d):
                lvl = jnp.clip(lvl + d, 0, num_levels - 1)
                return (lvl, lvl)
            init = jnp.zeros(token_ids.shape[0], dtype=jnp.int32)
            _, levels = jax.lax.scan(step, init, delta.T)
            return levels.T
        levels = _compute_levels(token_ids, NUM_LEVELS)
        hierarchy_pos = level_emb[levels]
        return hierarchy_pos * SCALE

    def _L0_attn_ref(x, w_in, b_in, w_dt, b_dt, A_log, w_B, b_B, w_C, b_C, D, w_out, b_out, gamma, beta):
        import jax, jax.numpy as jnp
        import numpy as np
        HIDDEN = 256
        STATE = 16
        BATCH = 4
        SEQ = 512
        LN_EPS = 1e-05

        def _selective_scan(x_ssm, dt, A, Bm, Cm):
            Bsz, L, D = x_ssm.shape
            N = A.shape[1]

            def step(h, inp):
                xt, dtt, bt, ct = inp
                dA = jnp.exp(A[None] * dtt[..., None])
                dB = dtt[..., None] * bt[:, None, :]
                h = dA * h + dB * xt[..., None]
                y = jnp.sum(h * ct[:, None, :], axis=-1)
                return (h, y)
            h0 = jnp.zeros((Bsz, D, N), x_ssm.dtype)
            xs = (jnp.swapaxes(x_ssm, 0, 1), jnp.swapaxes(dt, 0, 1), jnp.swapaxes(Bm, 0, 1), jnp.swapaxes(Cm, 0, 1))
            _, ys = jax.lax.scan(step, h0, xs)
            return jnp.swapaxes(ys, 0, 1)
        residual = x
        xz = x @ w_in.T + b_in
        x_ssm, z = jnp.split(xz, 2, axis=-1)
        z = jax.nn.silu(z)
        dt = jax.nn.softplus(x_ssm @ w_dt.T + b_dt)
        Bm = x_ssm @ w_B.T + b_B
        Cm = x_ssm @ w_C.T + b_C
        A = -jnp.exp(A_log)
        y = _selective_scan(x_ssm, dt, A, Bm, Cm)
        y = y + D[None, None, :] * x_ssm
        y = y * z
        y = y @ w_out.T + b_out
        pre = y + residual
        mu = jnp.mean(pre, axis=-1, keepdims=True)
        var = jnp.mean(jnp.square(pre - mu), axis=-1, keepdims=True)
        return (pre - mu) * jax.lax.rsqrt(var + LN_EPS) * gamma + beta

    def _L0_ffn_ref(x, router_w, w1, w2):
        import jax, jax.numpy as jnp
        import numpy as np
        HID, FFN, E, K = (256, 1024, 8, 2)
        CAP_FACTOR = 1.25
        B, T, H = x.shape
        N = B * T
        x_flat = x.reshape(N, H)
        C = max(1, int(CAP_FACTOR * N / E * K))
        logits = x_flat @ router_w.T
        probs = jax.nn.softmax(logits, axis=-1)
        top_v, top_i = jax.lax.top_k(probs, K)
        top_v = top_v / jnp.sum(top_v, axis=-1, keepdims=True)
        out = jnp.zeros_like(x_flat)
        for k in range(K):
            eid = top_i[:, k]
            gate = top_v[:, k]
            onehot = jax.nn.one_hot(eid, E, dtype=jnp.int32)
            pos = jnp.take_along_axis(jnp.cumsum(onehot, axis=0), eid[:, None], axis=1)[:, 0] - 1
            keep = pos < C
            slot = jnp.where(keep, eid * C + pos, E * C)
            buf = jnp.zeros((E * C + 1, H), dtype=x.dtype).at[slot].add(x_flat * keep[:, None].astype(x.dtype))
            expert_in = buf[:E * C].reshape(E, C, H)
            h = jax.nn.gelu(jnp.einsum('ech,ehf->ecf', expert_in, w1), approximate=False)
            y = jnp.einsum('ecf,efh->ech', h, w2)
            tok = y.reshape(E * C, H)[jnp.minimum(slot, E * C - 1)]
            out = out + tok * (gate * keep.astype(x.dtype))[:, None]
        return out.reshape(B, T, H)
    h = _L0_tok_ref(x, L0_tok_level_emb)
    h = h + _L0_attn_ref(_layernorm(h, axis=-1), L0_attn_w_in, L0_attn_b_in, L0_attn_w_dt, L0_attn_b_dt, L0_attn_A_log, L0_attn_w_B, L0_attn_b_B, L0_attn_w_C, L0_attn_b_C, L0_attn_D, L0_attn_w_out, L0_attn_b_out, L0_attn_gamma, L0_attn_beta)
    h = h + _L0_ffn_ref(_layernorm(h, axis=-1), L0_ffn_router_w, L0_ffn_w1, L0_ffn_w2)
    return h

_drawn_inputs = setup_inputs


def setup_inputs(seed=0):
    import zlib

    import numpy as np

    out = dict(_drawn_inputs(seed))
    spreads = {'L0_attn_b_in': (0.0, 0.792),
     'L0_attn_b_dt': (0.0, 0.8),
     'L0_attn_b_B': (0.0, 0.8),
     'L0_attn_b_C': (0.0, 0.8),
     'L0_attn_D': (1.0, 0.6),
     'L0_attn_b_out': (0.0, 0.8),
     'L0_attn_gamma': (1.0, 0.2),
     'L0_attn_beta': (0.0, 0.1)}
    factors = {'L0_attn_w_dt': 8.0, 'L0_attn_A_log': 8.0, 'L0_attn_w_B': 5.002, 'L0_attn_w_C': 8.0}
    for name, (base, spread) in spreads.items():
        noise = np.random.default_rng([zlib.crc32(name.encode()), seed]).standard_normal(out[name].shape)
        drawn = base * np.exp(spread * noise) if base else spread * noise
        out[name] = jnp.asarray(drawn.astype(out[name].dtype))
    for name, factor in factors.items():
        out[name] = (out[name] * factor).astype(out[name].dtype)
    return out
```

```python
import concourse.bass as bass
from concourse import mybir
from contextlib import ExitStack

BATCH, SEQ = 32, 128
NTOK = BATCH * SEQ
LEVELS = 32
HID = 256
STATE = 16
FFN = 1024
EXPERTS = 8
TOPK = 2
CAP = max(1, int(1.25 * NTOK / EXPERTS * TOPK))
TOK_SCALE = 0.15
EPS = 1e-5
P = 128

GCH = P // STATE
GROUPS = HID // GCH
CHUNK = 512
NCHUNK = NTOK // CHUNK
TILES = CHUNK // P
COPIES = 3 * LEVELS

TT = 256
REGION = TOPK * CAP
DUMMY_ROW = EXPERTS * REGION
FTILES = (TOPK * NTOK + EXPERTS * (TT - 1)) // TT
NROWS = DUMMY_ROW + TT
XW = HID + EXPERTS + 1
INIT_PARTS = 9
DROP = 1.0e6

X_UP = 16.0
W_UP = 64.0
H_UP = 16.0


def channel_order():
    order = []
    for half in range(2):
        for row in range(P):
            strip, block, e = row // 32, (row % 32) // GCH, row % GCH
            order.append(half * P + (4 * block + strip) * GCH + e)
    return order


def program(nc, x_tok, level_emb, w_inT, b_in, w_dtT, b_dt, a_log, w_BT, b_B, w_CT, b_C, d_skip,
            w_outT, b_out, gamma, beta, router_wT, w1, w2, out):
    f32, bf16, f16, i32 = mybir.dt.float32, mybir.dt.bfloat16, mybir.dt.float16, mybir.dt.int32
    ALU, ACT, AX = mybir.AluOpType, mybir.ActivationFunctionType, mybir.AxisListType

    ctx = ExitStack()
    with ctx:
        def sb(name, shape, dt=f32):
            return ctx.enter_context(nc.sbuf_tensor(name, shape, dt))

        def ps(name, shape, dt=f32):
            return ctx.enter_context(nc.psum_tensor(name, shape, dt))

        def sem(name):
            return ctx.enter_context(nc.semaphore(name))

        level_dram = nc.dram_tensor("level_scratch", [BATCH, SEQ], f32, kind="Internal").ap()
        rows_dram = nc.dram_tensor("dispatch_rows", [NROWS, XW], f32, kind="Internal").ap()

        WSEC = 2 * FFN
        weights = sb("weights", [P, EXPERTS * 4 * WSEC], f16)
        W1H, W1L, W2H, W2L = range(4)

        def wsec(e, which, at, n):
            return weights[:, bass.ds((e * 4 + which) * WSEC + at, n)]

        scratch = weights[:, 4 * 4 * WSEC:].bitcast(f32)
        T_N = HID * STATE
        expA = scratch[0:COPIES, 0:T_N]
        lev_all = scratch[0:COPIES, T_N:2 * T_N]
        tab_v = scratch[0:COPIES, 2 * T_N:3 * T_N]
        tab_h = scratch[0:COPIES, 3 * T_N:3 * T_N + T_N // 2].bitcast(bf16)

        arena_n = 17472 - FFN - CHUNK
        arena = sb("arena", [P, arena_n])
        used = [0, 0]

        def part(phase, n, dt=f32):
            words = n if dt in (f32, i32) else n // 2
            at = used[phase]
            used[phase] += words
            assert used[phase] <= arena_n
            a = arena[:, at:at + words]
            return a if dt == f32 else a.bitcast(dt)

        TA, TB, TC, TZ, TDX, TRB, THB = 0, T_N, 2 * T_N, 2 * T_N + P, 2 * T_N + P + HID, 2 * T_N + P + 2 * HID, 2 * T_N + P + 3 * HID
        NTAB = 2 * T_N + P + 4 * HID
        SMALL = NTAB - TC
        table = part(0, NTAB, bf16)[0:COPIES, :]
        onehot = part(0, NTOK, bf16)[0:COPIES, :]
        HRING, ARING = 8, 4
        h_all = part(0, HRING * CHUNK)
        a_all = part(0, ARING * CHUNK)
        c_sb = part(0, CHUNK)
        z_sb = part(0, CHUNK)
        v_sb = part(0, 2 * CHUNK)
        PIECE = FFN // 2
        PIECES = 8
        stage = part(0, 2 * PIECE)
        FR = 3
        x_in = [part(1, 2 * XW).rearrange("p (s w) -> p s w", s=2) for _ in range(FR)]
        x_T = [part(1, 2 * 2 * TT, f16).rearrange("p (l c t) -> p l c t", l=2, c=2) for _ in range(FR)]
        h_hi = [part(1, EXPERTS * TT, f16).rearrange("p (j t) -> p j t", j=8) for _ in range(FR)]
        h_lo = [part(1, EXPERTS * TT, f16).rearrange("p (j t) -> p j t", j=8) for _ in range(FR)]
        g_sb = [part(1, 2 * TT) for _ in range(4)]
        y_sb = [part(1, 2 * HID).rearrange("p (s n) -> p s n", s=2) for _ in range(FR)]

        def hslot(q):
            return h_all[:, (q % HRING) * CHUNK:(q % HRING + 1) * CHUNK]

        def aslot(q):
            return a_all[:, (q % ARING) * CHUNK:(q % ARING + 1) * CHUNK]

        rows4 = sb("rows4", [P, TILES, HID])
        x2T = v_sb[:, CHUNK:].rearrange("p (j c t) -> p j c t", j=2, c=2)
        payload = sb("payload", [P, TILES, XW])
        x_hi = payload[:, :, 0:HID].bitcast(f16)[:, :, 0:HID]
        x_lo = payload[:, :, 0:HID].bitcast(f16)[:, :, HID:2 * HID]
        bn6 = sb("bn6", [P, TILES, 6])
        mv = sb("mv", [P, TILES, 2])
        nrm = sb("nrm", [P, 4, TILES])
        carried = sb("carried", [P, 1])

        ident = sb("ident", [P, P])
        ident16 = sb("ident16", [P, P], f16)
        tri = sb("tri", [P, P], bf16)
        ones = sb("ones", [P, P], bf16)
        sel = sb("sel", [P, 4, 32])
        gamma_b = sb("gamma_b", [P, HID])
        wo = sb("wo", [P, 2, HID])
        rw = sb("rw", [P, 2, EXPERTS])
        segmask = sb("segmask", [P, TILES * EXPERTS])
        row_base = sb("row_base", [P, EXPERTS])
        tok_f = sb("tok_f", [P, TILES])
        init_row = scratch[:, 3 * T_N + T_N // 2:3 * T_N + T_N // 2 + 2 * XW].rearrange("p (s w) -> p s w", s=2)
        lvl_id = sb("lvl_id", [COPIES, 1])
        not_first = sb("not_first", [COPIES, 1])
        last_copy = sb("last_copy", [COPIES, 1])

        pro = weights[:, 3 * 4 * WSEC:4 * 4 * WSEC].bitcast(f32)
        pro_at = [0]

        def tmp(parts, *dims):
            n = 1
            for d in dims:
                n *= d
            at = pro_at[0]
            pro_at[0] += n
            assert pro_at[0] <= 2 * WSEC
            return pro[0:parts, at:at + n]

        xz = tmp(COPIES, 2 * HID)
        small = tmp(COPIES, SMALL)
        small_h = tmp(COPIES, SMALL // 2).bitcast(bf16)
        pro2 = weights[:, 2 * 4 * WSEC:3 * 4 * WSEC].bitcast(f32)
        pro_w = pro2[:, 0:2 * 2 * HID].rearrange("p (c n) -> p c n", c=2)
        NP = HID + 2 * STATE
        pro_p = pro2[:, 1024:1024 + 2 * NP].rearrange("p (c n) -> p c n", c=2)
        bin_b = pro2[0:COPIES, 1600:1600 + 2 * HID]
        bp_b = pro2[0:COPIES, 2112:2112 + NP]
        d_b = pro2[0:COPIES, 2400:2400 + HID]
        bo_b = pro2[0:COPIES, 2656:2656 + HID]
        be_b = pro2[0:COPIES, 2912:2912 + HID]
        dbc = pro2[0:COPIES, 3168:3168 + NP]
        rowsT = pro2[:, 3456:3456 + 2 * COPIES].rearrange("p (c m) -> p c m", c=2)
        sp = [weights[:, 1 * 4 * WSEC:2 * 4 * WSEC].bitcast(f32)[0:COPIES, k * HID:(k + 1) * HID] for k in range(10)]
        emb, h0, x0 = [
            weights[:, 0:4 * WSEC].bitcast(f32)[0:COPIES, k * HID:(k + 1) * HID] for k in range(13, 16)]
        lev = weights[:, 1 * 4 * WSEC:2 * 4 * WSEC].bitcast(f32)[0:BATCH, 10 * HID:10 * HID + 12 * SEQ]
        x_int = lev[:, 0:SEQ].bitcast(i32)
        x_f = lev[:, SEQ:2 * SEQ]
        acc = [lev[:, 2 * SEQ:3 * SEQ], lev[:, 3 * SEQ:4 * SEQ]]
        sc0, sc1, sc_o = lev[:, 4 * SEQ:6 * SEQ], lev[:, 6 * SEQ:8 * SEQ], lev[:, 8 * SEQ:10 * SEQ]
        lev_c = lev[:, 10 * SEQ:11 * SEQ]

        NE = EXPERTS
        lg = sb("lg", [P, TILES, NE])
        lg2 = sb("lg2", [P, TILES, NE])
        eq = sb("eq", [P, TILES, NE])
        cs = sb("cs", [P, TILES * NE])
        top = sb("top", [P, 3, TILES])
        hot = sb("hot", [P, TILES, 2, NE], bf16)
        dif = sb("dif", [P, TILES, NE])
        seen = sb("seen", [P, TILES + 1, 2 * NE])
        pos = sb("pos", [P, TILES, 2, NE])
        kept = sb("kept", [P, TILES, 2, NE])
        slot = sb("slot", [P, TILES, NE])
        mul1 = sb("mul1", [P, TILES, 2, NE])
        mul2 = sb("mul2", [P, TILES, 2, NE])
        red1 = sb("red1", [P, TILES, 2])
        red2 = sb("red2", [P, TILES, 2])
        drop = sb("drop", [P, TILES, 2])
        slot_i = sb("slot_i", [P, TILES, 2], i32)
        NT10 = REGION // TT
        FT = FTILES + 1
        thr = sb("thr", [1, NT10])
        tile_no = sb("tile_no", [1, FT])
        cnt = sb("cnt", [1, 2 * NE])
        n8 = sb("n8", [1, NE])
        gt = sb("gt", [1, NE, NT10])
        nt = sb("nt", [1, NE])
        one8 = sb("one8", [1, NE])
        ntc = sb("ntc", [1, NE])
        le = stage[0:1, 0:FT * NE].rearrange("p (i e) -> p i e", e=NE)
        le2 = stage[0:1, FT * NE:2 * FT * NE].rearrange("p (i e) -> p i e", e=NE)
        ex = sb("ex", [1, FT])
        bel = sb("bel", [1, FT])
        rw1 = sb("rw1", [1, FT])
        rw2 = sb("rw2", [1, FT])
        tile_expert = sb("tile_expert", [1, FT], i32)
        tile_row = sb("tile_row", [1, FT], i32)
        tgate = [part(1, 2) for k in range(FR)]
        gate = [part(1, 2) for k in range(FR)]
        tok_i = [part(1, 2, i32) for k in range(FR)]

        bank = [ps(f"bank{k}", [P, CHUNK]) for k in range(4)]
        xbank, bbank = bank[0:2], bank[2:4]
        ybank = ps("ybank", [P, CHUNK])
        pre = ps("pre", [P, TILES * HID])
        misc = ps("misc", [P, CHUNK])
        logit_ps = misc[:, 0:TILES * NE].rearrange("p (j e) -> p j e", e=NE)
        cnt1_ps, cnt2_ps = misc[:, 64:128], misc[:, 128:192]
        xTp16 = misc[:, :].bitcast(f16).rearrange("p (l c t) -> p l c t", l=2, c=2)
        yb = [ybank, pre[:, 0:CHUNK], pre[:, CHUNK:2 * CHUNK]]

        ld_tok, ld_emb, ld_w, ld_p, ld_a, ld_d, ld_g = [sem(f"ld_{k}") for k in ("tok", "emb", "w", "p", "a", "d", "g")]
        consts = sem("consts")
        consts2 = sem("consts2")
        rows_init = sem("rows_init")
        vstep = sem("vstep")
        lev_out, lev_back = sem("lev_out"), sem("lev_back")
        p_var, p_std, p_x0, p_x0T, p_x0Ts, p_xz, p_xzs, p_xsT, p_xsTs, p_dbc, p_abs, p_exp = [
            sem(f"p_{k}") for k in ("var", "std", "x0", "x0T", "x0Ts", "xz", "xzs", "xsT", "xsTs", "dbc", "abs", "exp")]
        p_zc, p_ez, p_eA, p_arg, p_v, p_hi, p_r, p_mid, p_tab, p_hot = [
            sem(f"p_{k}") for k in ("zc", "ez", "eA", "arg", "v", "hi", "r", "mid", "tab", "hot")]
        x_ready, x_copied, b_ready, scan_done = sem("x_ready"), sem("x_copied"), sem("b_ready"), sem("scan_done")
        mul_v, mul_p, sum_done, v_done = sem("mul_v"), sem("mul_p"), sem("sum_done"), sem("v_done")
        pre_ready, hb_ready, var1, std1, nrm1, t1_ready, h_ready = [
            sem(k) for k in ("pre_ready", "hb_ready", "var1", "std1", "nrm1", "t1_ready", "h_ready")]
        var2, std2, nrm2, x2_ready, hi_ready, lo_ready, xT_ready, xT_copied, logit_ready = [
            sem(k) for k in ("var2", "std2", "nrm2", "x2_ready", "hi_ready", "lo_ready", "xT_ready", "xT_copied", "logit_ready")]
        hot_ready, cnt_ready, route_done, scattered, h_stored = [
            sem(k) for k in ("hot_ready", "cnt_ready", "route_done", "scattered", "h_stored")]
        w_loaded = [sem("w_loaded0"), sem("w_loaded1")]
        w_hi, w_lo = sem("w_hi"), sem("w_lo")
        tiles_ready, scan_phase_over = sem("tiles_ready"), sem("scan_phase_over")
        f_in = [sem(f"f_in{k}") for k in range(FR)]
        f_tp, f_xT, f_h, f_g, f_hi, f_lo, f_y, f_tg, f_gate, f_meta, f_ys, f_out = [
            sem(f"f_{k}") for k in ("tp", "xT", "h", "g", "hi", "lo", "y", "tg", "gate", "meta", "ys", "out")]

        XPER = GROUPS + 4

        def xpos(q):
            return q if q < 4 else (q + 2 if q < 18 else q + 3)

        C_POS, Z_POS = 4, (20, 35)
        VEC_MULS = [q for q in range(GROUPS) if q % 4 == 3]
        POOL_MULS = [q for q in range(GROUPS) if q not in VEC_MULS]

        def muls_before(group_list, q):
            return sum(1 for k in group_list if k < q)

        S_GATE, S_PROJECT, S_STATS1, S_NORM1, S_GAMMA, S_H = 5, 7, 9, 12, 15, 17
        S_STATS2, S_NORM2, S_LOW, S_CHOOSE, S_PLACE = 18, 20, 24, 28, 31
        A_STD1, A_NORM1, A_STD2, A_NORM2, A_TURNED = 13, 14, 21, 22, (26, 28)
        T_BASE, T_TURN, T_LOGITS, T_COUNT = 17, 24, (27, 29), 31

        def piece_slot(k):
            return 2 + 3 * k

        def wait(eng, s, n):
            if not isinstance(n, int) or n > 0:
                eng.wait_ge(s, n)

        def chunks(eng, body):
            body(0, False, True)
            body(1, True, True)
            with eng.Fori(2, NCHUNK) as c:
                body(c, True, True)
            body(NCHUNK, True, False)

        def ahead(m, u, k):
            return FR * (m + (u + k) // FR) + (u + k) % FR, (u + k) % FR, m + (u + k) // FR

        block = ctx.enter_context(nc.Block())

        @block.sync
        def _(sp_):
            dma = sp_.dma_start
            dma(x_int, x_tok).then_inc(ld_tok, 16)
            for k in range(3):
                dma(emb[k * LEVELS:(k + 1) * LEVELS, :], level_emb).then_inc(ld_emb, 16)
            dma(pro_w, w_inT.rearrange("(c p) n -> p c n", p=P)).then_inc(ld_w, 16)
            dma(bin_b, b_in.partition_broadcast(COPIES)).then_inc(ld_w, 16)
            dma(pro_p[:, :, 0:HID], w_dtT.rearrange("(c p) n -> p c n", p=P)).then_inc(ld_p, 16)
            dma(pro_p[:, :, HID:HID + STATE], w_BT.rearrange("(c p) n -> p c n", p=P)).then_inc(ld_p, 16)
            dma(pro_p[:, :, HID + STATE:NP], w_CT.rearrange("(c p) n -> p c n", p=P)).then_inc(ld_p, 16)
            dma(bp_b[:, 0:HID], b_dt.partition_broadcast(COPIES)).then_inc(ld_p, 16)
            dma(bp_b[:, HID:HID + STATE], b_B.partition_broadcast(COPIES)).then_inc(ld_p, 16)
            dma(bp_b[:, HID + STATE:NP], b_C.partition_broadcast(COPIES)).then_inc(ld_p, 16)
            dma(expA, a_log.rearrange("d n -> (d n)").partition_broadcast(COPIES)).then_inc(ld_a, 16)
            sp_.wait_ge(p_hot, 1)
            dma(level_dram, lev_c).then_inc(lev_out, 16)
            sp_.wait_ge(lev_out, 16)
            dma(lev_all, level_dram.rearrange("b t -> (b t)").partition_broadcast(COPIES)).then_inc(lev_back, 16)
            dma(d_b, d_skip.partition_broadcast(COPIES)).then_inc(ld_d, 16)
            dma(bo_b, b_out.partition_broadcast(COPIES)).then_inc(ld_d, 16)
            dma(be_b, beta.partition_broadcast(COPIES)).then_inc(ld_d, 16)
            dma(gamma_b[:, :], gamma.partition_broadcast(P)).then_inc(ld_g, 16)
            dma(wo[:, :, :], w_outT.rearrange("(c p) n -> p c n", p=P)).then_inc(ld_g, 16)
            dma(rw[:, :, :], router_wT.rearrange("(c p) n -> p c n", p=P)).then_inc(ld_g, 16)
            sp_.wait_ge(consts2, 1)
            blk = NROWS // TT // INIT_PARTS
            for k in range(INIT_PARTS):
                view = rows_dram[k * blk * TT:(k + 1) * blk * TT, :].rearrange("(t s p) w -> s p t w", p=P, s=2)
                for s in range(2):
                    dma(view[s], init_row[:, s:s + 1, :].to_broadcast([P, blk, XW])).then_inc(rows_init, 16)
            dma(out[NTOK:NTOK + TT, :].rearrange("(s p) n -> p s n", p=P), init_row[:, :, 0:HID]).then_inc(rows_init, 16)

            def load_piece(c, k):
                wait(sp_, w_lo, PIECES * c + k - 1)
                dst = stage[:, (k % 2) * PIECE:(k % 2 + 1) * PIECE]
                if k < 4:
                    src = w1[bass.ds(c, 1), (k // 2) * P:(k // 2 + 1) * P, (k % 2) * PIECE:(k % 2 + 1) * PIECE]
                    dma(dst, src.rearrange("e p n -> p (e n)")).then_inc(w_loaded[k % 2], 16)
                else:
                    src = w2[bass.ds(c, 1), (k - 4) * 2 * P:(k - 3) * 2 * P, :].rearrange("e (j p) n -> p (e j) n", p=P)
                    dma(dst.rearrange("p (j n) -> p j n", j=2), src).then_inc(w_loaded[k % 2], 16)

            def store_h(cp):
                sp_.wait_ge(h_ready, cp + 1)
                dma(out[bass.ds(cp * CHUNK, CHUNK), :].rearrange("(j p) n -> p j n", p=P), rows4[:, :, :]).then_inc(h_stored, 16)

            def body(c, prev, main):
                for q in range(GROUPS):
                    if main:
                        for k in range(PIECES):
                            if q == max(piece_slot(k - 2), 0):
                                load_piece(c, k)
                    if prev and q == S_H:
                        store_h(c - 1)

            chunks(sp_, body)

            sp_.wait_ge(scattered, 16 * 2 * TILES * NCHUNK)
            sp_.wait_ge(tiles_ready, 1)
            sp_.wait_ge(scan_phase_over, 4)

            def load_x(i, s, first):
                if not first:
                    sp_.wait_ge(f_tp, i - FR + 1)
                    sp_.wait_ge(f_meta, i - FR + 1)
                row = sp_.value_load(tile_row[0:1, bass.ds(i, 1)], min_val=0, max_val=DUMMY_ROW)
                dma(x_in[s], rows_dram[bass.ds(row, TT), :].rearrange("(s p) w -> p s w", p=P)).then_inc(f_in[s], 16)

            for i in range(FR):
                load_x(i, i, True)
            with sp_.Fori(1, FTILES // FR) as m:
                for u in range(FR):
                    load_x(FR * m + u, u, False)

        @block.gpsimd
        def _(pool):
            g = nc.gpsimd
            n = [0]

            def link(ins):
                ins.then_inc(consts, 1)
                n[0] += 1
                pool.wait_ge(consts, n[0])

            def diag(t, last=False):
                link(g.memset(t[:, :], 0.0))
                link(g.affine_select(out=t[:, :], in_=t[:, :], compare_op=ALU.not_equal, fill=1.0, base=0,
                                     pattern=[[-1, P]], channel_multiplier=1))

            for k in range(3):
                link(g.iota(lvl_id[k * LEVELS:(k + 1) * LEVELS, :], pattern=[[0, 1]], base=0, channel_multiplier=1,
                            allow_small_or_imprecise_dtypes=True))
                link(g.memset(not_first[k * LEVELS:(k + 1) * LEVELS, :], 0.0 if k == 0 else -1.0))
                link(g.memset(last_copy[k * LEVELS:(k + 1) * LEVELS, :], -1.0 if k == 2 else 0.0))
            diag(ident)
            diag(ident16)
            link(g.memset(tri[:, :], 1.0))
            link(g.affine_select(out=tri[:, :], in_=tri[:, :], compare_op=ALU.is_ge, fill=0.0, base=0,
                                 pattern=[[1, P]], channel_multiplier=-1))
            link(g.memset(ones[:, :], 1.0))
            link(g.memset(sel[:, :, :], 1.0))
            link(g.affine_select(out=sel[:, :, :], in_=sel[:, :, :], compare_op=ALU.is_ge, fill=0.0, base=0,
                                 pattern=[[STATE * GCH, 4], [-STATE, 32]], channel_multiplier=1))
            link(g.affine_select(out=sel[:, :, :], in_=sel[:, :, :], compare_op=ALU.is_ge, fill=0.0, base=STATE - 1,
                                 pattern=[[-STATE * GCH, 4], [STATE, 32]], channel_multiplier=-1))
            link(g.memset(segmask[:, :], 1.0))
            link(g.memset(segmask[:, :].rearrange("p (j e) -> p j e", e=NE)[:, :, 0:1], 0.0))
            link(g.iota(row_base[:, :], pattern=[[REGION, NE]], base=-1, channel_multiplier=0,
                        allow_small_or_imprecise_dtypes=True))
            link(g.iota(tok_f[:, :], pattern=[[P, TILES]], base=-CHUNK, channel_multiplier=1,
                        allow_small_or_imprecise_dtypes=True))
            link(g.memset(seen[:, 0, :], 0.0))
            link(g.memset(one8[:, :], 1.0))
            link(g.iota(thr[:, :], pattern=[[TT, NT10]], base=0, channel_multiplier=0,
                        allow_small_or_imprecise_dtypes=True))
            link(g.iota(tile_no[:, :], pattern=[[1, FT]], base=0, channel_multiplier=0,
                        allow_small_or_imprecise_dtypes=True))
            link(g.memset(a_all.rearrange("p (s t) -> p s t", t=SEQ)[:, :, 0:1], 0.0))
            link(g.memset(init_row[:, :, :], 0.0))
            link(g.iota(init_row[:, :, XW - 1:XW].bitcast(i32), pattern=[[P, 2], [0, 1]], base=NTOK, channel_multiplier=1))
            pool.drain().then_inc(consts2, 1)

            last_row, last_sum = pool.to_reg(DUMMY_ROW - 1), pool.to_reg(NTOK + TT - 1)

            rows_sent, sums_sent = pool.alloc_register("rows_sent"), pool.alloc_register("sums_sent")
            pool.reg_mov(rows_sent, 0)
            pool.reg_mov(sums_sent, 0)

            def mul(c, q):
                pool.wait_ge(scan_done, GROUPS * c + q + 1)
                if q == POOL_MULS[0]:
                    pool.wait_ge(x_copied, XPER * c + C_POS + 2)
                g.tensor_tensor(hslot(q), hslot(q), c_sb, ALU.mult).then_inc(mul_p, 1)

            def body(c, prev, main):
                if main:
                    for q in POOL_MULS:
                        mul(c, q)
                if prev:
                    cp = c - 1
                    pool.wait_ge(route_done, cp + 1)
                    pool.reg_add(rows_sent, rows_sent, 16 * TOPK * TILES)
                    pool.wait_ge(rows_init, 16 * (2 * INIT_PARTS + 1))
                    for j in range(TILES):
                        for k in range(TOPK):
                            g.indirect_dma_start(
                                out=rows_dram, out_offset=bass.IndirectOffsetOnAxis(slot_i[:, j, k:k + 1], 0),
                                in_=payload[:, j, :], in_offset=None, bounds_check=last_row,
                                oob_is_err=False).then_inc(scattered, 16)

            chunks(pool, body)
            pool.drain().then_inc(scan_phase_over, 1)

            def step(m, u):
                i, s, _ = ahead(m, u, 0)
                pool.wait_ge(f_ys, i + 1)
                pool.wait_ge(f_meta, i + 1)
                if not isinstance(i, int) or i > 0:
                    pool.wait_ge(f_out, sums_sent)
                pool.reg_add(sums_sent, sums_sent, 32)
                pool.wait_ge(h_stored, 16 * NCHUNK)
                for k in range(2):
                    g.indirect_dma_start(
                        out=out, out_offset=bass.IndirectOffsetOnAxis(tok_i[s][:, k:k + 1], 0),
                        in_=y_sb[s][:, k, :], in_offset=None, compute_op=ALU.add,
                        bounds_check=last_sum, oob_is_err=True).then_inc(f_out, 16)

            for u in range(FR):
                step(0, u)
            with pool.Fori(1, FTILES // FR) as m:
                for u in range(FR):
                    step(m, u)
            pool.wait_ge(scattered, rows_sent)
            pool.wait_ge(f_out, sums_sent)

        @block.scalar
        def _(act):
            A = nc.scalar.activation
            act.wait_ge(p_var, 1)
            A(nrm[0:COPIES, 1, 0:1], nrm[0:COPIES, 0, 0:1], ACT.Sqrt).then_inc(p_std, 1)
            act.wait_ge(ld_a, 16)
            A(expA, expA, ACT.Exp).then_inc(p_eA, 1)
            act.wait_ge(p_zc, 1)
            A(sp[8], sp[8], ACT.Exp).then_inc(p_ez, 1)
            act.wait_ge(p_abs, 1)
            A(sp[1], sp[0], ACT.Exp, scale=-1.0).then_inc(p_exp, 1)

            def split(k, v, hi):
                act.wait_ge(p_v, k + 1)
                A(hi, v, ACT.Copy).then_inc(p_hi, 1)
                act.wait_ge(p_r, k + 1)
                A(hi, v, ACT.Copy).then_inc(p_mid, 1)

            split(0, small, small_h)
            act.wait_ge(p_arg, 1)
            A(tab_v, tab_v, ACT.Exp, scale=-1.0).then_inc(p_v, 1)
            split(1, tab_v, tab_h)
            split(2, tab_v, tab_h)

            def copy_decay(c, q):
                act.wait_ge(x_ready, XPER * c + xpos(q) + 1)
                wait(act, scan_done, GROUPS * c + q - (ARING - 1))
                dst = aslot(q).rearrange("p (b t) -> p b t", t=SEQ)[:, :, 1:]
                src = xbank[xpos(q) % 2][:, :].rearrange("p (b t) -> p b t", t=SEQ)[:, :, 1:]
                A(dst, src, ACT.Copy).then_inc(x_copied, 1)

            def copy_c(c):
                wait(act, mul_v, len(VEC_MULS) * c)
                wait(act, mul_p, len(POOL_MULS) * c)
                for k in range(2):
                    act.wait_ge(x_ready, XPER * c + C_POS + k + 1)
                    A(c_sb[:, k * TT:(k + 1) * TT], xbank[(C_POS + k) % 2][:, 0:TT], ACT.Copy).then_inc(x_copied, 1)

            def copy_z(c, half):
                act.wait_ge(x_ready, XPER * c + Z_POS[half] + 1)
                wait(act, v_done, 2 * c + half - 1)
                A(z_sb, xbank[Z_POS[half] % 2][:, :], ACT.Copy).then_inc(x_copied, 1)

            def weight_hi(c, k):
                act.wait_ge(w_loaded[k % 2], 16 * (PIECES // 2 * c + k // 2 + 1))
                which, at = (W1H, k * PIECE) if k < 4 else (W2H, (k - 4) * PIECE)
                A(wsec(c, which, at, PIECE), stage[:, (k % 2) * PIECE:(k % 2 + 1) * PIECE], ACT.Copy, scale=W_UP).then_inc(w_hi, 1)

            def end_op(cp, q):
                if q == A_STD1:
                    act.wait_ge(var1, cp + 1)
                    A(nrm[:, 1, :], nrm[:, 0, :], ACT.Sqrt).then_inc(std1, 1)
                if q == A_NORM1:
                    act.wait_ge(nrm1, cp + 1)
                    wait(act, xT_ready, cp)
                    wait(act, lo_ready, cp)
                if q in (A_NORM1, A_NORM1 + 1):
                    for j in range(2 * (q - A_NORM1), 2 * (q - A_NORM1) + 2):
                        A(rows4[:, j, :], pre[:, j * HID:(j + 1) * HID], ACT.Identity, bias=nrm[:, 3, j:j + 1],
                          scale=nrm[:, 2, j:j + 1]).then_inc(t1_ready, 1)
                if q == A_STD2:
                    act.wait_ge(var2, cp + 1)
                    A(nrm[:, 1, :], nrm[:, 0, :], ACT.Sqrt).then_inc(std2, 1)
                if q == A_NORM2:
                    act.wait_ge(nrm2, cp + 1)
                    act.wait_ge(h_stored, 16 * (cp + 1))
                if q in (A_NORM2, A_NORM2 + 1):
                    for j in range(2 * (q - A_NORM2), 2 * (q - A_NORM2) + 2):
                        A(rows4[:, j, :], rows4[:, j, :], ACT.Identity, bias=nrm[:, 3, j:j + 1],
                          scale=nrm[:, 2, j:j + 1]).then_inc(x2_ready, 1)
                if q == A_NORM2 + 1:
                    act.wait_ge(x2_ready, TILES * cp + TILES)
                    wait(act, scattered, 16 * 2 * TILES * cp)
                    A(x_hi, rows4[:, :, :], ACT.Copy, scale=X_UP).then_inc(hi_ready, 1)
                for k in range(2):
                    if q == A_TURNED[k]:
                        act.wait_ge(xT_ready, cp + 1)
                        wait(act, logit_ready, 2 * cp + k)
                        A(x2T, pre[:, k * CHUNK:(k + 1) * CHUNK].rearrange("p (j c t) -> p j c t", j=2, c=2),
                          ACT.Copy).then_inc(xT_copied, 1)

            def body(c, prev, main):
                for q in range(GROUPS):
                    if main:
                        copy_decay(c, q)
                        if q == 3:
                            copy_c(c)
                        if q == 17:
                            copy_z(c, 0)
                        if q == 31:
                            copy_z(c, 1)
                        for k in range(PIECES):
                            if q == piece_slot(k) + 2:
                                weight_hi(c, k)
                    if prev:
                        end_op(c - 1, q)

            chunks(act, body)
            act.drain().then_inc(scan_phase_over, 1)
            act.wait_ge(scan_phase_over, 4)

            def take_x(i, s, m):
                act.wait_ge(f_in[s], 16 * (m + 1))
                e = act.value_load(tile_expert[0:1, bass.ds(i, 1)], min_val=0, max_val=NE - 1)
                wait(act, f_gate, i - FR + 1)
                A(tgate[s][:, :].unsqueeze(2), x_in[s][:, :, bass.ds(HID + e, 1)], ACT.Tanh, scale=0.5).then_inc(f_tg, 1)
                act.wait_ge(f_tp, i + 1)
                wait(act, f_h, 4 * (i - FR + 1))
                A(x_T[s], xTp16, ACT.Copy).then_inc(f_xT, 1)

            def activate(i, s):
                for b in range(4):
                    act.wait_ge(f_h, 4 * i + b + 1)
                    wait(act, f_lo, 4 * (i - 1) + b + 1)
                    A(g_sb[b], bank[b][:, :], ACT.Gelu, scale=1.0 / (X_UP * W_UP)).then_inc(f_g, 1)
                    act.wait_ge(f_g, 4 * i + b + 1)
                    if b == 0:
                        wait(act, f_y, i - FR + 1)
                    A(h_hi[s][:, 2 * b:2 * b + 2, :], g_sb[b].rearrange("p (j t) -> p j t", j=2), ACT.Copy,
                      scale=H_UP).then_inc(f_hi, 1)

            act.wait_ge(tiles_ready, 1)
            take_x(0, 0, 0)
            activate(0, 0)
            take_x(1, 1, 0)

            def step(m, u):
                i1, s1, _ = ahead(m, u, 1)
                i2, s2, m2 = ahead(m, u, 2)
                if not isinstance(m, int) or i1 < FTILES:
                    activate(i1, s1)
                if not isinstance(m, int) or i2 < FTILES:
                    take_x(i2, s2, m2)

            for u in range(FR):
                step(0, u)
            with act.Fori(1, FTILES // FR - 1) as m:
                for u in range(FR):
                    step(m, u)
            for u in range(FR):
                step(FTILES // FR - 1, u)

        @block.vector
        def _(dve):
            v = nc.vector
            n = [0]
            base = [0]

            def done(ins):
                ins.then_inc(vstep, 1)
                n[0] += 1

            def after():
                dve.wait_ge(vstep, base[0] + n[0])

            def link(ins):
                done(ins)
                after()

            dve.wait_ge(ld_tok, 16)
            link(v.tensor_copy(x_f, x_int))
            link(v.tensor_scalar(acc[0], x_f, 40.0, None, ALU.is_equal))
            link(v.scalar_tensor_tensor(acc[1], x_f, 91.0, acc[0], ALU.is_equal, ALU.add))
            link(v.scalar_tensor_tensor(acc[0], x_f, 123.0, acc[1], ALU.is_equal, ALU.add))
            link(v.scalar_tensor_tensor(acc[1], x_f, 41.0, acc[0], ALU.is_equal, ALU.subtract))
            link(v.scalar_tensor_tensor(acc[0], x_f, 93.0, acc[1], ALU.is_equal, ALU.add))
            link(v.memset(sc0, 0.0))
            link(v.memset(sc1, 0.0))
            ev = "p (t k) -> p t k"
            link(v.scalar_tensor_tensor(sc0.rearrange(ev, k=2)[:, :, 0], x_f, 125.0, acc[0], ALU.is_equal, ALU.add))
            link(v.memset(sc1.rearrange(ev, k=2)[:, :, 0], -float(LEVELS - 1)))
            link(v.tensor_tensor_scan(sc_o, sc0, sc1, 0.0, ALU.subtract, ALU.max))
            v.tensor_copy(lev_c, sc_o.rearrange(ev, k=2)[:, :, 1]).then_inc(p_hot, 1)

            dve.wait_ge(ld_emb, 48)
            link(v.tensor_scalar(h0[:, :], emb[:, :], TOK_SCALE, None, ALU.mult))
            link(v.bn_stats(bn6[0:COPIES, 0, :], h0[:, :]))
            link(v.bn_aggr(mv[0:COPIES, 0, :], bn6[0:COPIES, 0, :]))
            v.tensor_scalar(nrm[0:COPIES, 0, 0:1], mv[0:COPIES, 0, 1:2], EPS, None, ALU.add).then_inc(p_var, 1)
            dve.wait_ge(p_std, 1)
            link(v.reciprocal(nrm[0:COPIES, 2, 0:1], nrm[0:COPIES, 1, 0:1]))
            v.tensor_scalar(x0[:, :], h0[:, :], mv[0:COPIES, 0, 0:1], nrm[0:COPIES, 2, 0:1], ALU.subtract, ALU.mult).then_inc(p_x0, 1)
            dve.wait_ge(p_x0T, 1)
            v.tensor_copy(rowsT[:, :, :], misc[:, 0:2 * COPIES].rearrange("p (c m) -> p c m", c=2)).then_inc(p_x0Ts, 1)
            dve.wait_ge(p_xz, 1)
            dve.wait_ge(ld_w, 32)
            v.tensor_tensor(xz, ybank[0:COPIES, :], bin_b, ALU.add).then_inc(p_xzs, 1)
            dve.wait_ge(p_xzs, 1)
            xs, zz = xz[:, 0:HID], xz[:, HID:2 * HID]
            v.tensor_scalar(sp[8], zz, -1.0, 80.0, ALU.mult, ALU.min).then_inc(p_zc, 1)
            dve.wait_ge(p_xsT, 1)
            v.tensor_copy(rowsT[:, :, :], misc[:, 0:2 * COPIES].rearrange("p (c m) -> p c m", c=2)).then_inc(p_xsTs, 1)
            dve.wait_ge(p_ez, 1)
            link(v.tensor_scalar(sp[8], sp[8], 1.0, None, ALU.add))
            link(v.reciprocal(sp[9], sp[8]))
            S0 = TC
            link(v.tensor_tensor(small[:, TZ - S0:TZ - S0 + HID], zz, sp[9], ALU.mult))
            dve.wait_ge(ld_d, 48)
            for half in range(2):
                turned = "p (r m e) -> p m r e"
                cols = slice(half * P, (half + 1) * P)
                link(v.tensor_tensor(small[:, TDX - S0 + half * P:TDX - S0 + (half + 1) * P].rearrange(
                    "p (m r e) -> p m r e", m=4, r=4), d_b[:, cols].rearrange(turned, m=4, r=4),
                    xs[:, cols].rearrange(turned, m=4, r=4), ALU.mult))
            link(v.tensor_tensor(small[:, TRB - S0:TRB - S0 + HID], x0[:, :], bo_b, ALU.add))
            link(v.tensor_tensor(small[:, THB - S0:THB - S0 + HID], h0[:, :], be_b, ALU.add))
            dve.wait_ge(p_dbc, 1)
            dve.wait_ge(ld_p, 96)
            link(v.tensor_tensor(dbc, ybank[0:COPIES, 0:NP], bp_b, ALU.add))
            dtp, Bl, Cl = dbc[:, 0:HID], dbc[:, HID:HID + STATE], dbc[:, HID + STATE:NP]
            link(v.tensor_copy(small[:, 0:P].rearrange("p (e n) -> p e n", n=STATE),
                               Cl.unsqueeze(1).to_broadcast([COPIES, GCH, STATE])))
            v.scalar_tensor_tensor(sp[0], dtp, -1.0, dtp, ALU.mult, ALU.max).then_inc(p_abs, 1)
            dve.wait_ge(p_exp, 1)
            link(v.tensor_scalar(sp[2], sp[1], 2.0, None, ALU.add))
            link(v.reciprocal(sp[3], sp[2]))
            link(v.tensor_tensor(sp[4], sp[1], sp[3], ALU.mult))
            link(v.tensor_tensor(sp[5], sp[4], sp[4], ALU.mult))
            link(v.tensor_scalar(sp[6], sp[5], 1.0 / 17, None, ALU.mult))
            for k in range(7, 0, -1):
                link(v.scalar_tensor_tensor(sp[6], sp[6], 1.0 / (2 * k + 1), sp[5], ALU.add, ALU.mult))
            link(v.scalar_tensor_tensor(sp[6], sp[6], 1.0, sp[4], ALU.add, ALU.mult))
            link(v.tensor_scalar(sp[7], dtp, 0.0, None, ALU.max))
            link(v.scalar_tensor_tensor(sp[2], sp[6], 2.0, sp[7], ALU.mult, ALU.add))
            dt = sp[2]
            v.tensor_tensor(sp[3], dt, xs, ALU.mult).then_inc(p_v, 1)
            dve.wait_ge(p_v, 1)

            def parts(k, val, hi, dst):
                dve.wait_ge(p_hi, k + 1)
                v.scalar_tensor_tensor(val, hi, not_first[:, :], val, ALU.mult, ALU.add).then_inc(p_r, 1)
                dve.wait_ge(p_mid, k + 1)
                v.scalar_tensor_tensor(dst, hi, last_copy[:, :], val, ALU.mult, ALU.add).then_inc(p_tab, 1)

            dve.wait_ge(consts2, 1)
            grid = "p (d n) -> p d n"
            dve.wait_ge(p_eA, 1)
            v.tensor_tensor(tab_v.rearrange(grid, n=STATE), expA.rearrange(grid, n=STATE),
                            dt.unsqueeze(2).to_broadcast([COPIES, HID, STATE]), ALU.mult).then_inc(p_arg, 1)
            parts(0, small, small_h, table[:, TC:NTAB])
            dve.wait_ge(lev_back, 16)
            link(v.tensor_scalar(onehot, lev_all, lvl_id[:, :], None, ALU.is_equal))
            parts(1, tab_v, tab_h, table[:, TA:TA + T_N])
            dve.wait_ge(p_tab, 2)
            v.tensor_tensor(tab_v.rearrange(grid, n=STATE), sp[3].unsqueeze(2).to_broadcast([COPIES, HID, STATE]),
                            Bl.unsqueeze(1).to_broadcast([COPIES, HID, STATE]), ALU.mult).then_inc(p_v, 1)
            parts(2, tab_v, tab_h, table[:, TB:TB + T_N])
            dve.wait_ge(ld_g, 48)

            def scan(c, q):
                dve.wait_ge(x_copied, XPER * c + xpos(q) + 1)
                dve.wait_ge(b_ready, GROUPS * c + q + 1)
                if q % 4 == 0:
                    wait(dve, sum_done, 8 * c + q // 4 - 1)
                v.tensor_tensor_scan(hslot(q), aslot(q), bbank[q % 2][:, :], 0.0, ALU.mult, ALU.add).then_inc(scan_done, 1)

            def mul(c, q):
                dve.wait_ge(scan_done, GROUPS * c + q + 1)
                dve.wait_ge(x_copied, XPER * c + C_POS + 2)
                v.tensor_tensor(hslot(q), hslot(q), c_sb, ALU.mult).then_inc(mul_v, 1)

            def gate_z(c, half):
                dve.wait_ge(sum_done, 8 * c + 4 * half + 4)
                dve.wait_ge(x_copied, XPER * c + Z_POS[half] + 1)
                wait(dve, pre_ready, 4 * c)
                v.tensor_tensor(v_sb[:, half * CHUNK:(half + 1) * CHUNK], ybank[:, :],
                                z_sb, ALU.mult).then_inc(v_done, 1)

            def weight_lo(c, k):
                dve.wait_ge(w_hi, PIECES * c + k + 1)
                hi, lo, at = (W1H, W1L, k * PIECE) if k < 4 else (W2H, W2L, (k - 4) * PIECE)
                v.scalar_tensor_tensor(wsec(c, lo, at, PIECE), stage[:, (k % 2) * PIECE:(k % 2 + 1) * PIECE], W_UP,
                                       wsec(c, hi, at, PIECE), ALU.mult, ALU.subtract).then_inc(w_lo, 1)

            def stats(src, j):
                done(v.bn_stats(bn6[:, j, :], src))

            def variance(ready):
                after()
                done(v.tensor_copy(carried[:, :], bn6[:, 0, 0:1]))
                for j in range(TILES):
                    done(v.bn_aggr(mv[:, j, :], bn6[:, j, :]))
                after()
                v.tensor_scalar(nrm[:, 0, :], mv[:, :, 1], EPS, None, ALU.add).then_inc(ready, 1)

            def norm(ready):
                link(v.reciprocal(nrm[:, 2, :], nrm[:, 1, :]))
                v.scalar_tensor_tensor(nrm[:, 3, :], mv[:, :, 0], -1.0, nrm[:, 2, :], ALU.mult, ALU.mult).then_inc(ready, 1)

            def end_op(cp, q):
                for k in range(2):
                    if q == S_STATS1 + 2 * k:
                        dve.wait_ge(pre_ready, TILES * cp + 2 * k + 2)
                        for j in (2 * k, 2 * k + 1):
                            stats(pre[:, j * HID:(j + 1) * HID], j)
                        if k == 1:
                            variance(var1)
                    if q == S_STATS2 + k:
                        for j in (2 * k, 2 * k + 1):
                            stats(rows4[:, j, :], j)
                        if k == 1:
                            variance(var2)
                if q == S_NORM1:
                    dve.wait_ge(std1, cp + 1)
                    norm(nrm1)
                if q == S_GAMMA:
                    dve.wait_ge(t1_ready, TILES * cp + TILES)
                    done(v.tensor_tensor(rows4[:, :, :], rows4[:, :, :],
                                         gamma_b[:, :].unsqueeze(1).to_broadcast([P, TILES, HID]), ALU.mult))
                if q == S_H:
                    after()
                    dve.wait_ge(hb_ready, cp + 1)
                    flat = "p j n -> p (j n)"
                    done(v.tensor_tensor(rows4[:, 0:2, :].rearrange(flat), pre[:, 0:CHUNK],
                                         rows4[:, 0:2, :].rearrange(flat), ALU.add))
                    v.tensor_tensor(rows4[:, 2:4, :].rearrange(flat), pre[:, CHUNK:],
                                    rows4[:, 2:4, :].rearrange(flat), ALU.add).then_inc(h_ready, 1)
                    dve.wait_ge(h_ready, cp + 1)
                if q == S_NORM2:
                    dve.wait_ge(std2, cp + 1)
                    norm(nrm2)
                if q == S_LOW:
                    dve.wait_ge(hi_ready, cp + 1)
                    v.scalar_tensor_tensor(x_lo, rows4[:, :, :], X_UP, x_hi, ALU.mult, ALU.subtract).then_inc(lo_ready, 1)
                if q == S_CHOOSE:
                    route_choose(cp)
                if q == S_PLACE:
                    route_place(cp)

            def first_max(src, k):
                m = top[:, k, :]
                link(v.tensor_reduce(m, src, AX.X, ALU.max))
                link(v.tensor_tensor(eq[:, :, :], src, m.unsqueeze(2).to_broadcast([P, TILES, NE]), ALU.is_ge))
                link(v.tensor_tensor_scan(cs[:, :], segmask[:, :], eq[:, :, :].rearrange("p j e -> p (j e)"), 0.0,
                                          ALU.mult, ALU.add))
                return v.scalar_tensor_tensor(hot[:, :, k, :], cs[:, :].rearrange("p (j e) -> p j e", e=NE), 1.0,
                                              eq[:, :, :], ALU.is_equal, ALU.mult)

            def route_choose(cp):
                dve.wait_ge(logit_ready, 2 * cp + 2)
                link(v.tensor_copy(lg[:, :, :], logit_ps))
                link(first_max(lg[:, :, :], 0))
                link(v.scalar_tensor_tensor(lg2[:, :, :], hot[:, :, 0, :], -1.0e30, lg[:, :, :], ALU.mult, ALU.add))
                first_max(lg2[:, :, :], 1).then_inc(hot_ready, 1)
                dve.wait_ge(hot_ready, cp + 1)
                done(v.tensor_tensor(top[:, 2, :], top[:, 0, :], top[:, 1, :], ALU.subtract))
                link(v.tensor_tensor(dif[:, :, :], hot[:, :, 0, :], hot[:, :, 1, :], ALU.subtract))
                done(v.tensor_tensor(payload[:, :, HID:HID + NE], dif[:, :, :],
                                     top[:, 2, :].unsqueeze(2).to_broadcast([P, TILES, NE]), ALU.mult))
                link(v.tensor_scalar(tok_f[:, :], tok_f[:, :], float(CHUNK), None, ALU.add))
                done(v.tensor_copy(payload[:, :, XW - 1:XW].bitcast(i32), tok_f[:, :].unsqueeze(2)))

            def route_place(cp):
                dve.wait_ge(cnt_ready, cp + 1)
                for j in range(TILES):
                    link(v.tensor_tensor(seen[:, j + 1, :], cnt2_ps[:, j * 2 * NE:(j + 1) * 2 * NE], seen[:, j, :], ALU.add))
                flat = "p j k e -> p j (k e)"
                link(v.tensor_tensor(pos[:, :, :, :].rearrange(flat), cnt1_ps.rearrange("p (j f) -> p j f", j=TILES),
                                     seen[:, 0:TILES, :], ALU.add))
                done(v.tensor_copy(seen[:, 0, :], seen[:, TILES, :]))
                link(v.tensor_scalar(kept[:, :, :, :].rearrange(flat), pos[:, :, :, :].rearrange(flat), float(CAP), None, ALU.min))
                link(v.tensor_tensor(slot[:, :, :], kept[:, :, 0, :], kept[:, :, 1, :], ALU.add))
                link(v.tensor_tensor(slot[:, :, :], slot[:, :, :], row_base[:, :].unsqueeze(1).to_broadcast([P, TILES, NE]), ALU.add))
                done(v.tensor_tensor(mul2[:, :, :, :].rearrange(flat), hot[:, :, :, :].rearrange(flat),
                                     pos[:, :, :, :].rearrange(flat), ALU.mult))
                for k in range(2):
                    done(v.tensor_tensor(mul1[:, :, k, :], hot[:, :, k, :], slot[:, :, :], ALU.mult))
                after()
                done(v.tensor_reduce(red1[:, :, :], mul1[:, :, :, :], AX.X, ALU.add))
                link(v.tensor_reduce(red2[:, :, :], mul2[:, :, :, :], AX.X, ALU.add))
                link(v.tensor_scalar(drop[:, :, :], red2[:, :, :], float(CAP), DROP, ALU.is_gt, ALU.mult))
                v.tensor_tensor(slot_i[:, :, :], red1[:, :, :], drop[:, :, :], ALU.add).then_inc(route_done, 1)
                dve.wait_ge(route_done, cp + 1)

            def body(c, prev, main):
                for q in range(GROUPS):
                    if main:
                        scan(c, q)
                        for k in VEC_MULS:
                            if q == min(max(k, 4) + 1, GROUPS - 1):
                                mul(c, k)
                        for k in range(PIECES):
                            if q == piece_slot(k):
                                weight_lo(c, k)
                        if q == 21:
                            gate_z(c, 0)
                    if prev:
                        if q == S_GATE:
                            gate_z(c - 1, 1)
                        end_op(c - 1, q)

            body(0, False, True)
            before = n[0]
            body(1, True, True)
            per_chunk = n[0] - before
            with dve.Fori(2, NCHUNK) as c:
                base[0] = (c - 1) * per_chunk + before
                n[0] = 0
                body(c, True, True)
            n[0] = before + per_chunk * (NCHUNK - 1)
            base[0] = 0
            body(NCHUNK, True, False)

            link(v.tensor_scalar(cnt[:, :], seen[0:1, TILES, :], float(CAP), None, ALU.min))
            link(v.tensor_tensor(n8[:, :], cnt[:, 0:NE], cnt[:, NE:2 * NE], ALU.add))
            link(v.tensor_tensor(gt[:, :, :], n8[:, :].unsqueeze(2).to_broadcast([1, NE, NT10]),
                                 thr[:, :].unsqueeze(1).to_broadcast([1, NE, NT10]), ALU.is_gt))
            link(v.tensor_reduce(nt[:, :], gt[:, :, :], AX.X, ALU.add))
            link(v.tensor_tensor_scan(ntc[:, :], one8[:, :], nt[:, :], 0.0, ALU.mult, ALU.add))
            link(v.tensor_tensor(le[:, :, :], tile_no[:, :].unsqueeze(2).to_broadcast([1, FT, NE]), ntc[:, :].unsqueeze(1).to_broadcast([1, FT, NE]), ALU.is_ge))
            link(v.tensor_tensor(le2[:, :, :], le[:, :, :], nt[:, :].unsqueeze(1).to_broadcast([1, FT, NE]), ALU.mult))
            link(v.tensor_reduce(ex[:, :], le[:, :, :], AX.X, ALU.add))
            link(v.tensor_reduce(bel[:, :], le2[:, :, :], AX.X, ALU.add))
            link(v.tensor_tensor(rw1[:, :], tile_no[:, :], bel[:, :], ALU.subtract))
            link(v.tensor_scalar(rw2[:, :], ex[:, :], float(REGION), None, ALU.mult))
            link(v.scalar_tensor_tensor(bel[:, :], rw1[:, :], float(TT), rw2[:, :], ALU.mult, ALU.add))
            link(v.tensor_scalar(tile_row[:, :], bel[:, :], float(DUMMY_ROW), None, ALU.min))
            v.tensor_scalar(tile_expert[:, :], ex[:, :], float(NE - 1), None, ALU.min).then_inc(tiles_ready, 1)
            dve.drain().then_inc(scan_phase_over, 1)
            dve.wait_ge(scan_phase_over, 4)

            def low_half(i, s):
                for b in range(4):
                    dve.wait_ge(f_hi, 4 * i + b + 1)
                    if b == 0:
                        wait(dve, f_y, i - FR + 1)
                    pair = "p (j t) -> p j t"
                    v.scalar_tensor_tensor(h_lo[s][:, 2 * b:2 * b + 2, :], g_sb[b].rearrange(pair, j=2), H_UP,
                                           h_hi[s][:, 2 * b:2 * b + 2, :], ALU.mult, ALU.subtract).then_inc(f_lo, 1)

            def meta(i, s, m):
                back = 0.5 / (H_UP * W_UP)
                dve.wait_ge(f_tg, i + 1)
                wait(dve, f_ys, i - FR + 1)
                v.tensor_scalar(gate[s][:, :], tgate[s][:, :], back, back, ALU.mult, ALU.add).then_inc(f_gate, 1)
                dve.wait_ge(f_in[s], 16 * (m + 1))
                wait(dve, f_out, 32 * (i - FR + 1))
                v.tensor_copy(tok_i[s][:, :].unsqueeze(2), x_in[s][:, :, XW - 1:XW].bitcast(i32)).then_inc(f_meta, 1)

            def evacuate(i, s):
                dve.wait_ge(f_y, i + 1)
                dve.wait_ge(f_gate, i + 1)
                wait(dve, f_out, 32 * (i - FR + 1))
                last = None
                for k in range(2):
                    last = v.tensor_scalar(y_sb[s][:, k, :], yb[s][:, k * HID:(k + 1) * HID], gate[s][:, k:k + 1], None, ALU.mult)
                last.then_inc(f_ys, 1)

            meta(0, 0, 0)
            low_half(0, 0)
            meta(1, 1, 0)

            def step(m, u):
                i, s, _ = ahead(m, u, 0)
                i1, s1, _ = ahead(m, u, 1)
                i2, s2, m2 = ahead(m, u, 2)
                if not isinstance(m, int) or i1 < FTILES:
                    low_half(i1, s1)
                evacuate(i, s)
                if not isinstance(m, int) or i2 < FTILES:
                    meta(i2, s2, m2)

            for u in range(FR):
                step(0, u)
            with dve.Fori(1, FTILES // FR - 1) as m:
                for u in range(FR):
                    step(m, u)
            for u in range(FR):
                step(FTILES // FR - 1, u)

        @block.tensor
        def _(pe):
            mm = nc.tensor.matmul
            pe.wait_ge(consts2, 1)
            pe.wait_ge(p_x0, 1)
            for k in range(2):
                last = nc.tensor.transpose(misc[:, k * COPIES:(k + 1) * COPIES], x0[:, k * P:(k + 1) * P], ident[0:COPIES, 0:COPIES])
            last.then_inc(p_x0T, 1)
            pe.wait_ge(p_x0Ts, 1)
            pe.wait_ge(ld_w, 32)
            for k in range(2):
                last = mm(ybank[0:COPIES, :], rowsT[:, k, :], pro_w[:, k, :], start=(k == 0), stop=(k == 1))
            last.then_inc(p_xz, 1)
            pe.wait_ge(p_xzs, 1)
            for k in range(2):
                last = nc.tensor.transpose(misc[:, k * COPIES:(k + 1) * COPIES], xz[:, k * P:(k + 1) * P], ident[0:COPIES, 0:COPIES])
            last.then_inc(p_xsT, 1)
            pe.wait_ge(p_xsTs, 1)
            pe.wait_ge(ld_p, 96)
            for k in range(2):
                last = mm(ybank[0:COPIES, 0:NP], rowsT[:, k, :], pro_p[:, k, :], start=(k == 0), stop=(k == 1))
            last.then_inc(p_dbc, 1)
            pe.wait_ge(p_tab, 3)
            pe.wait_ge(ld_g, 48)

            def hot_cols(c, at, n):
                return onehot[:, bass.ds(c * CHUNK + at, n)]

            def expand(c, pos_, lhsT, at=0, n=CHUNK):
                wait(pe, x_copied, XPER * c + pos_ - 1)
                mm(xbank[pos_ % 2][:, 0:n], lhsT, hot_cols(c, at, n), start=True, stop=True).then_inc(x_ready, 1)

            def expand_input(c, q):
                wait(pe, scan_done, GROUPS * c + q - 1)
                mm(bbank[q % 2][:, :], table[:, TB + q * P:TB + (q + 1) * P], hot_cols(c, 0, CHUNK),
                   start=True, stop=True).then_inc(b_ready, 1)

            def sum_states(c, b):
                half, blk = b // 4, b % 4
                if blk == 0:
                    wait(pe, v_done, 2 * c + half)
                    mm(ybank[:, :], table[:, TDX + half * P:TDX + (half + 1) * P], hot_cols(c, 0, CHUNK), start=True, stop=False)
                q1 = 4 * b + 4
                pe.wait_ge(mul_v, len(VEC_MULS) * c + muls_before(VEC_MULS, q1))
                pe.wait_ge(mul_p, len(POOL_MULS) * c + muls_before(POOL_MULS, q1))
                for m in range(4):
                    last = mm(ybank[32 * m:32 * m + 32, :], sel[:, blk, :], hslot(4 * b + m), start=False, stop=(blk == 3))
                last.then_inc(sum_done, 1)

            def project_out(cp, j):
                if j == 0:
                    pe.wait_ge(v_done, 2 * cp + 2)
                    wait(pe, route_done, cp)
                o = pre[:, j * HID:(j + 1) * HID]
                for half in range(2):
                    at = half * CHUNK + j * P
                    mm(o, v_sb[:, at:at + P], wo[:, half, :], start=(half == 0), stop=False)
                mm(o, hot_cols(cp, j * P, P), table[:, TRB:TRB + HID], start=False, stop=True).then_inc(pre_ready, 1)

            def row_base_terms(cp):
                pe.wait_ge(t1_ready, TILES * cp + TILES)
                for j in range(TILES):
                    last = mm(pre[:, j * HID:(j + 1) * HID], hot_cols(cp, j * P, P), table[:, THB:THB + HID], start=True, stop=True)
                last.then_inc(hb_ready, 1)

            def turn_x2(cp):
                pe.wait_ge(x2_ready, TILES * cp + TILES)
                for j in range(TILES):
                    for k in range(2):
                        at = j * HID + k * P
                        last = nc.tensor.transpose(pre[:, at:at + P], rows4[:, j, k * P:(k + 1) * P], ident[:, :])
                last.then_inc(xT_ready, 1)

            def logits(cp, part_):
                pe.wait_ge(xT_copied, 2 * cp + part_ + 1)
                for j in range(2):
                    for k in range(2):
                        last = mm(logit_ps[:, 2 * part_ + j, :], x2T[:, j, k, :], rw[:, k, :], start=(k == 0), stop=(k == 1))
                last.then_inc(logit_ready, 1)

            def count_pairs(cp):
                pe.wait_ge(hot_ready, cp + 1)
                oh = hot[:, :, :, :].rearrange("p j k e -> p (j k e)")
                mm(cnt1_ps, tri[:, :], oh, start=True, stop=True)
                mm(cnt2_ps, ones[:, :], oh, start=True, stop=True).then_inc(cnt_ready, 1)

            def body(c, prev, main):
                for q in range(GROUPS):
                    if main:
                        expand(c, xpos(q), table[:, TA + q * P:TA + (q + 1) * P])
                        expand_input(c, q)
                        if q == 3:
                            for k in range(2):
                                expand(c, C_POS + k, table[:, TC:TC + P], k * TT, TT)
                        if q == 17:
                            expand(c, Z_POS[0], table[:, TZ:TZ + P])
                        if q == 31:
                            expand(c, Z_POS[1], table[:, TZ + P:TZ + 2 * P])
                        if q >= 7 and q % 4 == 3:
                            sum_states(c, (q - 7) // 4)
                    if prev:
                        if q == 3:
                            sum_states(c - 1, 7)
                        if S_PROJECT <= q < S_PROJECT + TILES:
                            project_out(c - 1, q - S_PROJECT)
                        if q == T_BASE:
                            row_base_terms(c - 1)
                        if q == T_TURN:
                            turn_x2(c - 1)
                        for k in range(2):
                            if q == T_LOGITS[k]:
                                logits(c - 1, k)
                        if q == T_COUNT:
                            count_pairs(c - 1)

            chunks(pe, body)
            pe.drain().then_inc(scan_phase_over, 1)
            pe.wait_ge(scan_phase_over, 4)
            pe.wait_ge(tiles_ready, 1)
            pe.wait_ge(w_lo, PIECES * NCHUNK)

            def expert_of(i):
                return pe.value_load(tile_expert[0:1, bass.ds(i, 1)], min_val=0, max_val=NE - 1)

            def turn_rows(i, s, m):
                pe.wait_ge(f_in[s], 16 * (m + 1))
                wait(pe, f_xT, i)
                for k in range(2):
                    halves = x_in[s][:, k, 0:HID].bitcast(f16)
                    for l in range(2):
                        for c in range(2):
                            last = nc.tensor.transpose(xTp16[:, l, c, k * P:(k + 1) * P],
                                                       halves[:, l * HID + c * P:l * HID + (c + 1) * P], ident16[:, :])
                last.then_inc(f_tp, 1)

            def first_product(i, s):
                e = expert_of(i)
                pe.wait_ge(f_xT, i + 1)
                for j in range(8):
                    b = j // 2
                    if j % 2 == 0:
                        wait(pe, f_g, 4 * (i - 1) + b + 1)
                    o = bank[b][:, (j % 2) * TT:(j % 2 + 1) * TT]
                    for c in range(2):
                        at = c * FFN + j * P
                        wh, wl = wsec(e, W1H, at, P), wsec(e, W1L, at, P)
                        mm(o, wh, x_T[s][:, 0, c, :], start=(c == 0), stop=False)
                        mm(o, wh, x_T[s][:, 1, c, :], start=False, stop=False)
                        last = mm(o, wl, x_T[s][:, 0, c, :], start=False, stop=(c == 1))
                    if j % 2 == 1:
                        last.then_inc(f_h, 1)

            def second_product(i, s):
                e = expert_of(i)
                pe.wait_ge(f_lo, 4 * i + 4)
                wait(pe, f_ys, i - FR + 1)
                for k in range(2):
                    o = yb[s][:, k * HID:(k + 1) * HID]
                    for j in range(8):
                        hh, hl = h_hi[s][:, j, k * P:(k + 1) * P], h_lo[s][:, j, k * P:(k + 1) * P]
                        wh, wl = wsec(e, W2H, j * HID, HID), wsec(e, W2L, j * HID, HID)
                        mm(o, hh, wh, start=(j == 0), stop=False)
                        mm(o, hh, wl, start=False, stop=False)
                        last = mm(o, hl, wh, start=False, stop=(j == 7))
                last.then_inc(f_y, 1)

            turn_rows(0, 0, 0)
            first_product(0, 0)
            turn_rows(1, 1, 0)

            def step(m, u):
                i, s, _ = ahead(m, u, 0)
                i1, s1, _ = ahead(m, u, 1)
                i2, s2, m2 = ahead(m, u, 2)
                if not isinstance(m, int) or i1 < FTILES:
                    first_product(i1, s1)
                if not isinstance(m, int) or i2 < FTILES:
                    turn_rows(i2, s2, m2)
                second_product(i, s)

            for u in range(FR):
                step(0, u)
            with pe.Fori(1, FTILES // FR - 1) as m:
                for u in range(FR):
                    step(m, u)
            for u in range(FR):
                step(FTILES // FR - 1, u)


def kernel(**inputs):
    import numpy as np
    import concourse.bacc as bacc
    from concourse.bass_utils import run_bass_kernel_spmd

    order = np.array(channel_order())
    a = {k: np.asarray(v) for k, v in inputs.items()}
    z_rows = HID + order
    w_in = np.concatenate([a["L0_attn_w_in"][:HID], a["L0_attn_w_in"][z_rows]], axis=0)
    b_in = np.concatenate([a["L0_attn_b_in"][:HID], a["L0_attn_b_in"][z_rows]], axis=0)
    laid = {
        "x_tok": a["x"], "level_emb": a["L0_tok_level_emb"], "w_inT": w_in.T, "b_in": b_in,
        "w_dtT": a["L0_attn_w_dt"].T, "b_dt": a["L0_attn_b_dt"], "a_log": a["L0_attn_A_log"],
        "w_BT": a["L0_attn_w_B"].T, "b_B": a["L0_attn_b_B"], "w_CT": a["L0_attn_w_C"].T, "b_C": a["L0_attn_b_C"],
        "d_skip": a["L0_attn_D"], "w_outT": a["L0_attn_w_out"].T[order], "b_out": a["L0_attn_b_out"],
        "gamma": a["L0_attn_gamma"], "beta": a["L0_attn_beta"], "router_wT": a["L0_ffn_router_w"].T,
        "w1": a["L0_ffn_w1"], "w2": a["L0_ffn_w2"],
    }
    nc = bacc.Bacc("TRN2", target_bir_lowering=False, num_devices=1)
    arrays, args = {}, []
    for name, value in laid.items():
        value = np.ascontiguousarray(value)
        arrays[f"in_{name}"] = value
        args.append(nc.dram_tensor(f"in_{name}", value.shape, mybir.dt.from_np(value.dtype), kind="ExternalInput").ap())
    out = nc.dram_tensor("out_0", (NTOK + TT, HID), mybir.dt.float32, kind="ExternalOutput").ap()
    program(nc, *args, out)
    r = run_bass_kernel_spmd(nc, [arrays], core_ids=[0])
    return r.results[0]["out_0"][:NTOK].reshape(BATCH, SEQ, HID)
```

```python
import concourse.bass as bass
from concourse import mybir
from contextlib import ExitStack

BATCH, SEQ = 32, 128
NTOK = BATCH * SEQ
LEVELS = 32
HID = 256
STATE = 16
FFN = 1024
EXPERTS = 8
TOPK = 2
CAP = max(1, int(1.25 * NTOK / EXPERTS * TOPK))
TOK_SCALE = 0.15
EPS = 1e-5
P = 128

GCH = P // STATE
GROUPS = HID // GCH
CHUNK = 512
NCHUNK = NTOK // CHUNK
TILES = CHUNK // P
COPIES = 3 * LEVELS

TT = 256
REGION = TOPK * CAP
DUMMY_ROW = EXPERTS * REGION
FTILES = (TOPK * NTOK + EXPERTS * (TT - 1)) // TT
NROWS = DUMMY_ROW + TT
XW = HID + EXPERTS + 1
INIT_PARTS = 9
DROP = 1.0e6

X_UP = 16.0
W_UP = 64.0
H_UP = 16.0


def channel_order():
    order = []
    for half in range(2):
        for row in range(P):
            strip, block, e = row // 32, (row % 32) // GCH, row % GCH
            order.append(half * P + (4 * block + strip) * GCH + e)
    return order


def program(nc, x_tok, level_emb, w_inT, b_in, w_dtT, b_dt, a_log, w_BT, b_B, w_CT, b_C, d_skip,
            w_outT, b_out, gamma, beta, router_wT, w1, w2, out):
    f32, bf16, f16, i32 = mybir.dt.float32, mybir.dt.bfloat16, mybir.dt.float16, mybir.dt.int32
    ALU, ACT, AX = mybir.AluOpType, mybir.ActivationFunctionType, mybir.AxisListType

    ctx = ExitStack()
    with ctx:
        def sb(name, shape, dt=f32):
            return ctx.enter_context(nc.sbuf_tensor(name, shape, dt))

        def ps(name, shape, dt=f32):
            return ctx.enter_context(nc.psum_tensor(name, shape, dt))

        def sem(name):
            return ctx.enter_context(nc.semaphore(name))

        level_dram = nc.dram_tensor("level_scratch", [BATCH, SEQ], f32, kind="Internal").ap()
        rows_dram = nc.dram_tensor("dispatch_rows", [NROWS, XW], f32, kind="Internal").ap()

        WSEC = 2 * FFN
        weights = sb("weights", [P, EXPERTS * 4 * WSEC], f16)
        W1H, W1L, W2H, W2L = range(4)

        def wsec(e, which, at, n):
            return weights[:, bass.ds((e * 4 + which) * WSEC + at, n)]

        scratch = weights[:, 4 * 4 * WSEC:].bitcast(f32)
        T_N = HID * STATE
        expA = scratch[0:COPIES, 0:T_N]
        lev_all = scratch[0:COPIES, T_N:2 * T_N]
        tab_v = scratch[0:COPIES, 2 * T_N:3 * T_N]
        tab_h = scratch[0:COPIES, 3 * T_N:3 * T_N + T_N // 2].bitcast(bf16)

        arena_n = 17472 - FFN - CHUNK
        arena = sb("arena", [P, arena_n])
        used = [0, 0]

        def part(phase, n, dt=f32):
            words = n if dt in (f32, i32) else n // 2
            at = used[phase]
            used[phase] += words
            assert used[phase] <= arena_n
            a = arena[:, at:at + words]
            return a if dt == f32 else a.bitcast(dt)

        TA, TB, TC, TZ, TDX, TRB, THB = 0, T_N, 2 * T_N, 2 * T_N + P, 2 * T_N + P + HID, 2 * T_N + P + 2 * HID, 2 * T_N + P + 3 * HID
        NTAB = 2 * T_N + P + 4 * HID
        SMALL = NTAB - TC
        table = part(0, NTAB, bf16)[0:COPIES, :]
        onehot = part(0, NTOK, bf16)[0:COPIES, :]
        HRING, ARING = 16, 4
        h_ring = [part(0, HRING // 2 * CHUNK), weights[:, (EXPERTS - 1) * 4 * WSEC:].bitcast(f32)]
        a_all = part(0, ARING * CHUNK)
        c_sb = part(0, CHUNK)
        z_sb = part(0, CHUNK)
        v_sb = part(0, 2 * CHUNK)
        PIECE = FFN // 2
        PIECES = 8
        stage = part(0, 2 * PIECE)
        FR = 3
        x_in = [part(1, 2 * XW).rearrange("p (s w) -> p s w", s=2) for _ in range(FR)]
        x_T = [part(1, 2 * 2 * TT, f16).rearrange("p (l c t) -> p l c t", l=2, c=2) for _ in range(FR)]
        h_hi = [part(1, EXPERTS * TT, f16).rearrange("p (j t) -> p j t", j=8) for _ in range(FR)]
        h_lo = [part(1, EXPERTS * TT, f16).rearrange("p (j t) -> p j t", j=8) for _ in range(FR)]
        g_sb = [part(1, 2 * TT) for _ in range(4)]
        y_sb = [part(1, 2 * HID).rearrange("p (s n) -> p s n", s=2) for _ in range(FR)]

        def hslot(q):
            half, k = divmod(q % HRING, HRING // 2)
            return h_ring[half][:, k * CHUNK:(k + 1) * CHUNK]

        def aslot(q):
            return a_all[:, (q % ARING) * CHUNK:(q % ARING + 1) * CHUNK]

        rows4 = sb("rows4", [P, TILES, HID])
        x2T = v_sb[:, CHUNK:].rearrange("p (j c t) -> p j c t", j=2, c=2)
        payload = sb("payload", [P, TILES, XW])
        x_hi = payload[:, :, 0:HID].bitcast(f16)[:, :, 0:HID]
        x_lo = payload[:, :, 0:HID].bitcast(f16)[:, :, HID:2 * HID]
        bn6 = sb("bn6", [P, TILES, 6])
        mv = sb("mv", [P, TILES, 2])
        nrm = sb("nrm", [P, 4, TILES])
        carried = sb("carried", [P, 1])

        ident = sb("ident", [P, P])
        ident16 = sb("ident16", [P, P], f16)
        tri = sb("tri", [P, P], bf16)
        ones = sb("ones", [P, P], bf16)
        sel = sb("sel", [P, 4, 32])
        gamma_b = sb("gamma_b", [P, HID])
        wo = sb("wo", [P, 2, HID])
        rw = sb("rw", [P, 2, EXPERTS])
        segmask = sb("segmask", [P, TILES * EXPERTS])
        row_base = sb("row_base", [P, EXPERTS])
        tok_f = sb("tok_f", [P, TILES])
        lvl_id = sb("lvl_id", [COPIES, 1])
        not_first = sb("not_first", [COPIES, 1])
        last_copy = sb("last_copy", [COPIES, 1])

        pro = weights[:, 3 * 4 * WSEC:4 * 4 * WSEC].bitcast(f32)
        pro_at = [0]

        def tmp(parts, *dims):
            n = 1
            for d in dims:
                n *= d
            at = pro_at[0]
            pro_at[0] += n
            assert pro_at[0] <= 2 * WSEC
            return pro[0:parts, at:at + n]

        xz = tmp(COPIES, 2 * HID)
        small = tmp(COPIES, SMALL)
        small_h = tmp(COPIES, SMALL // 2).bitcast(bf16)
        init_row = tmp(P, 2 * XW).rearrange("p (s w) -> p s w", s=2)
        pro2 = weights[:, 2 * 4 * WSEC:3 * 4 * WSEC].bitcast(f32)
        pro_w = pro2[:, 0:2 * 2 * HID].rearrange("p (c n) -> p c n", c=2)
        NP = HID + 2 * STATE
        pro_p = pro2[:, 1024:1024 + 2 * NP].rearrange("p (c n) -> p c n", c=2)
        bin_b = pro2[0:COPIES, 1600:1600 + 2 * HID]
        bp_b = pro2[0:COPIES, 2112:2112 + NP]
        d_b = pro2[0:COPIES, 2400:2400 + HID]
        bo_b = pro2[0:COPIES, 2656:2656 + HID]
        be_b = pro2[0:COPIES, 2912:2912 + HID]
        dbc = pro2[0:COPIES, 3168:3168 + NP]
        rowsT = pro2[:, 3456:3456 + 2 * COPIES].rearrange("p (c m) -> p c m", c=2)
        sp = [weights[:, 1 * 4 * WSEC:2 * 4 * WSEC].bitcast(f32)[0:COPIES, k * HID:(k + 1) * HID] for k in range(10)]
        emb, h0, x0 = [
            weights[:, 0:4 * WSEC].bitcast(f32)[0:COPIES, k * HID:(k + 1) * HID] for k in range(13, 16)]
        lev = weights[:, 1 * 4 * WSEC:2 * 4 * WSEC].bitcast(f32)[0:BATCH, 10 * HID:10 * HID + 12 * SEQ]
        x_int = lev[:, 0:SEQ].bitcast(i32)
        x_f = lev[:, SEQ:2 * SEQ]
        acc = [lev[:, 2 * SEQ:3 * SEQ], lev[:, 3 * SEQ:4 * SEQ]]
        sc0, sc1, sc_o = lev[:, 4 * SEQ:6 * SEQ], lev[:, 6 * SEQ:8 * SEQ], lev[:, 8 * SEQ:10 * SEQ]
        lev_c = lev[:, 10 * SEQ:11 * SEQ]

        NE = EXPERTS
        lg = sb("lg", [P, TILES, NE])
        lg2 = sb("lg2", [P, TILES, NE])
        eq = sb("eq", [P, TILES, NE])
        cs = sb("cs", [P, TILES * NE])
        top = sb("top", [P, 3, TILES])
        hot = sb("hot", [P, TILES, 2, NE], bf16)
        dif = sb("dif", [P, TILES, NE])
        seen = sb("seen", [P, TILES + 1, 2 * NE])
        counts = sb("counts", [P, 2, TILES * 2 * NE])
        pos = sb("pos", [P, TILES, 2, NE])
        kept = sb("kept", [P, TILES, 2, NE])
        slot = sb("slot", [P, TILES, NE])
        mul1 = sb("mul1", [P, TILES, 2, NE])
        mul2 = sb("mul2", [P, TILES, 2, NE])
        red1 = sb("red1", [P, TILES, 2])
        red2 = sb("red2", [P, TILES, 2])
        drop = sb("drop", [P, TILES, 2])
        slot_i = sb("slot_i", [P, TILES, 2], i32)
        NT10 = REGION // TT
        FT = FTILES + FR
        thr = sb("thr", [1, NT10])
        tile_no = sb("tile_no", [1, FT])
        one8 = sb("one8", [1, NE])
        stage_at = [0]

        def row(n):
            at = stage_at[0]
            stage_at[0] += n
            assert stage_at[0] <= 2 * PIECE
            return stage[0:1, at:at + n]

        le = row(FT * NE).rearrange("p (i e) -> p i e", e=NE)
        le2 = row(FT * NE).rearrange("p (i e) -> p i e", e=NE)
        gt = row(NE * NT10).rearrange("p (e k) -> p e k", e=NE)
        cnt, n8, nt, ntc = row(2 * NE), row(NE), row(NE), row(NE)
        ex, bel, rw1, rw2 = row(FT), row(FT), row(FT), row(FT)
        tile_expert = sb("tile_expert", [1, FT], i32)
        tile_row = sb("tile_row", [1, FT], i32)
        tile_count = sb("tile_count", [1, 1], i32)
        tgate = [part(1, 2) for k in range(FR)]
        gate = [part(1, 2) for k in range(FR)]
        tok_i = [part(1, 2, i32) for k in range(FR)]

        bank = [ps(f"bank{k}", [P, CHUNK]) for k in range(4)]
        misc = ps("misc", [P, CHUNK])
        xbank, bbank = bank[0:2], bank[2:4] + [misc]
        ybank = ps("ybank", [P, CHUNK])
        pre = ps("pre", [P, TILES * HID])
        logit_ps = pre[:, 0:TILES * NE].rearrange("p (j e) -> p j e", e=NE)
        cnt_ps = pre[:, 64:192].rearrange("p (k f) -> p k f", k=2)
        xTp16 = misc[:, :].bitcast(f16).rearrange("p (l c t) -> p l c t", l=2, c=2)
        yb = [ybank, pre[:, 0:CHUNK], pre[:, CHUNK:2 * CHUNK]]

        ld_tok, ld_emb, ld_w, ld_p, ld_a, ld_d, ld_g = [sem(f"ld_{k}") for k in ("tok", "emb", "w", "p", "a", "d", "g")]
        consts = sem("consts")
        consts2 = sem("consts2")
        rows_init = sem("rows_init")
        vstep = sem("vstep")
        lev_out, lev_back = sem("lev_out"), sem("lev_back")
        p_var, p_std, p_x0, p_x0T, p_x0Ts, p_xz, p_xzs, p_xsT, p_xsTs, p_dbc, p_abs, p_exp = [
            sem(f"p_{k}") for k in ("var", "std", "x0", "x0T", "x0Ts", "xz", "xzs", "xsT", "xsTs", "dbc", "abs", "exp")]
        p_zc, p_ez, p_eA, p_arg, p_v, p_hi, p_r, p_mid, p_tab, p_hot = [
            sem(f"p_{k}") for k in ("zc", "ez", "eA", "arg", "v", "hi", "r", "mid", "tab", "hot")]
        x_ready, x_copied, b_ready, scan_done = sem("x_ready"), sem("x_copied"), sem("b_ready"), sem("scan_done")
        mul_v, mul_p, sum_done, v_done = sem("mul_v"), sem("mul_p"), sem("sum_done"), sem("v_done")
        pre_ready, hb_ready, var1, std1, t1_ready, h_ready = [
            sem(k) for k in ("pre_ready", "hb_ready", "var1", "std1", "t1_ready", "h_ready")]
        var2, std2, nrm2, x2_ready, hi_ready, xT_ready, xT_copied, logit_ready = [
            sem(k) for k in ("var2", "std2", "nrm2", "x2_ready", "hi_ready", "xT_ready", "xT_copied", "logit_ready")]
        hot_ready, cnt_ready, cnt_taken, route_done, scattered, h_stored = [
            sem(k) for k in ("hot_ready", "cnt_ready", "cnt_taken", "route_done", "scattered", "h_stored")]
        w_loaded = [sem("w_loaded0"), sem("w_loaded1")]
        w_hi, w_lo = sem("w_hi"), sem("w_lo")
        tiles_ready, scan_phase_over = sem("tiles_ready"), sem("scan_phase_over")
        f_in = [sem(f"f_in{k}") for k in range(FR)]
        f_tp, f_xT, f_h, f_g, f_hi, f_lo, f_y, f_tg, f_gate, f_meta, f_ys, f_out = [
            sem(f"f_{k}") for k in ("tp", "xT", "h", "g", "hi", "lo", "y", "tg", "gate", "meta", "ys", "out")]

        XPER = GROUPS + 4

        def xpos(q):
            return q if q < 4 else (q + 2 if q < 18 else q + 3)

        C_POS, Z_POS = 4, (20, 35)
        VEC_MULS = [q for q in range(GROUPS) if q % 4 == 3]
        POOL_MULS = [q for q in range(GROUPS) if q not in VEC_MULS]

        def muls_before(group_list, q):
            return sum(1 for k in group_list if k < q)

        S_GATE, S_STATS1, S_GAMMA, S_H = (21, 5), (10, 11, 12, 12), 13, 17
        S_STATS2, S_NORM2, S_LOW, S_CHOOSE, S_PLACE = 19, 22, 27, 30, 36
        A_STD1, A_STD2, A_NORM2, A_HIGH, A_TURNED = 16, 23, 25, 27, (28, 30)
        T_PROJECT, T_BASE, T_TURN, T_LOGITS, T_COUNT = (7, 9, 10, 11), 17, (27, 29), (29, 31), 36
        P_SEND = 11
        T_SUM = 8

        def piece_slot(k):
            return 2 + 3 * k

        def wait(eng, s, n):
            if not isinstance(n, int) or n > 0:
                eng.wait_ge(s, n)

        def chunks(eng, body):
            body(0, True, False, False)
            body(1, True, True, False)
            with eng.Fori(2, NCHUNK) as c:
                body(c, True, True, True)
            body(NCHUNK, False, True, True)
            body(NCHUNK + 1, False, False, True)

        def tile_steps(eng, step, ahead_=0):
            count = eng.value_load(tile_count[0:1, 0:1], min_val=1, max_val=FTILES)

            def guarded(m, u):
                with eng.If(count > FR * m + u + ahead_):
                    step(m, u)
                eng.end_ifs()

            step(0, 0)
            for u in range(1, FR):
                guarded(0, u)
            with eng.Fori(1, FTILES // FR) as m:
                for u in range(FR):
                    guarded(m, u)

        def ahead(m, u, k):
            return FR * (m + (u + k) // FR) + (u + k) % FR, (u + k) % FR, m + (u + k) // FR

        block = ctx.enter_context(nc.Block())

        @block.sync
        def _(sp_):
            dma = sp_.dma_start
            dma(x_int, x_tok).then_inc(ld_tok, 16)
            for k in range(3):
                dma(emb[k * LEVELS:(k + 1) * LEVELS, :], level_emb).then_inc(ld_emb, 16)
            dma(pro_w, w_inT.rearrange("(c p) n -> p c n", p=P)).then_inc(ld_w, 16)
            dma(bin_b, b_in.partition_broadcast(COPIES)).then_inc(ld_w, 16)
            dma(pro_p[:, :, 0:HID], w_dtT.rearrange("(c p) n -> p c n", p=P)).then_inc(ld_p, 16)
            dma(pro_p[:, :, HID:HID + STATE], w_BT.rearrange("(c p) n -> p c n", p=P)).then_inc(ld_p, 16)
            dma(pro_p[:, :, HID + STATE:NP], w_CT.rearrange("(c p) n -> p c n", p=P)).then_inc(ld_p, 16)
            dma(bp_b[:, 0:HID], b_dt.partition_broadcast(COPIES)).then_inc(ld_p, 16)
            dma(bp_b[:, HID:HID + STATE], b_B.partition_broadcast(COPIES)).then_inc(ld_p, 16)
            dma(bp_b[:, HID + STATE:NP], b_C.partition_broadcast(COPIES)).then_inc(ld_p, 16)
            dma(expA, a_log.rearrange("d n -> (d n)").partition_broadcast(COPIES)).then_inc(ld_a, 16)
            sp_.wait_ge(p_hot, 1)
            dma(level_dram, lev_c).then_inc(lev_out, 16)
            sp_.wait_ge(lev_out, 16)
            dma(lev_all, level_dram.rearrange("b t -> (b t)").partition_broadcast(COPIES)).then_inc(lev_back, 16)
            dma(d_b, d_skip.partition_broadcast(COPIES)).then_inc(ld_d, 16)
            dma(bo_b, b_out.partition_broadcast(COPIES)).then_inc(ld_d, 16)
            dma(be_b, beta.partition_broadcast(COPIES)).then_inc(ld_d, 16)
            dma(gamma_b[:, :], gamma.partition_broadcast(P)).then_inc(ld_g, 16)
            dma(wo[:, :, :], w_outT.rearrange("(c p) n -> p c n", p=P)).then_inc(ld_g, 16)
            dma(rw[:, :, :], router_wT.rearrange("(c p) n -> p c n", p=P)).then_inc(ld_g, 16)
            sp_.wait_ge(consts2, 1)
            blk = NROWS // TT // INIT_PARTS
            for k in range(INIT_PARTS):
                view = rows_dram[k * blk * TT:(k + 1) * blk * TT, :].rearrange("(t s p) w -> s p t w", p=P, s=2)
                for s in range(2):
                    dma(view[s], init_row[:, s:s + 1, :].to_broadcast([P, blk, XW])).then_inc(rows_init, 16)
            dma(out[NTOK:NTOK + TT, :].rearrange("(s p) n -> p s n", p=P), init_row[:, :, 0:HID]).then_inc(rows_init, 16)

            def load_piece(c, k):
                wait(sp_, w_lo, PIECES * c + k - 1)
                dst = stage[:, (k % 2) * PIECE:(k % 2 + 1) * PIECE]
                if k < 4:
                    src = w1[bass.ds(c, 1), (k // 2) * P:(k // 2 + 1) * P, (k % 2) * PIECE:(k % 2 + 1) * PIECE]
                    dma(dst, src.rearrange("e p n -> p (e n)")).then_inc(w_loaded[k % 2], 16)
                else:
                    src = w2[bass.ds(c, 1), (k - 4) * 2 * P:(k - 3) * 2 * P, :].rearrange("e (j p) n -> p (e j) n", p=P)
                    dma(dst.rearrange("p (j n) -> p j n", j=2), src).then_inc(w_loaded[k % 2], 16)

            def store_h(cp):
                sp_.wait_ge(h_ready, TILES * cp + TILES)
                dma(out[bass.ds(cp * CHUNK, CHUNK), :].rearrange("(j p) n -> p j n", p=P), rows4[:, :, :]).then_inc(h_stored, 16)

            def body(c, main, prev, prev2):
                for q in range(GROUPS):
                    if prev:
                        for k in range(PIECES):
                            if q == max(piece_slot(k - 2), 0):
                                load_piece(c - 1, k)
                        if q == S_H + 1:
                            store_h(c - 1)

            chunks(sp_, body)

            sp_.wait_ge(scattered, 16 * 2 * TILES * NCHUNK)
            sp_.wait_ge(tiles_ready, 1)
            sp_.wait_ge(scan_phase_over, 4)

            def load_x(i, s, first):
                if not first:
                    sp_.wait_ge(f_tp, i - FR + 1)
                    sp_.wait_ge(f_meta, i - FR + 1)
                row = sp_.value_load(tile_row[0:1, bass.ds(i, 1)], min_val=0, max_val=DUMMY_ROW)
                dma(x_in[s], rows_dram[bass.ds(row, TT), :].rearrange("(s p) w -> p s w", p=P)).then_inc(f_in[s], 16)

            for i in range(FR):
                load_x(i, i, True)
            tile_steps(sp_, lambda m, u: load_x(FR * (m + 1) + u, u, False), 1)

        @block.gpsimd
        def _(pool):
            g = nc.gpsimd
            n = [0]

            def link(ins):
                ins.then_inc(consts, 1)
                n[0] += 1
                pool.wait_ge(consts, n[0])

            def diag(t, last=False):
                link(g.memset(t[:, :], 0.0))
                link(g.affine_select(out=t[:, :], in_=t[:, :], compare_op=ALU.not_equal, fill=1.0, base=0,
                                     pattern=[[-1, P]], channel_multiplier=1))

            for k in range(3):
                link(g.iota(lvl_id[k * LEVELS:(k + 1) * LEVELS, :], pattern=[[0, 1]], base=0, channel_multiplier=1,
                            allow_small_or_imprecise_dtypes=True))
                link(g.memset(not_first[k * LEVELS:(k + 1) * LEVELS, :], 0.0 if k == 0 else -1.0))
                link(g.memset(last_copy[k * LEVELS:(k + 1) * LEVELS, :], -1.0 if k == 2 else 0.0))
            diag(ident)
            diag(ident16)
            link(g.memset(tri[:, :], 1.0))
            link(g.affine_select(out=tri[:, :], in_=tri[:, :], compare_op=ALU.is_ge, fill=0.0, base=0,
                                 pattern=[[1, P]], channel_multiplier=-1))
            link(g.memset(ones[:, :], 1.0))
            link(g.memset(sel[:, :, :], 1.0))
            link(g.affine_select(out=sel[:, :, :], in_=sel[:, :, :], compare_op=ALU.is_ge, fill=0.0, base=0,
                                 pattern=[[STATE * GCH, 4], [-STATE, 32]], channel_multiplier=1))
            link(g.affine_select(out=sel[:, :, :], in_=sel[:, :, :], compare_op=ALU.is_ge, fill=0.0, base=STATE - 1,
                                 pattern=[[-STATE * GCH, 4], [STATE, 32]], channel_multiplier=-1))
            link(g.memset(segmask[:, :], 1.0))
            link(g.memset(segmask[:, :].rearrange("p (j e) -> p j e", e=NE)[:, :, 0:1], 0.0))
            link(g.iota(row_base[:, :], pattern=[[REGION, NE]], base=-1, channel_multiplier=0,
                        allow_small_or_imprecise_dtypes=True))
            link(g.iota(tok_f[:, :], pattern=[[P, TILES]], base=-CHUNK, channel_multiplier=1,
                        allow_small_or_imprecise_dtypes=True))
            link(g.memset(seen[:, 0, :], 0.0))
            link(g.memset(one8[:, :], 1.0))
            link(g.iota(thr[:, :], pattern=[[TT, NT10]], base=0, channel_multiplier=0,
                        allow_small_or_imprecise_dtypes=True))
            link(g.iota(tile_no[:, :], pattern=[[1, FT]], base=0, channel_multiplier=0,
                        allow_small_or_imprecise_dtypes=True))
            link(g.memset(a_all.rearrange("p (s t) -> p s t", t=SEQ)[:, :, 0:1], 0.0))
            link(g.memset(init_row[:, :, :], 0.0))
            link(g.iota(init_row[:, :, XW - 1:XW].bitcast(i32), pattern=[[P, 2], [0, 1]], base=NTOK, channel_multiplier=1))
            pool.drain().then_inc(consts2, 1)

            last_row, last_sum = pool.to_reg(DUMMY_ROW - 1), pool.to_reg(NTOK + TT - 1)

            rows_sent, sums_sent = pool.alloc_register("rows_sent"), pool.alloc_register("sums_sent")
            pool.reg_mov(rows_sent, 0)
            pool.reg_mov(sums_sent, 0)

            def mul(c, q):
                pool.wait_ge(scan_done, GROUPS * c + q + 1)
                if q == POOL_MULS[0]:
                    pool.wait_ge(x_copied, XPER * c + C_POS + 2)
                g.tensor_tensor(hslot(q), hslot(q), c_sb, ALU.mult).then_inc(mul_p, 1)

            def send(cp, j, k):
                if j == 0 and k == 0:
                    pool.wait_ge(route_done, cp + 1)
                    pool.reg_add(rows_sent, rows_sent, 16 * TOPK * TILES)
                    pool.wait_ge(rows_init, 16 * (2 * INIT_PARTS + 1))
                g.indirect_dma_start(
                    out=rows_dram, out_offset=bass.IndirectOffsetOnAxis(slot_i[:, j, k:k + 1], 0),
                    in_=payload[:, j, :], in_offset=None, bounds_check=last_row,
                    oob_is_err=False).then_inc(scattered, 16)

            def body(c, main, prev, prev2):
                pairs = [(j, k) for j in range(TILES) for k in range(TOPK)]
                for q in POOL_MULS:
                    if main:
                        mul(c, q)
                    if prev2 and q >= P_SEND and pairs:
                        send(c - 2, *pairs.pop(0))

            chunks(pool, body)
            pool.drain().then_inc(scan_phase_over, 1)

            def step(m, u):
                i, s, _ = ahead(m, u, 0)
                pool.wait_ge(f_ys, i + 1)
                pool.wait_ge(f_meta, i + 1)
                if not isinstance(i, int) or i > 0:
                    pool.wait_ge(f_out, sums_sent)
                pool.reg_add(sums_sent, sums_sent, 32)
                pool.wait_ge(h_stored, 16 * NCHUNK)
                for k in range(2):
                    g.indirect_dma_start(
                        out=out, out_offset=bass.IndirectOffsetOnAxis(tok_i[s][:, k:k + 1], 0),
                        in_=y_sb[s][:, k, :], in_offset=None, compute_op=ALU.add,
                        bounds_check=last_sum, oob_is_err=True).then_inc(f_out, 16)

            pool.wait_ge(tiles_ready, 1)
            tile_steps(pool, step)
            pool.wait_ge(scattered, rows_sent)
            pool.wait_ge(f_out, sums_sent)

        @block.scalar
        def _(act):
            A = nc.scalar.activation
            act.wait_ge(p_var, 1)
            A(nrm[0:COPIES, 1, 0:1], nrm[0:COPIES, 0, 0:1], ACT.Sqrt).then_inc(p_std, 1)
            act.wait_ge(ld_a, 16)
            A(expA, expA, ACT.Exp).then_inc(p_eA, 1)
            act.wait_ge(p_zc, 1)
            A(sp[8], sp[8], ACT.Exp).then_inc(p_ez, 1)
            act.wait_ge(p_abs, 1)
            A(sp[1], sp[0], ACT.Exp, scale=-1.0).then_inc(p_exp, 1)

            def split(k, v, hi):
                act.wait_ge(p_v, k + 1)
                A(hi, v, ACT.Copy).then_inc(p_hi, 1)
                act.wait_ge(p_r, k + 1)
                A(hi, v, ACT.Copy).then_inc(p_mid, 1)

            split(0, small, small_h)
            act.wait_ge(p_arg, 1)
            A(tab_v, tab_v, ACT.Exp, scale=-1.0).then_inc(p_v, 1)
            split(1, tab_v, tab_h)
            split(2, tab_v, tab_h)

            def copy_decay(c, q):
                act.wait_ge(x_ready, XPER * c + xpos(q) + 1)
                wait(act, scan_done, GROUPS * c + q - (ARING - 1))
                dst = aslot(q).rearrange("p (b t) -> p b t", t=SEQ)[:, :, 1:]
                src = xbank[xpos(q) % 2][:, :].rearrange("p (b t) -> p b t", t=SEQ)[:, :, 1:]
                A(dst, src, ACT.Copy).then_inc(x_copied, 1)

            def copy_c(c):
                wait(act, mul_v, len(VEC_MULS) * c)
                wait(act, mul_p, len(POOL_MULS) * c)
                for k in range(2):
                    act.wait_ge(x_ready, XPER * c + C_POS + k + 1)
                    A(c_sb[:, k * TT:(k + 1) * TT], xbank[(C_POS + k) % 2][:, 0:TT], ACT.Copy).then_inc(x_copied, 1)

            def copy_z(c, half):
                act.wait_ge(x_ready, XPER * c + Z_POS[half] + 1)
                wait(act, v_done, 2 * c + half - 1)
                A(z_sb, xbank[Z_POS[half] % 2][:, :], ACT.Copy).then_inc(x_copied, 1)

            def weight_hi(c, k):
                if isinstance(c, int) and c == NCHUNK - 1 and k == 0:
                    act.wait_ge(sum_done, 8 * NCHUNK)
                act.wait_ge(w_loaded[k % 2], 16 * (PIECES // 2 * c + k // 2 + 1))
                which, at = (W1H, k * PIECE) if k < 4 else (W2H, (k - 4) * PIECE)
                A(wsec(c, which, at, PIECE), stage[:, (k % 2) * PIECE:(k % 2 + 1) * PIECE], ACT.Copy, scale=W_UP).then_inc(w_hi, 1)

            def end_op(cp, q):
                if q == A_STD1:
                    act.wait_ge(var1, cp + 1)
                    A(nrm[:, 1, :], nrm[:, 0, :], ACT.Sqrt).then_inc(std1, 1)
                if q == A_STD2:
                    act.wait_ge(var2, cp + 1)
                    A(nrm[:, 1, :], nrm[:, 0, :], ACT.Sqrt).then_inc(std2, 1)
                if q == A_NORM2:
                    act.wait_ge(nrm2, cp + 1)
                    act.wait_ge(h_stored, 16 * (cp + 1))
                if q in (A_NORM2, A_NORM2 + 1):
                    for j in range(2 * (q - A_NORM2), 2 * (q - A_NORM2) + 2):
                        A(rows4[:, j, :], rows4[:, j, :], ACT.Identity, bias=nrm[:, 3, j:j + 1],
                          scale=nrm[:, 2, j:j + 1]).then_inc(x2_ready, 1)
                if q == A_HIGH:
                    act.wait_ge(x2_ready, TILES * cp + TILES)
                    wait(act, scattered, 16 * 2 * TILES * cp)
                    A(x_hi, rows4[:, :, :], ACT.Copy, scale=X_UP).then_inc(hi_ready, 1)
                for k in range(2):
                    if q == A_TURNED[k]:
                        act.wait_ge(xT_ready, 2 * cp + k + 1)
                        wait(act, logit_ready, 2 * cp + k)
                        A(x2T, pre[:, k * CHUNK:(k + 1) * CHUNK].rearrange("p (j c t) -> p j c t", j=2, c=2),
                          ACT.Copy).then_inc(xT_copied, 1)

            def body(c, main, prev, prev2):
                for q in range(GROUPS):
                    if main:
                        copy_decay(c, q)
                        if q == 3:
                            copy_c(c)
                        if q == 17:
                            copy_z(c, 0)
                        if q == 31:
                            copy_z(c, 1)
                    if prev:
                        for k in range(PIECES):
                            if q == piece_slot(k):
                                weight_hi(c - 1, k)
                        end_op(c - 1, q)

            chunks(act, body)
            act.drain().then_inc(scan_phase_over, 1)
            act.wait_ge(scan_phase_over, 4)

            def take_x(i, s, m):
                act.wait_ge(f_in[s], 16 * (m + 1))
                e = act.value_load(tile_expert[0:1, bass.ds(i, 1)], min_val=0, max_val=NE - 1)
                wait(act, f_gate, i - FR + 1)
                A(tgate[s][:, :].unsqueeze(2), x_in[s][:, :, bass.ds(HID + e, 1)], ACT.Tanh, scale=0.5).then_inc(f_tg, 1)
                act.wait_ge(f_tp, i + 1)
                wait(act, f_h, 4 * (i - FR + 1))
                A(x_T[s], xTp16, ACT.Copy).then_inc(f_xT, 1)

            def activate(i, s):
                for b in range(4):
                    act.wait_ge(f_h, 4 * i + b + 1)
                    wait(act, f_lo, 4 * (i - 1) + b + 1)
                    A(g_sb[b], bank[b][:, :], ACT.Gelu, scale=1.0 / (X_UP * W_UP)).then_inc(f_g, 1)
                    act.wait_ge(f_g, 4 * i + b + 1)
                    if b == 0:
                        wait(act, f_y, i - FR + 1)
                    A(h_hi[s][:, 2 * b:2 * b + 2, :], g_sb[b].rearrange("p (j t) -> p j t", j=2), ACT.Copy,
                      scale=H_UP).then_inc(f_hi, 1)

            act.wait_ge(tiles_ready, 1)
            take_x(0, 0, 0)
            activate(0, 0)
            take_x(1, 1, 0)

            def step(m, u):
                i1, s1, _ = ahead(m, u, 1)
                i2, s2, m2 = ahead(m, u, 2)
                activate(i1, s1)
                take_x(i2, s2, m2)

            tile_steps(act, step)

        @block.vector
        def _(dve):
            v = nc.vector
            n = [0]
            base = [0]

            def done(ins):
                ins.then_inc(vstep, 1)
                n[0] += 1

            def after():
                dve.wait_ge(vstep, base[0] + n[0])

            def link(ins):
                done(ins)
                after()

            dve.wait_ge(ld_tok, 16)
            link(v.tensor_copy(x_f, x_int))
            link(v.tensor_scalar(acc[0], x_f, 40.0, None, ALU.is_equal))
            link(v.scalar_tensor_tensor(acc[1], x_f, 91.0, acc[0], ALU.is_equal, ALU.add))
            link(v.scalar_tensor_tensor(acc[0], x_f, 123.0, acc[1], ALU.is_equal, ALU.add))
            link(v.scalar_tensor_tensor(acc[1], x_f, 41.0, acc[0], ALU.is_equal, ALU.subtract))
            link(v.scalar_tensor_tensor(acc[0], x_f, 93.0, acc[1], ALU.is_equal, ALU.add))
            link(v.memset(sc0, 0.0))
            link(v.memset(sc1, 0.0))
            ev = "p (t k) -> p t k"
            link(v.scalar_tensor_tensor(sc0.rearrange(ev, k=2)[:, :, 0], x_f, 125.0, acc[0], ALU.is_equal, ALU.add))
            link(v.memset(sc1.rearrange(ev, k=2)[:, :, 0], -float(LEVELS - 1)))
            link(v.tensor_tensor_scan(sc_o, sc0, sc1, 0.0, ALU.subtract, ALU.max))
            v.tensor_copy(lev_c, sc_o.rearrange(ev, k=2)[:, :, 1]).then_inc(p_hot, 1)

            dve.wait_ge(ld_emb, 48)
            link(v.tensor_scalar(h0[:, :], emb[:, :], TOK_SCALE, None, ALU.mult))
            link(v.bn_stats(bn6[0:COPIES, 0, :], h0[:, :]))
            link(v.bn_aggr(mv[0:COPIES, 0, :], bn6[0:COPIES, 0, :]))
            v.tensor_scalar(nrm[0:COPIES, 0, 0:1], mv[0:COPIES, 0, 1:2], EPS, None, ALU.add).then_inc(p_var, 1)
            dve.wait_ge(p_std, 1)
            link(v.reciprocal(nrm[0:COPIES, 2, 0:1], nrm[0:COPIES, 1, 0:1]))
            v.tensor_scalar(x0[:, :], h0[:, :], mv[0:COPIES, 0, 0:1], nrm[0:COPIES, 2, 0:1], ALU.subtract, ALU.mult).then_inc(p_x0, 1)
            dve.wait_ge(p_x0T, 1)
            v.tensor_copy(rowsT[:, :, :], misc[:, 0:2 * COPIES].rearrange("p (c m) -> p c m", c=2)).then_inc(p_x0Ts, 1)
            dve.wait_ge(p_xz, 1)
            dve.wait_ge(ld_w, 32)
            v.tensor_tensor(xz, ybank[0:COPIES, :], bin_b, ALU.add).then_inc(p_xzs, 1)
            dve.wait_ge(p_xzs, 1)
            xs, zz = xz[:, 0:HID], xz[:, HID:2 * HID]
            v.tensor_scalar(sp[8], zz, -1.0, 80.0, ALU.mult, ALU.min).then_inc(p_zc, 1)
            dve.wait_ge(p_xsT, 1)
            v.tensor_copy(rowsT[:, :, :], misc[:, 0:2 * COPIES].rearrange("p (c m) -> p c m", c=2)).then_inc(p_xsTs, 1)
            dve.wait_ge(p_ez, 1)
            link(v.tensor_scalar(sp[8], sp[8], 1.0, None, ALU.add))
            link(v.reciprocal(sp[9], sp[8]))
            S0 = TC
            link(v.tensor_tensor(small[:, TZ - S0:TZ - S0 + HID], zz, sp[9], ALU.mult))
            dve.wait_ge(ld_d, 48)
            for half in range(2):
                turned = "p (r m e) -> p m r e"
                cols = slice(half * P, (half + 1) * P)
                link(v.tensor_tensor(small[:, TDX - S0 + half * P:TDX - S0 + (half + 1) * P].rearrange(
                    "p (m r e) -> p m r e", m=4, r=4), d_b[:, cols].rearrange(turned, m=4, r=4),
                    xs[:, cols].rearrange(turned, m=4, r=4), ALU.mult))
            link(v.tensor_tensor(small[:, TRB - S0:TRB - S0 + HID], x0[:, :], bo_b, ALU.add))
            link(v.tensor_tensor(small[:, THB - S0:THB - S0 + HID], h0[:, :], be_b, ALU.add))
            dve.wait_ge(p_dbc, 1)
            dve.wait_ge(ld_p, 96)
            link(v.tensor_tensor(dbc, ybank[0:COPIES, 0:NP], bp_b, ALU.add))
            dtp, Bl, Cl = dbc[:, 0:HID], dbc[:, HID:HID + STATE], dbc[:, HID + STATE:NP]
            link(v.tensor_copy(small[:, 0:P].rearrange("p (e n) -> p e n", n=STATE),
                               Cl.unsqueeze(1).to_broadcast([COPIES, GCH, STATE])))
            v.scalar_tensor_tensor(sp[0], dtp, -1.0, dtp, ALU.mult, ALU.max).then_inc(p_abs, 1)
            dve.wait_ge(p_exp, 1)
            link(v.tensor_scalar(sp[2], sp[1], 2.0, None, ALU.add))
            link(v.reciprocal(sp[3], sp[2]))
            link(v.tensor_tensor(sp[4], sp[1], sp[3], ALU.mult))
            link(v.tensor_tensor(sp[5], sp[4], sp[4], ALU.mult))
            link(v.tensor_scalar(sp[6], sp[5], 1.0 / 17, None, ALU.mult))
            for k in range(7, 0, -1):
                link(v.scalar_tensor_tensor(sp[6], sp[6], 1.0 / (2 * k + 1), sp[5], ALU.add, ALU.mult))
            link(v.scalar_tensor_tensor(sp[6], sp[6], 1.0, sp[4], ALU.add, ALU.mult))
            link(v.tensor_scalar(sp[7], dtp, 0.0, None, ALU.max))
            link(v.scalar_tensor_tensor(sp[2], sp[6], 2.0, sp[7], ALU.mult, ALU.add))
            dt = sp[2]
            v.tensor_tensor(sp[3], dt, xs, ALU.mult).then_inc(p_v, 1)
            dve.wait_ge(p_v, 1)

            def parts(k, val, hi, dst):
                dve.wait_ge(p_hi, k + 1)
                v.scalar_tensor_tensor(val, hi, not_first[:, :], val, ALU.mult, ALU.add).then_inc(p_r, 1)
                dve.wait_ge(p_mid, k + 1)
                v.scalar_tensor_tensor(dst, hi, last_copy[:, :], val, ALU.mult, ALU.add).then_inc(p_tab, 1)

            dve.wait_ge(consts2, 1)
            grid = "p (d n) -> p d n"
            dve.wait_ge(p_eA, 1)
            v.tensor_tensor(tab_v.rearrange(grid, n=STATE), expA.rearrange(grid, n=STATE),
                            dt.unsqueeze(2).to_broadcast([COPIES, HID, STATE]), ALU.mult).then_inc(p_arg, 1)
            parts(0, small, small_h, table[:, TC:NTAB])
            dve.wait_ge(lev_back, 16)
            link(v.tensor_scalar(onehot, lev_all, lvl_id[:, :], None, ALU.is_equal))
            parts(1, tab_v, tab_h, table[:, TA:TA + T_N])
            dve.wait_ge(p_tab, 2)
            v.tensor_tensor(tab_v.rearrange(grid, n=STATE), sp[3].unsqueeze(2).to_broadcast([COPIES, HID, STATE]),
                            Bl.unsqueeze(1).to_broadcast([COPIES, HID, STATE]), ALU.mult).then_inc(p_v, 1)
            parts(2, tab_v, tab_h, table[:, TB:TB + T_N])
            dve.wait_ge(ld_g, 48)

            def scan(c, q):
                dve.wait_ge(x_copied, XPER * c + xpos(q) + 1)
                dve.wait_ge(b_ready, GROUPS * c + q + 1)
                if q % 4 == 0:
                    wait(dve, sum_done, 8 * c + q // 4 - HRING // 4 + 1)
                v.tensor_tensor_scan(hslot(q), aslot(q), bbank[q % 3][:, :], 0.0, ALU.mult, ALU.add).then_inc(scan_done, 1)

            def mul(c, q):
                dve.wait_ge(scan_done, GROUPS * c + q + 1)
                dve.wait_ge(x_copied, XPER * c + C_POS + 2)
                v.tensor_tensor(hslot(q), hslot(q), c_sb, ALU.mult).then_inc(mul_v, 1)

            def gate_z(c, half):
                dve.wait_ge(sum_done, 8 * c + 4 * half + 4)
                dve.wait_ge(x_copied, XPER * c + Z_POS[half] + 1)
                wait(dve, pre_ready, 4 * c)
                v.tensor_tensor(v_sb[:, half * CHUNK:(half + 1) * CHUNK], ybank[:, :],
                                z_sb, ALU.mult).then_inc(v_done, 1)

            def weight_lo(c, k):
                dve.wait_ge(w_hi, PIECES * c + k + 1)
                hi, lo, at = (W1H, W1L, k * PIECE) if k < 4 else (W2H, W2L, (k - 4) * PIECE)
                v.scalar_tensor_tensor(wsec(c, lo, at, PIECE), stage[:, (k % 2) * PIECE:(k % 2 + 1) * PIECE], W_UP,
                                       wsec(c, hi, at, PIECE), ALU.mult, ALU.subtract).then_inc(w_lo, 1)

            def stats(src, j):
                done(v.bn_stats(bn6[:, j, :], src))

            def aggregate():
                after()
                done(v.tensor_copy(carried[:, :], bn6[:, 0, 0:1]))
                for j in range(TILES):
                    done(v.bn_aggr(mv[:, j, :], bn6[:, j, :]))

            def variance(ready):
                after()
                v.tensor_scalar(nrm[:, 0, :], mv[:, :, 1], EPS, None, ALU.add).then_inc(ready, 1)

            def end_op(cp, q):
                for j in range(TILES):
                    if q == S_STATS1[j]:
                        dve.wait_ge(pre_ready, TILES * cp + 2 * (j // 2) + 2)
                        stats(pre[:, j * HID:(j + 1) * HID], j)
                if q == S_GAMMA:
                    aggregate()
                if q in (S_GAMMA, S_GAMMA + 1):
                    if q == S_GAMMA:
                        wait(dve, xT_ready, 2 * cp)
                        after()
                    for j in range(2 * (q - S_GAMMA), 2 * (q - S_GAMMA) + 2):
                        v.scalar_tensor_tensor(rows4[:, j, :], pre[:, j * HID:(j + 1) * HID], mv[:, j, 0:1],
                                               gamma_b[:, :], ALU.subtract, ALU.mult).then_inc(t1_ready, 1)
                    if q == S_GAMMA:
                        variance(var1)
                if q == S_H - 1:
                    dve.wait_ge(std1, cp + 1)
                    done(v.reciprocal(nrm[:, 2, :], nrm[:, 1, :]))
                if q in (S_H, S_H + 1):
                    if q == S_H:
                        after()
                        dve.wait_ge(t1_ready, TILES * cp + TILES)
                        dve.wait_ge(hb_ready, cp + 1)
                    for j in range(2 * (q - S_H), 2 * (q - S_H) + 2):
                        v.scalar_tensor_tensor(rows4[:, j, :], rows4[:, j, :], nrm[:, 2, j:j + 1],
                                               pre[:, j * HID:(j + 1) * HID], ALU.mult, ALU.add).then_inc(h_ready, 1)
                if q in (S_STATS2, S_STATS2 + 1):
                    if q == S_STATS2:
                        dve.wait_ge(h_ready, TILES * cp + TILES)
                    for j in range(2 * (q - S_STATS2), 2 * (q - S_STATS2) + 2):
                        stats(rows4[:, j, :], j)
                if q == S_STATS2 + 2:
                    aggregate()
                    variance(var2)
                if q == S_NORM2:
                    dve.wait_ge(std2, cp + 1)
                    done(v.reciprocal(nrm[:, 2, :], nrm[:, 1, :]))
                if q == S_NORM2 + 1:
                    after()
                    v.scalar_tensor_tensor(nrm[:, 3, :], mv[:, :, 0], -1.0, nrm[:, 2, :], ALU.mult,
                                           ALU.mult).then_inc(nrm2, 1)
                if q == S_LOW:
                    dve.wait_ge(hi_ready, cp + 1)
                    v.scalar_tensor_tensor(x_lo, rows4[:, :, :], X_UP, x_hi, ALU.mult, ALU.subtract)

            def first_max(src, k, i):
                m = top[:, k, :]
                if i == 0:
                    done(v.tensor_reduce(m, src, AX.X, ALU.max))
                elif i == 1:
                    done(v.tensor_tensor(eq[:, :, :], src, m.unsqueeze(2).to_broadcast([P, TILES, NE]), ALU.is_ge))
                elif i == 2:
                    done(v.tensor_tensor_scan(cs[:, :], segmask[:, :], eq[:, :, :].rearrange("p j e -> p (j e)"), 0.0,
                                              ALU.mult, ALU.add))
                else:
                    return v.scalar_tensor_tensor(hot[:, :, k, :], cs[:, :].rearrange("p (j e) -> p j e", e=NE), 1.0,
                                                  eq[:, :, :], ALU.is_equal, ALU.mult)

            def choose(cp, i):
                if i == 0:
                    dve.wait_ge(logit_ready, 2 * cp + 2)
                    done(v.tensor_copy(lg[:, :, :], logit_ps))
                    return
                after()
                if i < 4:
                    first_max(lg[:, :, :], 0, i - 1)
                elif i == 4:
                    done(first_max(lg[:, :, :], 0, 3))
                elif i == 5:
                    done(v.scalar_tensor_tensor(lg2[:, :, :], hot[:, :, 0, :], -1.0e30, lg[:, :, :], ALU.mult, ALU.add))
                elif i < 9:
                    first_max(lg2[:, :, :], 1, i - 6)
                elif i == 9:
                    first_max(lg2[:, :, :], 1, 3).then_inc(hot_ready, 1)
                elif i == 10:
                    dve.wait_ge(hot_ready, cp + 1)
                    done(v.tensor_tensor(top[:, 2, :], top[:, 0, :], top[:, 1, :], ALU.subtract))
                    done(v.tensor_tensor(dif[:, :, :], hot[:, :, 0, :], hot[:, :, 1, :], ALU.subtract))
                elif i == 11:
                    done(v.tensor_tensor(payload[:, :, HID:HID + NE], dif[:, :, :],
                                         top[:, 2, :].unsqueeze(2).to_broadcast([P, TILES, NE]), ALU.mult))
                    done(v.tensor_scalar(tok_f[:, :], tok_f[:, :], float(CHUNK), None, ALU.add))
                else:
                    done(v.tensor_copy(payload[:, :, XW - 1:XW].bitcast(i32), tok_f[:, :].unsqueeze(2)))

            CHOOSE_STEPS, PLACE_STEPS = 13, 12

            def place(cp, i):
                flat = "p j k e -> p j (k e)"
                if i == 0:
                    dve.wait_ge(cnt_ready, cp + 1)
                    v.tensor_copy(counts[:, :, :], cnt_ps).then_inc(cnt_taken, 1)
                    return
                if i == 1:
                    dve.wait_ge(cnt_taken, cp + 1)
                after()
                if i < 5:
                    done(v.tensor_tensor(seen[:, i, :], counts[:, 1, (i - 1) * 2 * NE:i * 2 * NE], seen[:, i - 1, :], ALU.add))
                elif i == 5:
                    done(v.tensor_tensor(pos[:, :, :, :].rearrange(flat), counts[:, 0, :].rearrange("p (j f) -> p j f", j=TILES),
                                         seen[:, 0:TILES, :], ALU.add))
                elif i == 6:
                    done(v.tensor_copy(seen[:, 0, :], seen[:, TILES, :]))
                    done(v.tensor_scalar(kept[:, :, :, :].rearrange(flat), pos[:, :, :, :].rearrange(flat), float(CAP), None, ALU.min))
                    done(v.tensor_tensor(mul2[:, :, :, :].rearrange(flat), hot[:, :, :, :].rearrange(flat),
                                         pos[:, :, :, :].rearrange(flat), ALU.mult))
                elif i == 7:
                    done(v.tensor_tensor(slot[:, :, :], kept[:, :, 0, :], kept[:, :, 1, :], ALU.add))
                    done(v.tensor_reduce(red2[:, :, :], mul2[:, :, :, :], AX.X, ALU.add))
                elif i == 8:
                    done(v.tensor_tensor(slot[:, :, :], slot[:, :, :], row_base[:, :].unsqueeze(1).to_broadcast([P, TILES, NE]), ALU.add))
                    done(v.tensor_scalar(drop[:, :, :], red2[:, :, :], float(CAP), DROP, ALU.is_gt, ALU.mult))
                elif i == 9:
                    for k in range(2):
                        done(v.tensor_tensor(mul1[:, :, k, :], hot[:, :, k, :], slot[:, :, :], ALU.mult))
                elif i == 10:
                    done(v.tensor_reduce(red1[:, :, :], mul1[:, :, :, :], AX.X, ALU.add))
                else:
                    v.tensor_tensor(slot_i[:, :, :], red1[:, :, :], drop[:, :, :], ALU.add).then_inc(route_done, 1)
                    dve.wait_ge(route_done, cp + 1)

            def routing(cp, q, odd):
                i = 2 * (q - S_CHOOSE) + odd
                if 0 <= i < CHOOSE_STEPS:
                    choose(cp, i)
                i = 2 * (q - S_PLACE) + odd
                if 0 <= i < PLACE_STEPS:
                    place(cp, i)

            def body(c, main, prev, prev2):
                for q in range(GROUPS):
                    if main:
                        scan(c, q)
                    if prev:
                        routing(c - 1, q, 0)
                    if prev2:
                        routing(c - 2, q + GROUPS, 0)
                    if prev and q == 0:
                        mul(c - 1, VEC_MULS[-1])
                    if main:
                        for k in VEC_MULS:
                            if q == max(k, 4) + 1:
                                mul(c, k)
                        if q == S_GATE[0]:
                            gate_z(c, 0)
                    if prev:
                        for k in range(PIECES):
                            if q == piece_slot(k):
                                weight_lo(c - 1, k)
                        if q == S_GATE[1]:
                            gate_z(c - 1, 1)
                        end_op(c - 1, q)
                        routing(c - 1, q, 1)
                    if prev2:
                        routing(c - 2, q + GROUPS, 1)

            LN_STEPS, CHOOSE_COUNT, PLACE_COUNT = TILES + (1 + TILES) + 1, 14, 15
            PER_BODY = 2 * LN_STEPS + CHOOSE_COUNT + PLACE_COUNT
            body(0, True, False, False)
            body(1, True, True, False)
            before = n[0]
            with dve.Fori(2, NCHUNK) as c:
                base[0] = (c - 2) * PER_BODY + before
                n[0] = 0
                body(c, True, True, True)
                assert n[0] == PER_BODY, n[0]
            n[0] = before + PER_BODY * (NCHUNK - 2)
            base[0] = 0
            body(NCHUNK, False, True, True)
            body(NCHUNK + 1, False, False, True)

            link(v.tensor_scalar(cnt[:, :], seen[0:1, TILES, :], float(CAP), None, ALU.min))
            link(v.tensor_tensor(n8[:, :], cnt[:, 0:NE], cnt[:, NE:2 * NE], ALU.add))
            link(v.tensor_tensor(gt[:, :, :], n8[:, :].unsqueeze(2).to_broadcast([1, NE, NT10]),
                                 thr[:, :].unsqueeze(1).to_broadcast([1, NE, NT10]), ALU.is_gt))
            link(v.tensor_reduce(nt[:, :], gt[:, :, :], AX.X, ALU.add))
            link(v.tensor_tensor_scan(ntc[:, :], one8[:, :], nt[:, :], 0.0, ALU.mult, ALU.add))
            link(v.tensor_tensor(le[:, :, :], tile_no[:, :].unsqueeze(2).to_broadcast([1, FT, NE]), ntc[:, :].unsqueeze(1).to_broadcast([1, FT, NE]), ALU.is_ge))
            link(v.tensor_tensor(le2[:, :, :], le[:, :, :], nt[:, :].unsqueeze(1).to_broadcast([1, FT, NE]), ALU.mult))
            link(v.tensor_reduce(ex[:, :], le[:, :, :], AX.X, ALU.add))
            link(v.tensor_reduce(bel[:, :], le2[:, :, :], AX.X, ALU.add))
            link(v.tensor_tensor(rw1[:, :], tile_no[:, :], bel[:, :], ALU.subtract))
            link(v.tensor_scalar(rw2[:, :], ex[:, :], float(REGION), None, ALU.mult))
            link(v.scalar_tensor_tensor(bel[:, :], rw1[:, :], float(TT), rw2[:, :], ALU.mult, ALU.add))
            link(v.tensor_scalar(tile_row[:, :], bel[:, :], float(DUMMY_ROW), None, ALU.min))
            link(v.tensor_copy(tile_count[:, :], ntc[:, NE - 1:NE]))
            v.tensor_scalar(tile_expert[:, :], ex[:, :], float(NE - 1), None, ALU.min).then_inc(tiles_ready, 1)
            dve.drain().then_inc(scan_phase_over, 1)
            dve.wait_ge(scan_phase_over, 4)

            def low_half(i, s):
                for b in range(4):
                    dve.wait_ge(f_hi, 4 * i + b + 1)
                    if b == 0:
                        wait(dve, f_y, i - FR + 1)
                    pair = "p (j t) -> p j t"
                    v.scalar_tensor_tensor(h_lo[s][:, 2 * b:2 * b + 2, :], g_sb[b].rearrange(pair, j=2), H_UP,
                                           h_hi[s][:, 2 * b:2 * b + 2, :], ALU.mult, ALU.subtract).then_inc(f_lo, 1)

            def meta(i, s, m):
                back = 0.5 / (H_UP * W_UP)
                dve.wait_ge(f_tg, i + 1)
                wait(dve, f_ys, i - FR + 1)
                v.tensor_scalar(gate[s][:, :], tgate[s][:, :], back, back, ALU.mult, ALU.add).then_inc(f_gate, 1)
                dve.wait_ge(f_in[s], 16 * (m + 1))
                wait(dve, f_out, 32 * (i - FR + 1))
                v.tensor_copy(tok_i[s][:, :].unsqueeze(2), x_in[s][:, :, XW - 1:XW].bitcast(i32)).then_inc(f_meta, 1)

            def evacuate(i, s):
                dve.wait_ge(f_y, i + 1)
                dve.wait_ge(f_gate, i + 1)
                wait(dve, f_out, 32 * (i - FR + 1))
                last = None
                for k in range(2):
                    last = v.tensor_scalar(y_sb[s][:, k, :], yb[s][:, k * HID:(k + 1) * HID], gate[s][:, k:k + 1], None, ALU.mult)
                last.then_inc(f_ys, 1)

            meta(0, 0, 0)
            low_half(0, 0)
            meta(1, 1, 0)

            def step(m, u):
                i, s, _ = ahead(m, u, 0)
                i1, s1, _ = ahead(m, u, 1)
                i2, s2, m2 = ahead(m, u, 2)
                low_half(i1, s1)
                evacuate(i, s)
                meta(i2, s2, m2)

            tile_steps(dve, step)

        @block.tensor
        def _(pe):
            mm = nc.tensor.matmul
            pe.wait_ge(consts2, 1)
            pe.wait_ge(p_x0, 1)
            for k in range(2):
                last = nc.tensor.transpose(misc[:, k * COPIES:(k + 1) * COPIES], x0[:, k * P:(k + 1) * P], ident[0:COPIES, 0:COPIES])
            last.then_inc(p_x0T, 1)
            pe.wait_ge(p_x0Ts, 1)
            pe.wait_ge(ld_w, 32)
            for k in range(2):
                last = mm(ybank[0:COPIES, :], rowsT[:, k, :], pro_w[:, k, :], start=(k == 0), stop=(k == 1))
            last.then_inc(p_xz, 1)
            pe.wait_ge(p_xzs, 1)
            for k in range(2):
                last = nc.tensor.transpose(misc[:, k * COPIES:(k + 1) * COPIES], xz[:, k * P:(k + 1) * P], ident[0:COPIES, 0:COPIES])
            last.then_inc(p_xsT, 1)
            pe.wait_ge(p_xsTs, 1)
            pe.wait_ge(ld_p, 96)
            for k in range(2):
                last = mm(ybank[0:COPIES, 0:NP], rowsT[:, k, :], pro_p[:, k, :], start=(k == 0), stop=(k == 1))
            last.then_inc(p_dbc, 1)
            pe.wait_ge(p_tab, 3)
            pe.wait_ge(ld_g, 48)

            def hot_cols(c, at, n):
                return onehot[:, bass.ds(c * CHUNK + at, n)]

            def expand(c, pos_, lhsT, at=0, n=CHUNK):
                wait(pe, x_copied, XPER * c + pos_ - 1)
                mm(xbank[pos_ % 2][:, 0:n], lhsT, hot_cols(c, at, n), start=True, stop=True).then_inc(x_ready, 1)

            def expand_decay(c, q):
                expand(c, xpos(q), table[:, TA + q * P:TA + (q + 1) * P])
                if q == 3:
                    for k in range(2):
                        expand(c, C_POS + k, table[:, TC:TC + P], k * TT, TT)
                if q == 17:
                    expand(c, Z_POS[0], table[:, TZ:TZ + P])
                if q == 31:
                    expand(c, Z_POS[1], table[:, TZ + P:TZ + 2 * P])

            def expand_input(c, q):
                wait(pe, scan_done, GROUPS * c + (q - 2 if q > 2 else (-1, 0, -2)[q]))
                mm(bbank[q % 3][:, :], table[:, TB + q * P:TB + (q + 1) * P], hot_cols(c, 0, CHUNK),
                   start=True, stop=True).then_inc(b_ready, 1)

            def sum_states(c, b):
                half, blk = b // 4, b % 4
                if blk == 0:
                    wait(pe, v_done, 2 * c + half)
                    mm(ybank[:, :], table[:, TDX + half * P:TDX + (half + 1) * P], hot_cols(c, 0, CHUNK), start=True, stop=False)
                q1 = 4 * b + 4
                pe.wait_ge(mul_v, len(VEC_MULS) * c + muls_before(VEC_MULS, q1))
                pe.wait_ge(mul_p, len(POOL_MULS) * c + muls_before(POOL_MULS, q1))
                for m in range(4):
                    last = mm(ybank[32 * m:32 * m + 32, :], sel[:, blk, :], hslot(4 * b + m), start=False, stop=(blk == 3))
                last.then_inc(sum_done, 1)

            def project_out(cp, j):
                if j == 0:
                    pe.wait_ge(v_done, 2 * cp + 2)
                    wait(pe, cnt_taken, cp)
                o = pre[:, j * HID:(j + 1) * HID]
                for half in range(2):
                    at = half * CHUNK + j * P
                    mm(o, v_sb[:, at:at + P], wo[:, half, :], start=(half == 0), stop=False)
                mm(o, hot_cols(cp, j * P, P), table[:, TRB:TRB + HID], start=False, stop=True).then_inc(pre_ready, 1)

            def row_base_terms(cp):
                pe.wait_ge(t1_ready, TILES * cp + TILES)
                for j in range(TILES):
                    last = mm(pre[:, j * HID:(j + 1) * HID], hot_cols(cp, j * P, P), table[:, THB:THB + HID], start=True, stop=True)
                last.then_inc(hb_ready, 1)

            def turn_x2(cp, part_):
                pe.wait_ge(x2_ready, TILES * cp + 2 * part_ + 2)
                for j in (2 * part_, 2 * part_ + 1):
                    for k in range(2):
                        at = j * HID + k * P
                        last = nc.tensor.transpose(pre[:, at:at + P], rows4[:, j, k * P:(k + 1) * P], ident[:, :])
                last.then_inc(xT_ready, 1)

            def logits(cp, part_):
                pe.wait_ge(xT_copied, 2 * cp + part_ + 1)
                for j in range(2):
                    for k in range(2):
                        last = mm(logit_ps[:, 2 * part_ + j, :], x2T[:, j, k, :], rw[:, k, :], start=(k == 0), stop=(k == 1))
                last.then_inc(logit_ready, 1)

            def count_pairs(cp):
                pe.wait_ge(hot_ready, cp + 1)
                oh = hot[:, :, :, :].rearrange("p j k e -> p (j k e)")
                mm(cnt_ps[:, 0, :], tri[:, :], oh, start=True, stop=True)
                mm(cnt_ps[:, 1, :], ones[:, :], oh, start=True, stop=True).then_inc(cnt_ready, 1)

            def body(c, main, prev, prev2):
                for q in range(GROUPS):
                    if main:
                        for k in ((0, 1) if q == 0 else (q + 1,)):
                            if k < GROUPS:
                                expand_decay(c, k)
                        expand_input(c, q)
                        if q >= T_SUM and (q - T_SUM) % 4 == 0:
                            sum_states(c, (q - T_SUM) // 4)
                    if prev:
                        if q < T_SUM and q % 4 == 0:
                            sum_states(c - 1, (q + GROUPS - T_SUM) // 4)
                        for j in range(TILES):
                            if q == T_PROJECT[j]:
                                project_out(c - 1, j)
                        if q == T_BASE:
                            row_base_terms(c - 1)
                        for k in range(2):
                            if q == T_TURN[k]:
                                turn_x2(c - 1, k)
                            if q == T_LOGITS[k]:
                                logits(c - 1, k)
                    if prev2 and q + GROUPS == T_COUNT:
                        count_pairs(c - 2)

            chunks(pe, body)
            pe.drain().then_inc(scan_phase_over, 1)
            pe.wait_ge(scan_phase_over, 4)
            pe.wait_ge(tiles_ready, 1)
            pe.wait_ge(w_lo, PIECES * NCHUNK)

            def expert_of(i):
                return pe.value_load(tile_expert[0:1, bass.ds(i, 1)], min_val=0, max_val=NE - 1)

            def turn_rows(i, s, m):
                pe.wait_ge(f_in[s], 16 * (m + 1))
                wait(pe, f_xT, i)
                for k in range(2):
                    halves = x_in[s][:, k, 0:HID].bitcast(f16)
                    for l in range(2):
                        for c in range(2):
                            last = nc.tensor.transpose(xTp16[:, l, c, k * P:(k + 1) * P],
                                                       halves[:, l * HID + c * P:l * HID + (c + 1) * P], ident16[:, :])
                last.then_inc(f_tp, 1)

            def first_product(i, s):
                e = expert_of(i)
                pe.wait_ge(f_xT, i + 1)
                for j in range(8):
                    b = j // 2
                    if j % 2 == 0:
                        wait(pe, f_g, 4 * (i - 1) + b + 1)
                    o = bank[b][:, (j % 2) * TT:(j % 2 + 1) * TT]
                    for c in range(2):
                        at = c * FFN + j * P
                        wh, wl = wsec(e, W1H, at, P), wsec(e, W1L, at, P)
                        mm(o, wh, x_T[s][:, 0, c, :], start=(c == 0), stop=False)
                        mm(o, wh, x_T[s][:, 1, c, :], start=False, stop=False)
                        last = mm(o, wl, x_T[s][:, 0, c, :], start=False, stop=(c == 1))
                    if j % 2 == 1:
                        last.then_inc(f_h, 1)

            def second_product(i, s):
                e = expert_of(i)
                pe.wait_ge(f_lo, 4 * i + 4)
                wait(pe, f_ys, i - FR + 1)
                for k in range(2):
                    o = yb[s][:, k * HID:(k + 1) * HID]
                    for j in range(8):
                        hh, hl = h_hi[s][:, j, k * P:(k + 1) * P], h_lo[s][:, j, k * P:(k + 1) * P]
                        wh, wl = wsec(e, W2H, j * HID, HID), wsec(e, W2L, j * HID, HID)
                        mm(o, hh, wh, start=(j == 0), stop=False)
                        mm(o, hh, wl, start=False, stop=False)
                        last = mm(o, hl, wh, start=False, stop=(j == 7))
                last.then_inc(f_y, 1)

            turn_rows(0, 0, 0)
            first_product(0, 0)
            turn_rows(1, 1, 0)

            def step(m, u):
                i, s, _ = ahead(m, u, 0)
                i1, s1, _ = ahead(m, u, 1)
                i2, s2, m2 = ahead(m, u, 2)
                first_product(i1, s1)
                turn_rows(i2, s2, m2)
                second_product(i, s)

            tile_steps(pe, step)


def kernel(**inputs):
    import numpy as np
    import concourse.bacc as bacc
    from concourse.bass_utils import run_bass_kernel_spmd

    order = np.array(channel_order())
    a = {k: np.asarray(v) for k, v in inputs.items()}
    z_rows = HID + order
    w_in = np.concatenate([a["L0_attn_w_in"][:HID], a["L0_attn_w_in"][z_rows]], axis=0)
    b_in = np.concatenate([a["L0_attn_b_in"][:HID], a["L0_attn_b_in"][z_rows]], axis=0)
    laid = {
        "x_tok": a["x"], "level_emb": a["L0_tok_level_emb"], "w_inT": w_in.T, "b_in": b_in,
        "w_dtT": a["L0_attn_w_dt"].T, "b_dt": a["L0_attn_b_dt"], "a_log": a["L0_attn_A_log"],
        "w_BT": a["L0_attn_w_B"].T, "b_B": a["L0_attn_b_B"], "w_CT": a["L0_attn_w_C"].T, "b_C": a["L0_attn_b_C"],
        "d_skip": a["L0_attn_D"], "w_outT": a["L0_attn_w_out"].T[order], "b_out": a["L0_attn_b_out"],
        "gamma": a["L0_attn_gamma"], "beta": a["L0_attn_beta"], "router_wT": a["L0_ffn_router_w"].T,
        "w1": a["L0_ffn_w1"], "w2": a["L0_ffn_w2"],
    }
    nc = bacc.Bacc("TRN2", target_bir_lowering=False, num_devices=1)
    arrays, args = {}, []
    for name, value in laid.items():
        value = np.ascontiguousarray(value)
        arrays[f"in_{name}"] = value
        args.append(nc.dram_tensor(f"in_{name}", value.shape, mybir.dt.from_np(value.dtype), kind="ExternalInput").ap())
    out = nc.dram_tensor("out_0", (NTOK + TT, HID), mybir.dt.float32, kind="ExternalOutput").ap()
    program(nc, *args, out)
    r = run_bass_kernel_spmd(nc, [arrays], core_ids=[0])
    return r.results[0]["out_0"][:NTOK].reshape(BATCH, SEQ, HID)
```

```python
import concourse.bass as bass
from concourse import mybir
from contextlib import ExitStack

BATCH, SEQ = 32, 128
NTOK = BATCH * SEQ
LEVELS = 32
HID = 256
STATE = 16
FFN = 1024
EXPERTS = 8
TOPK = 2
CAP = max(1, int(1.25 * NTOK / EXPERTS * TOPK))
TOK_SCALE = 0.15
EPS = 1e-5
P = 128

GCH = P // STATE
GROUPS = HID // GCH
CHUNK = 512
NCHUNK = NTOK // CHUNK
TILES = CHUNK // P
COPIES = 3 * LEVELS

TT = 256
REGION = TOPK * CAP
DUMMY_ROW = EXPERTS * REGION
FR = 3
FTILES = (TOPK * NTOK + EXPERTS * (TT - 1)) // TT
NROWS = DUMMY_ROW + TT
XW = HID + EXPERTS + 1
INIT_PARTS = 9
DROP = 1.0e6

X_UP = 16.0
W_UP = 64.0
H_UP = 16.0


def channel_order():
    order = []
    for half in range(2):
        for row in range(P):
            strip, block, e = row // 32, (row % 32) // GCH, row % GCH
            order.append(half * P + (4 * block + strip) * GCH + e)
    return order


def program(nc, x_tok, level_emb, w_inT, b_in, w_dtT, b_dt, a_log, w_BT, b_B, w_CT, b_C, d_skip,
            w_outT, b_out, gamma, beta, router_wT, w1, w2, out):
    f32, bf16, f16, i32 = mybir.dt.float32, mybir.dt.bfloat16, mybir.dt.float16, mybir.dt.int32
    ALU, ACT, AX = mybir.AluOpType, mybir.ActivationFunctionType, mybir.AxisListType

    ctx = ExitStack()
    with ctx:
        def sb(name, shape, dt=f32):
            return ctx.enter_context(nc.sbuf_tensor(name, shape, dt))

        def ps(name, shape, dt=f32):
            return ctx.enter_context(nc.psum_tensor(name, shape, dt))

        def sem(name):
            return ctx.enter_context(nc.semaphore(name))

        level_dram = nc.dram_tensor("level_scratch", [BATCH, SEQ], f32, kind="Internal").ap()
        rows_dram = nc.dram_tensor("dispatch_rows", [NROWS, XW], f32, kind="Internal").ap()

        WSEC = 2 * FFN
        weights = sb("weights", [P, EXPERTS * 4 * WSEC], f16)
        W1H, W1L, W2H, W2L = range(4)

        def wsec(e, which, at, n):
            return weights[:, bass.ds((e * 4 + which) * WSEC + at, n)]

        scratch = weights[:, 4 * 4 * WSEC:].bitcast(f32)
        T_N = HID * STATE
        expA = scratch[0:COPIES, 0:T_N]
        lev_all = scratch[0:COPIES, T_N:2 * T_N]
        QUARTERS = 4
        QN, QG = T_N // QUARTERS, GROUPS // QUARTERS
        b_val = scratch[0:COPIES, 2 * T_N:3 * T_N]
        first = weights[:, 0:4 * WSEC].bitcast(f32)[0:COPIES, :]
        a_val = [first[:, k * QN:(k + 1) * QN] for k in range(2)]
        a_hi, b_hi = [first[:, 2 * QN + k * QN // 2:2 * QN + (k + 1) * QN // 2].bitcast(bf16) for k in range(2)]

        arena_n = 17472 - FFN - CHUNK
        arena = sb("arena", [P, arena_n])
        used = [0, 0]

        def part(phase, n, dt=f32):
            words = n if dt in (f32, i32) else n // 2
            at = used[phase]
            used[phase] += words
            assert used[phase] <= arena_n
            a = arena[:, at:at + words]
            return a if dt == f32 else a.bitcast(dt)

        TA, TB, TC = 0, T_N, 2 * T_N
        TDX, TZ, TRB, THB = [TC + P + k * HID for k in range(4)]
        NTAB = 2 * T_N + P + 4 * HID
        SMALL, SMALL_1 = NTAB - TC, TZ - TC
        table = part(0, NTAB, bf16)[0:COPIES, :]
        onehot = part(0, NTOK, bf16)[0:COPIES, :]
        HRING, ARING = 16, 4
        h_ring = [part(0, HRING // 2 * CHUNK), weights[:, (EXPERTS - 1) * 4 * WSEC:].bitcast(f32)]
        a_all = part(0, ARING * CHUNK)
        cz_sb = part(0, 2 * CHUNK)
        c_sb, z_sb = cz_sb[:, 0:CHUNK], cz_sb[:, CHUNK:]
        v_sb = part(0, 2 * CHUNK)
        PIECE = FFN // 2
        PIECES = 8
        stage_start = used[0]
        stage = part(0, 2 * PIECE)
        x_in = [part(1, 2 * XW).rearrange("p (s w) -> p s w", s=2) for _ in range(FR)]
        x_T = [part(1, 2 * 2 * TT, f16).rearrange("p (l c t) -> p l c t", l=2, c=2) for _ in range(FR)]
        h_hi = [part(1, EXPERTS * TT, f16).rearrange("p (j t) -> p j t", j=8) for _ in range(FR)]
        h_lo = [part(1, EXPERTS * TT, f16).rearrange("p (j t) -> p j t", j=8) for _ in range(FR)]
        g_sb = [part(1, 2 * TT) for _ in range(4)]
        y_sb = [part(1, 2 * HID).rearrange("p (s n) -> p s n", s=2) for _ in range(FR)]

        def hslot(q):
            half, k = divmod(q % HRING, HRING // 2)
            return h_ring[half][:, k * CHUNK:(k + 1) * CHUNK]

        def aslot(q):
            return a_all[:, (q % ARING) * CHUNK:(q % ARING + 1) * CHUNK]

        rows4 = sb("rows4", [P, TILES, HID])
        x2T = v_sb[:, CHUNK:].rearrange("p (j c t) -> p j c t", j=2, c=2)
        payload = sb("payload", [P, TILES, XW])
        x_hi = payload[:, :, 0:HID].bitcast(f16)[:, :, 0:HID]
        x_lo = payload[:, :, 0:HID].bitcast(f16)[:, :, HID:2 * HID]
        bn6 = sb("bn6", [P, TILES, 6])
        mv = sb("mv", [P, TILES, 2])
        nrm = sb("nrm", [P, 4, TILES])
        carried = sb("carried", [P, 1])

        ident = sb("ident", [P, P])
        ident16 = sb("ident16", [P, P], f16)
        tri = sb("tri", [P, P], bf16)
        ones = sb("ones", [P, P], bf16)
        sel = sb("sel", [P, 4, 32])
        gamma_b = sb("gamma_b", [P, HID])
        wo = sb("wo", [P, 2, HID])
        rw = sb("rw", [P, 2, EXPERTS])
        segmask = sb("segmask", [P, TILES * EXPERTS])
        row_base = sb("row_base", [P, EXPERTS])
        tok_f = sb("tok_f", [P, TILES])
        lvl_id = sb("lvl_id", [COPIES, 1])
        not_first = sb("not_first", [COPIES, 1])
        last_copy = sb("last_copy", [COPIES, 1])

        pro = weights[:, 3 * 4 * WSEC:4 * 4 * WSEC].bitcast(f32)
        pro_at = [0]

        def tmp(parts, *dims):
            n = 1
            for d in dims:
                n *= d
            at = pro_at[0]
            pro_at[0] += n
            assert pro_at[0] <= 2 * WSEC
            return pro[0:parts, at:at + n]

        xz = tmp(COPIES, 2 * HID)
        small = tmp(COPIES, SMALL)
        small_h = tmp(COPIES, SMALL // 2).bitcast(bf16)
        init_row = tmp(P, 2 * XW).rearrange("p (s w) -> p s w", s=2)
        pro2 = weights[:, 2 * 4 * WSEC:3 * 4 * WSEC].bitcast(f32)
        pro_w = pro2[:, 0:2 * 2 * HID].rearrange("p (c n) -> p c n", c=2)
        NP = HID + 2 * STATE
        pro_p = pro2[:, 1024:1024 + 2 * NP].rearrange("p (c n) -> p c n", c=2)
        bin_b = pro2[0:COPIES, 1600:1600 + 2 * HID]
        bp_b = pro2[0:COPIES, 2112:2112 + NP]
        d_b = pro2[0:COPIES, 2400:2400 + HID]
        bo_b = pro2[0:COPIES, 2656:2656 + HID]
        be_b = pro2[0:COPIES, 2912:2912 + HID]
        dbc = pro2[0:COPIES, 3168:3168 + NP]
        rowsT = pro2[:, 3456:3456 + 2 * COPIES].rearrange("p (c m) -> p c m", c=2)
        tmps = [weights[:, 1 * 4 * WSEC:2 * 4 * WSEC].bitcast(f32)[0:COPIES, k * HID:(k + 1) * HID] for k in range(10)]
        emb, h0, x0 = [
            weights[:, 0:4 * WSEC].bitcast(f32)[0:COPIES, k * HID:(k + 1) * HID] for k in range(13, 16)]
        lev = weights[:, 1 * 4 * WSEC:2 * 4 * WSEC].bitcast(f32)[0:BATCH, 10 * HID:10 * HID + 12 * SEQ]
        x_int = lev[:, 0:SEQ].bitcast(i32)
        x_f = lev[:, SEQ:2 * SEQ]
        acc = [lev[:, 2 * SEQ:3 * SEQ], lev[:, 3 * SEQ:4 * SEQ]]
        sc0, sc1, sc_o = lev[:, 4 * SEQ:6 * SEQ], lev[:, 6 * SEQ:8 * SEQ], lev[:, 8 * SEQ:10 * SEQ]
        lev_c = lev[:, 10 * SEQ:11 * SEQ]

        NE = EXPERTS
        lg = sb("lg", [P, TILES, NE])
        lg2 = sb("lg2", [P, TILES, NE])
        eq = sb("eq", [P, TILES, NE])
        cs = sb("cs", [P, TILES * NE])
        top = sb("top", [P, 3, TILES])
        hot = sb("hot", [P, TILES, 2, NE], bf16)
        dif = sb("dif", [P, TILES, NE])
        seen = sb("seen", [P, TILES + 1, 2 * NE])
        counts = sb("counts", [P, 2, TILES * 2 * NE])
        pos = sb("pos", [P, TILES, 2, NE])
        kept = sb("kept", [P, TILES, 2, NE])
        slot = sb("slot", [P, TILES, NE])
        mul1 = sb("mul1", [P, TILES, 2, NE])
        mul2 = sb("mul2", [P, TILES, 2, NE])
        red1 = sb("red1", [P, TILES, 2])
        red2 = sb("red2", [P, TILES, 2])
        drop = sb("drop", [P, TILES, 2])
        slot_i = sb("slot_i", [P, TILES, 2], i32)
        REGION_TILES = REGION // TT
        FT = -(-FTILES // FR) * FR + FR
        thr = sb("thr", [1, REGION_TILES])
        tile_no = sb("tile_no", [1, FT])
        one8 = sb("one8", [1, NE])
        row_at = [0]

        def row(n):
            at = row_at[0]
            row_at[0] += n
            assert row_at[0] <= 2 * CHUNK
            return cz_sb[0:1, at:at + n]

        le = row(FT * NE).rearrange("p (i e) -> p i e", e=NE)
        le2 = row(FT * NE).rearrange("p (i e) -> p i e", e=NE)
        gt = row(NE * REGION_TILES).rearrange("p (e k) -> p e k", e=NE)
        cnt, n8, nt, ntc = row(2 * NE), row(NE), row(NE), row(NE)
        ex, bel, rw1, rw2 = row(FT), row(FT), row(FT), row(FT)
        tile_expert = sb("tile_expert", [1, FT], i32)
        tile_row = sb("tile_row", [1, FT], i32)
        tile_count = sb("tile_count", [1, 1], i32)
        tgate = [part(1, 2) for k in range(FR)]
        gate = [part(1, 2) for k in range(FR)]
        tok_i = [part(1, 2, i32) for k in range(FR)]

        assert used[1] <= stage_start
        bank = [ps(f"bank{k}", [P, CHUNK]) for k in range(4)]
        zbank = bank[0]
        misc = ps("misc", [P, CHUNK])
        xbank, bbank = bank[0:2], bank[2:4] + [misc]
        ybank = ps("ybank", [P, CHUNK])
        pre = ps("pre", [P, TILES * HID])
        logit_ps = pre[:, 0:TILES * NE].rearrange("p (j e) -> p j e", e=NE)
        cnt_ps = pre[:, 64:192].rearrange("p (k f) -> p k f", k=2)
        xTp16 = misc[:, :].bitcast(f16).rearrange("p (l c t) -> p l c t", l=2, c=2)
        yb = [ybank, pre[:, 0:CHUNK], pre[:, CHUNK:2 * CHUNK]]

        ld_tok, ld_emb, ld_w, ld_p, ld_a, ld_d, ld_g = [sem(f"ld_{k}") for k in ("tok", "emb", "w", "p", "a", "d", "g")]
        consts = sem("consts")
        consts2 = sem("consts2")
        rows_init = sem("rows_init")
        vstep = sem("vstep")
        lev_out, lev_back = sem("lev_out"), sem("lev_back")
        p_var, p_std, p_x0, p_x0T, p_x0Ts, p_xs, p_x, p_z, p_xsT, p_xsTs, p_dbc, p_abs, p_exp = [
            sem(f"p_{k}") for k in ("var", "std", "x0", "x0T", "x0Ts", "xs", "x", "z", "xsT", "xsTs", "dbc", "abs", "exp")]
        p_zc, p_ez, p_eA, p_arg, p_dtx, p_hot, onehot_ready = [
            sem(f"p_{k}") for k in ("zc", "ez", "eA", "arg", "dtx", "hot", "onehot")]
        split_val, split_hi, split_rest, split_mid, table_ready = [
            {t: sem(f"{k}_{t}") for t in ("a", "b", "s")} for k in ("val", "hi", "rest", "mid", "table")]
        small_pool = sem("small_pool")
        x_ready, x_copied, b_ready, scan_done = sem("x_ready"), sem("x_copied"), sem("b_ready"), sem("scan_done")
        mul_v, mul_p, sum_done, v_done = sem("mul_v"), sem("mul_p"), sem("sum_done"), sem("v_done")
        pre_ready, hb_ready, var1, std1, t1_ready, h_ready = [
            sem(k) for k in ("pre_ready", "hb_ready", "var1", "std1", "t1_ready", "h_ready")]
        var2, std2, nrm2, x2_ready, hi_ready, xT_ready, xT_copied, logit_ready = [
            sem(k) for k in ("var2", "std2", "nrm2", "x2_ready", "hi_ready", "xT_ready", "xT_copied", "logit_ready")]
        hot_ready, cnt_ready, cnt_taken, route_done, scattered, h_stored = [
            sem(k) for k in ("hot_ready", "cnt_ready", "cnt_taken", "route_done", "scattered", "h_stored")]
        w_loaded = [sem("w_loaded0"), sem("w_loaded1")]
        w_hi, w_lo = sem("w_hi"), sem("w_lo")
        tiles_ready, scan_phase_over = sem("tiles_ready"), sem("scan_phase_over")
        f_in = [sem(f"f_in{k}") for k in range(FR)]
        f_tp, f_xT, f_h, f_g, f_hi, f_lo, f_y, f_tg, f_gate, f_meta, f_ys, f_out = [
            sem(f"f_{k}") for k in ("tp", "xT", "h", "g", "hi", "lo", "y", "tg", "gate", "meta", "ys", "out")]

        XPER = GROUPS + 4

        def xpos(q):
            return q if q < 4 else (q + 2 if q < 18 else q + 3)

        C_POS, Z_POS = 4, (20, 35)
        VEC_MULS = [q for q in range(7, GROUPS, 4) if q != 19]
        POOL_MULS = [q for q in range(GROUPS) if q not in VEC_MULS]

        def muls_before(group_list, q):
            return sum(1 for k in group_list if k < q)

        S_GATE, S_STATS1, S_GAMMA, S_H = (21, 4), (10, 11, 11, 12), 13, 17
        S_STATS2, S_NORM2, S_LOW, S_CHOOSE, S_PLACE = 19, 22, 27, 30, 36
        A_STD1, A_STD2, A_NORM2, A_HIGH, A_TURNED = 16, 24, 25, 27, (28, 30)
        T_PROJECT, T_BASE, T_TURN, T_LOGITS, T_COUNT = (8, 9, 11, 11), 17, (26, 28), (29, 31), 36
        P_SEND = 11
        T_SUM = 8

        def piece_slot(k):
            return 3 + 3 * k

        def wait(eng, s, n):
            if not isinstance(n, int) or n > 0:
                eng.wait_ge(s, n)

        def chunks(eng, body):
            body(0, True, False, False)
            body(1, True, True, False)
            with eng.Fori(2, NCHUNK) as c:
                body(c, True, True, True)
            body(NCHUNK, False, True, True)
            body(NCHUNK + 1, False, False, True)

        LEAST_TILES, EARLY = TOPK * (CAP // TT), CAP // TT
        assert NTOK >= CAP and LEAST_TILES > FR + 2 and EARLY > FR + 1
        assert PIECES == 2 * (FR + 1)

        def tile_steps(eng, *parts):
            count = eng.value_load(tile_count[0:1, 0:1], min_val=LEAST_TILES, max_val=FTILES)
            for u in range(FR):
                for part_, _ in parts:
                    part_(0, u)
            with eng.Fori(1, -(-FTILES // FR)) as m:
                for u in range(FR):
                    for part_, tiles_ahead in parts:
                        with eng.If(count > FR * m + u + tiles_ahead):
                            part_(m, u)
                        eng.end_ifs()

        def ahead(m, u, k):
            return FR * (m + (u + k) // FR) + (u + k) % FR, (u + k) % FR, m + (u + k) // FR

        block = ctx.enter_context(nc.Block())

        @block.sync
        def _(sp_):
            dma = sp_.dma_start
            dma(x_int, x_tok).then_inc(ld_tok, 16)
            for k in range(3):
                dma(emb[k * LEVELS:(k + 1) * LEVELS, :], level_emb).then_inc(ld_emb, 16)
            for k in range(2):
                half = slice(k * HID, (k + 1) * HID)
                dma(pro_w[:, :, half], w_inT[:, half].rearrange("(c p) n -> p c n", p=P)).then_inc(ld_w, 16)
            dma(bin_b, b_in.partition_broadcast(COPIES)).then_inc(ld_w, 16)
            dma(pro_p[:, :, 0:HID], w_dtT.rearrange("(c p) n -> p c n", p=P)).then_inc(ld_p, 16)
            dma(pro_p[:, :, HID:HID + STATE], w_BT.rearrange("(c p) n -> p c n", p=P)).then_inc(ld_p, 16)
            dma(pro_p[:, :, HID + STATE:NP], w_CT.rearrange("(c p) n -> p c n", p=P)).then_inc(ld_p, 16)
            dma(bp_b[:, 0:HID], b_dt.partition_broadcast(COPIES)).then_inc(ld_p, 16)
            dma(bp_b[:, HID:HID + STATE], b_B.partition_broadcast(COPIES)).then_inc(ld_p, 16)
            dma(bp_b[:, HID + STATE:NP], b_C.partition_broadcast(COPIES)).then_inc(ld_p, 16)
            dma(expA, a_log.rearrange("d n -> (d n)").partition_broadcast(COPIES)).then_inc(ld_a, 16)
            dma(d_b, d_skip.partition_broadcast(COPIES)).then_inc(ld_d, 16)
            dma(bo_b, b_out.partition_broadcast(COPIES)).then_inc(ld_d, 16)
            dma(be_b, beta.partition_broadcast(COPIES)).then_inc(ld_d, 16)
            sp_.wait_ge(p_hot, 1)
            dma(level_dram, lev_c).then_inc(lev_out, 16)
            dma(gamma_b[:, :], gamma.partition_broadcast(P)).then_inc(ld_g, 16)
            dma(wo[:, :, :], w_outT.rearrange("(c p) n -> p c n", p=P)).then_inc(ld_g, 16)
            dma(rw[:, :, :], router_wT.rearrange("(c p) n -> p c n", p=P)).then_inc(ld_g, 16)
            sp_.wait_ge(lev_out, 16)
            dma(lev_all, level_dram.rearrange("b t -> (b t)").partition_broadcast(COPIES)).then_inc(lev_back, 16)
            sp_.wait_ge(consts2, 1)
            blk = NROWS // TT // INIT_PARTS
            for k in range(INIT_PARTS):
                view = rows_dram[k * blk * TT:(k + 1) * blk * TT, :].rearrange("(t s p) w -> s p t w", p=P, s=2)
                for s in range(2):
                    dma(view[s], init_row[:, s:s + 1, :].to_broadcast([P, blk, XW])).then_inc(rows_init, 16)
            dma(out[NTOK:NTOK + TT, :].rearrange("(s p) n -> p s n", p=P), init_row[:, :, 0:HID]).then_inc(rows_init, 16)

            def load_piece(c, k):
                wait(sp_, w_lo, PIECES * c + k - 1)
                dst = stage[:, (k % 2) * PIECE:(k % 2 + 1) * PIECE]
                if k < 4:
                    src = w1[bass.ds(c, 1), (k // 2) * P:(k // 2 + 1) * P, (k % 2) * PIECE:(k % 2 + 1) * PIECE]
                    dma(dst, src.rearrange("e p n -> p (e n)")).then_inc(w_loaded[k % 2], 16)
                else:
                    src = w2[bass.ds(c, 1), (k - 4) * 2 * P:(k - 3) * 2 * P, :].rearrange("e (j p) n -> p (e j) n", p=P)
                    dma(dst.rearrange("p (j n) -> p j n", j=2), src).then_inc(w_loaded[k % 2], 16)

            def store_h(cp):
                sp_.wait_ge(h_ready, TILES * cp + TILES)
                rows = out[bass.ds(cp * CHUNK, CHUNK), :].rearrange("(j p) n -> p j n", p=P)
                dma(rows, rows4[:, :, :]).then_inc(h_stored, 16)

            def body(c, main, prev, prev2):
                for q in range(GROUPS):
                    if prev:
                        for k in range(PIECES):
                            if main and q == max(piece_slot(k - 2), 0):
                                load_piece(c - 1, k)
                        if q == S_H + 1:
                            store_h(c - 1)

            chunks(sp_, body)

            for k in range(2):
                load_piece(EXPERTS - 1, k)

            sp_.wait_ge(scattered, 16 * 2 * TILES * NCHUNK)
            sp_.wait_ge(tiles_ready, 1)
            sp_.wait_ge(scan_phase_over, 3)

            def load_x(i, s, first):
                if not first:
                    sp_.wait_ge(f_tp, i - FR + 1)
                    sp_.wait_ge(f_meta, i - FR + 1)
                row = sp_.value_load(tile_row[0:1, bass.ds(i, 1)], min_val=0, max_val=DUMMY_ROW)
                dma(x_in[s], rows_dram[bass.ds(row, TT), :].rearrange("(s p) w -> p s w", p=P)).then_inc(f_in[s], 16)

            for i in range(FR):
                load_x(i, i, True)
            for k in (2, 3):
                load_piece(EXPERTS - 1, k)
            def step(m, u):
                load_x(FR * (m + 1) + u, u, False)
                if isinstance(m, int) and u < FR - 1:
                    for k in (2 * u + 4, 2 * u + 5):
                        load_piece(EXPERTS - 1, k)

            tile_steps(sp_, (step, 2))

        @block.gpsimd
        def _(pool):
            g = nc.gpsimd
            n = [0]

            def link(ins):
                ins.then_inc(consts, 1)
                n[0] += 1
                pool.wait_ge(consts, n[0])

            def diag(t, last=False):
                link(g.memset(t[:, :], 0.0))
                link(g.affine_select(out=t[:, :], in_=t[:, :], compare_op=ALU.not_equal, fill=1.0, base=0,
                                     pattern=[[-1, P]], channel_multiplier=1))

            for k in range(3):
                link(g.iota(lvl_id[k * LEVELS:(k + 1) * LEVELS, :], pattern=[[0, 1]], base=0, channel_multiplier=1,
                            allow_small_or_imprecise_dtypes=True))
                link(g.memset(not_first[k * LEVELS:(k + 1) * LEVELS, :], 0.0 if k == 0 else -1.0))
                link(g.memset(last_copy[k * LEVELS:(k + 1) * LEVELS, :], -1.0 if k == 2 else 0.0))
            diag(ident)
            diag(ident16)
            link(g.memset(tri[:, :], 1.0))
            link(g.affine_select(out=tri[:, :], in_=tri[:, :], compare_op=ALU.is_ge, fill=0.0, base=0,
                                 pattern=[[1, P]], channel_multiplier=-1))
            link(g.memset(ones[:, :], 1.0))
            link(g.memset(sel[:, :, :], 1.0))
            link(g.affine_select(out=sel[:, :, :], in_=sel[:, :, :], compare_op=ALU.is_ge, fill=0.0, base=0,
                                 pattern=[[STATE * GCH, 4], [-STATE, 32]], channel_multiplier=1))
            link(g.affine_select(out=sel[:, :, :], in_=sel[:, :, :], compare_op=ALU.is_ge, fill=0.0, base=STATE - 1,
                                 pattern=[[-STATE * GCH, 4], [STATE, 32]], channel_multiplier=-1))
            link(g.memset(segmask[:, :], 1.0))
            link(g.memset(segmask[:, :].rearrange("p (j e) -> p j e", e=NE)[:, :, 0:1], 0.0))
            link(g.iota(row_base[:, :], pattern=[[REGION, NE]], base=-1, channel_multiplier=0,
                        allow_small_or_imprecise_dtypes=True))
            link(g.iota(tok_f[:, :], pattern=[[P, TILES]], base=-CHUNK, channel_multiplier=1,
                        allow_small_or_imprecise_dtypes=True))
            link(g.memset(seen[:, 0, :], 0.0))
            link(g.memset(one8[:, :], 1.0))
            link(g.iota(thr[:, :], pattern=[[TT, REGION_TILES]], base=0, channel_multiplier=0,
                        allow_small_or_imprecise_dtypes=True))
            link(g.iota(tile_no[:, :], pattern=[[1, FT]], base=0, channel_multiplier=0,
                        allow_small_or_imprecise_dtypes=True))
            link(g.memset(a_all.rearrange("p (s t) -> p s t", t=SEQ)[:, :, 0:1], 0.0))
            link(g.memset(init_row[:, :, :], 0.0))
            link(g.iota(init_row[:, :, XW - 1:XW].bitcast(i32), pattern=[[P, 2], [0, 1]], base=NTOK, channel_multiplier=1))
            pool.drain().then_inc(consts2, 1)

            xs = xz[:, 0:HID]
            pool.wait_ge(p_x, 1)
            pool.wait_ge(ld_d, 48)
            for half in range(2):
                turned = "p (r m e) -> p m r e"
                cols = slice(half * P, (half + 1) * P)
                g.tensor_tensor(small[:, TDX - TC + half * P:TDX - TC + (half + 1) * P].rearrange(
                    "p (m r e) -> p m r e", m=4, r=4), d_b[:, cols].rearrange(turned, m=4, r=4),
                    xs[:, cols].rearrange(turned, m=4, r=4), ALU.mult).then_inc(small_pool, 1)
            grid = "p (d n) -> p d n"
            pool.wait_ge(p_dtx, 1)
            DQ = QN // STATE

            def input_quarter(k):
                g.tensor_tensor(b_val[:, k * QN:(k + 1) * QN].rearrange(grid, n=STATE),
                                tmps[3][:, k * DQ:(k + 1) * DQ].unsqueeze(2).to_broadcast([COPIES, DQ, STATE]),
                                dbc[:, HID:HID + STATE].unsqueeze(1).to_broadcast([COPIES, DQ, STATE]),
                                ALU.mult).then_inc(split_val["b"], 1)

            input_quarter(0)
            g.tensor_tensor(small[:, TRB - TC:TRB - TC + HID], x0[:, :], bo_b, ALU.add).then_inc(small_pool, 1)
            g.tensor_tensor(small[:, THB - TC:THB - TC + HID], h0[:, :], be_b, ALU.add).then_inc(small_pool, 1)
            for k in range(1, QUARTERS):
                input_quarter(k)

            last_row, last_sum = pool.to_reg(DUMMY_ROW - 1), pool.to_reg(NTOK + TT - 1)

            rows_sent, sums_sent = pool.alloc_register("rows_sent"), pool.alloc_register("sums_sent")
            pool.reg_mov(rows_sent, 0)
            pool.reg_mov(sums_sent, 0)

            def mul(c, q):
                pool.wait_ge(scan_done, GROUPS * c + q + 1)
                if q == POOL_MULS[0]:
                    pool.wait_ge(x_copied, XPER * c + C_POS + 2)
                g.tensor_tensor(hslot(q), hslot(q), c_sb, ALU.mult).then_inc(mul_p, 1)

            def send(cp, j, k):
                if j == 0 and k == 0:
                    pool.wait_ge(route_done, cp + 1)
                    pool.reg_add(rows_sent, rows_sent, 16 * TOPK * TILES)
                    pool.wait_ge(rows_init, 16 * (2 * INIT_PARTS + 1))
                g.indirect_dma_start(
                    out=rows_dram, out_offset=bass.IndirectOffsetOnAxis(slot_i[:, j, k:k + 1], 0),
                    in_=payload[:, j, :], in_offset=None, bounds_check=last_row,
                    oob_is_err=False).then_inc(scattered, 16)

            def body(c, main, prev, prev2):
                pairs = [(j, k) for j in range(TILES) for k in range(TOPK)]
                for q in POOL_MULS:
                    if main:
                        mul(c, q)
                    if prev2 and q >= P_SEND and pairs:
                        send(c - 2, *pairs.pop(0))

            chunks(pool, body)

            def step(m, u):
                i, s, _ = ahead(m, u, 0)
                pool.wait_ge(f_ys, i + 1)
                pool.wait_ge(f_meta, i + 1)
                if not isinstance(i, int) or i > 0:
                    pool.wait_ge(f_out, sums_sent)
                pool.reg_add(sums_sent, sums_sent, 32)
                pool.wait_ge(h_stored, 16 * NCHUNK)
                for k in range(2):
                    g.indirect_dma_start(
                        out=out, out_offset=bass.IndirectOffsetOnAxis(tok_i[s][:, k:k + 1], 0),
                        in_=y_sb[s][:, k, :], in_offset=None, compute_op=ALU.add,
                        bounds_check=last_sum, oob_is_err=True).then_inc(f_out, 16)

            pool.wait_ge(tiles_ready, 1)
            tile_steps(pool, (step, 0))
            pool.wait_ge(scattered, rows_sent)
            pool.wait_ge(f_out, sums_sent)

        @block.scalar
        def _(act):
            A = nc.scalar.activation
            act.wait_ge(p_var, 1)
            A(nrm[0:COPIES, 1, 0:1], nrm[0:COPIES, 0, 0:1], ACT.Sqrt).then_inc(p_std, 1)
            act.wait_ge(ld_a, 16)
            A(expA, expA, ACT.Exp).then_inc(p_eA, 1)
            act.wait_ge(p_abs, 1)
            A(tmps[1], tmps[0], ACT.Exp, scale=-1.0).then_inc(p_exp, 1)
            act.wait_ge(p_zc, 1)
            A(tmps[8], tmps[8], ACT.Exp).then_inc(p_ez, 1)

            def high(t, k, val, hi):
                act.wait_ge(split_val[t], k + 1)
                wait(act, table_ready[t], k)
                A(hi, val, ACT.Copy).then_inc(split_hi[t], 1)

            def middle(t, k, val, hi):
                act.wait_ge(split_rest[t], k + 1)
                A(hi, val, ACT.Copy).then_inc(split_mid[t], 1)

            def decay_quarter(k):
                act.wait_ge(p_arg, k + 1)
                A(a_val[k % 2], a_val[k % 2], ACT.Exp, scale=-1.0).then_inc(split_val["a"], 1)

            def table_op(q):
                k = q // QG + 1
                if k < QUARTERS:
                    b_part = b_val[:, k * QN:(k + 1) * QN]
                    if q % QG == 0:
                        decay_quarter(k)
                    if q % QG == 1:
                        high("a", k, a_val[k % 2], a_hi)
                        high("b", k, b_part, b_hi)
                    if q % QG == 4:
                        middle("a", k, a_val[k % 2], a_hi)
                    if q % QG == 5:
                        middle("b", k, b_part, b_hi)
                if q == 8:
                    high("s", 1, small[:, SMALL_1:], small_h[:, SMALL_1:])
                if q == 12:
                    middle("s", 1, small[:, SMALL_1:], small_h[:, SMALL_1:])

            high("s", 0, small[:, 0:SMALL_1], small_h[:, 0:SMALL_1])
            decay_quarter(0)
            high("a", 0, a_val[0], a_hi)
            high("b", 0, b_val[:, 0:QN], b_hi)
            middle("s", 0, small[:, 0:SMALL_1], small_h[:, 0:SMALL_1])
            middle("a", 0, a_val[0], a_hi)
            middle("b", 0, b_val[:, 0:QN], b_hi)

            def copy_decay(c, q):
                act.wait_ge(x_ready, XPER * c + xpos(q) + 1)
                wait(act, scan_done, GROUPS * c + q - (ARING - 1))
                dst = aslot(q).rearrange("p (b t) -> p b t", t=SEQ)[:, :, 1:]
                src = xbank[xpos(q) % 2][:, :].rearrange("p (b t) -> p b t", t=SEQ)[:, :, 1:]
                A(dst, src, ACT.Copy).then_inc(x_copied, 1)

            def copy_c(c):
                wait(act, mul_v, len(VEC_MULS) * c)
                wait(act, mul_p, len(POOL_MULS) * c)
                for k in range(2):
                    act.wait_ge(x_ready, XPER * c + C_POS + k + 1)
                    A(c_sb[:, k * TT:(k + 1) * TT], xbank[(C_POS + k) % 2][:, 0:TT], ACT.Copy).then_inc(x_copied, 1)

            def copy_z(c, half):
                act.wait_ge(x_ready, XPER * c + Z_POS[half] + 1)
                wait(act, v_done, 2 * c + half - 1)
                A(z_sb, xbank[Z_POS[half] % 2][:, :], ACT.Copy).then_inc(x_copied, 1)

            def weight_hi(c, k):
                act.wait_ge(w_loaded[k % 2], 16 * (PIECES // 2 * c + k // 2 + 1))
                which, at = (W1H, k * PIECE) if k < 4 else (W2H, (k - 4) * PIECE)
                A(wsec(c, which, at, PIECE), stage[:, (k % 2) * PIECE:(k % 2 + 1) * PIECE], ACT.Copy,
                  scale=W_UP).then_inc(w_hi, 1)

            def end_op(cp, q):
                if q == A_STD1:
                    act.wait_ge(var1, cp + 1)
                    A(nrm[:, 1, :], nrm[:, 0, :], ACT.Sqrt).then_inc(std1, 1)
                if q == A_STD2:
                    act.wait_ge(var2, cp + 1)
                    A(nrm[:, 1, :], nrm[:, 0, :], ACT.Sqrt).then_inc(std2, 1)
                if q == A_NORM2:
                    act.wait_ge(nrm2, cp + 1)
                    act.wait_ge(h_stored, 16 * (cp + 1))
                if q in (A_NORM2, A_NORM2 + 1):
                    for j in range(2 * (q - A_NORM2), 2 * (q - A_NORM2) + 2):
                        A(rows4[:, j, :], rows4[:, j, :], ACT.Identity, bias=nrm[:, 3, j:j + 1],
                          scale=nrm[:, 2, j:j + 1]).then_inc(x2_ready, 1)
                if q == A_HIGH:
                    act.wait_ge(x2_ready, TILES * cp + TILES)
                    wait(act, scattered, 16 * 2 * TILES * cp)
                    A(x_hi, rows4[:, :, :], ACT.Copy, scale=X_UP).then_inc(hi_ready, 1)
                for k in range(2):
                    if q == A_TURNED[k]:
                        act.wait_ge(xT_ready, 2 * cp + k + 1)
                        wait(act, logit_ready, 2 * cp + k)
                        A(x2T, pre[:, k * CHUNK:(k + 1) * CHUNK].rearrange("p (j c t) -> p j c t", j=2, c=2),
                          ACT.Copy).then_inc(xT_copied, 1)

            def body(c, main, prev, prev2):
                for q in range(GROUPS):
                    if main:
                        copy_decay(c, q)
                        if q == 3:
                            copy_c(c)
                        if q == 17:
                            copy_z(c, 0)
                        if q == 31:
                            copy_z(c, 1)
                        if not prev:
                            table_op(q)
                    if prev and main:
                        for k in range(PIECES):
                            if q == piece_slot(k):
                                weight_hi(c - 1, k)
                    if prev:
                        end_op(c - 1, q)

            chunks(act, body)
            act.wait_ge(sum_done, 8 * NCHUNK)
            for k in range(2):
                weight_hi(EXPERTS - 1, k)
            act.drain().then_inc(scan_phase_over, 1)
            A(nrm[:, 1, :], nrm[:, 0, :], ACT.Gelu)
            act.wait_ge(scan_phase_over, 3)

            def take_x(i, s, m):
                act.wait_ge(f_in[s], 16 * (m + 1))
                e = act.value_load(tile_expert[0:1, bass.ds(i, 1)], min_val=0, max_val=NE - 1)
                wait(act, f_gate, i - FR + 1)
                A(tgate[s][:, :].unsqueeze(2), x_in[s][:, :, bass.ds(HID + e, 1)], ACT.Tanh, scale=0.5).then_inc(f_tg, 1)
                act.wait_ge(f_tp, i + 1)
                wait(act, f_h, 4 * (i - FR + 1))
                A(x_T[s], xTp16, ACT.Copy).then_inc(f_xT, 1)

            def activate(i, s):
                for b in range(4):
                    act.wait_ge(f_h, 4 * i + b + 1)
                    wait(act, f_lo, 4 * (i - 1) + b + 1)
                    A(g_sb[b], bank[b][:, :], ACT.Gelu, scale=1.0 / (X_UP * W_UP)).then_inc(f_g, 1)
                    act.wait_ge(f_g, 4 * i + b + 1)
                    if b == 0:
                        wait(act, f_y, i - FR + 1)
                    A(h_hi[s][:, 2 * b:2 * b + 2, :], g_sb[b].rearrange("p (j t) -> p j t", j=2), ACT.Copy,
                      scale=H_UP).then_inc(f_hi, 1)

            act.wait_ge(tiles_ready, 1)
            take_x(0, 0, 0)
            activate(0, 0)
            take_x(1, 1, 0)

            def step(m, u):
                i1, s1, _ = ahead(m, u, 1)
                i2, s2, m2 = ahead(m, u, 2)
                activate(i1, s1)
                take_x(i2, s2, m2)
                if isinstance(m, int):
                    for k in (2 * u + 2, 2 * u + 3):
                        weight_hi(EXPERTS - 1, k)

            tile_steps(act, (step, 1))

        @block.vector
        def _(dve):
            v = nc.vector
            n = [0]
            base = [0]

            def done(ins):
                ins.then_inc(vstep, 1)
                n[0] += 1

            def after():
                dve.wait_ge(vstep, base[0] + n[0])

            def link(ins):
                done(ins)
                after()

            dve.wait_ge(ld_emb, 48)
            link(v.tensor_scalar(h0[:, :], emb[:, :], TOK_SCALE, None, ALU.mult))
            link(v.bn_stats(bn6[0:COPIES, 0, :], h0[:, :]))
            link(v.bn_aggr(mv[0:COPIES, 0, :], bn6[0:COPIES, 0, :]))
            v.tensor_scalar(nrm[0:COPIES, 0, 0:1], mv[0:COPIES, 0, 1:2], EPS, None, ALU.add).then_inc(p_var, 1)
            dve.wait_ge(ld_tok, 16)
            link(v.tensor_copy(x_f, x_int))
            dve.wait_ge(p_std, 1)
            link(v.reciprocal(nrm[0:COPIES, 2, 0:1], nrm[0:COPIES, 1, 0:1]))
            v.tensor_scalar(x0[:, :], h0[:, :], mv[0:COPIES, 0, 0:1], nrm[0:COPIES, 2, 0:1], ALU.subtract,
                            ALU.mult).then_inc(p_x0, 1)
            link(v.tensor_scalar(acc[0], x_f, 40.0, None, ALU.is_equal))
            link(v.scalar_tensor_tensor(acc[1], x_f, 91.0, acc[0], ALU.is_equal, ALU.add))
            dve.wait_ge(p_x0T, 1)
            v.tensor_copy(rowsT[:, :, :], misc[:, 0:2 * COPIES].rearrange("p (c m) -> p c m", c=2)).then_inc(p_x0Ts, 1)
            link(v.scalar_tensor_tensor(acc[0], x_f, 123.0, acc[1], ALU.is_equal, ALU.add))
            link(v.scalar_tensor_tensor(acc[1], x_f, 41.0, acc[0], ALU.is_equal, ALU.subtract))
            link(v.scalar_tensor_tensor(acc[0], x_f, 93.0, acc[1], ALU.is_equal, ALU.add))
            done(v.memset(sc0, 0.0))
            link(v.memset(sc1, 0.0))
            ev = "p (t k) -> p t k"
            done(v.scalar_tensor_tensor(sc0.rearrange(ev, k=2)[:, :, 0], x_f, 125.0, acc[0], ALU.is_equal, ALU.add))
            done(v.memset(sc1.rearrange(ev, k=2)[:, :, 0], -float(LEVELS - 1)))
            dve.wait_ge(p_xs, 1)
            dve.wait_ge(ld_w, 48)
            xs, zz = xz[:, 0:HID], xz[:, HID:2 * HID]
            v.tensor_tensor(xs, ybank[0:COPIES, 0:HID], bin_b[:, 0:HID], ALU.add).then_inc(p_x, 1)
            after()
            link(v.tensor_tensor_scan(sc_o, sc0, sc1, 0.0, ALU.subtract, ALU.max))
            v.tensor_copy(lev_c, sc_o.rearrange(ev, k=2)[:, :, 1]).then_inc(p_hot, 1)
            dve.wait_ge(p_xsT, 1)
            v.tensor_copy(rowsT[:, :, :], misc[:, 0:2 * COPIES].rearrange("p (c m) -> p c m", c=2)).then_inc(p_xsTs, 1)
            dve.wait_ge(p_dbc, 1)
            dve.wait_ge(ld_p, 96)
            link(v.tensor_tensor(dbc, ybank[0:COPIES, 0:NP], bp_b, ALU.add))
            dtp, Bl, Cl = dbc[:, 0:HID], dbc[:, HID:HID + STATE], dbc[:, HID + STATE:NP]
            v.scalar_tensor_tensor(tmps[0], dtp, -1.0, dtp, ALU.mult, ALU.max).then_inc(p_abs, 1)
            dve.wait_ge(p_z, 1)
            done(v.tensor_tensor(zz, zbank[0:COPIES, 0:HID], bin_b[:, HID:], ALU.add))
            dve.wait_ge(p_exp, 1)
            link(v.tensor_scalar(tmps[2], tmps[1], 2.0, None, ALU.add))
            v.tensor_scalar(tmps[8], zz, -1.0, 80.0, ALU.mult, ALU.min).then_inc(p_zc, 1)
            link(v.reciprocal(tmps[3], tmps[2]))
            link(v.tensor_tensor(tmps[4], tmps[1], tmps[3], ALU.mult))
            link(v.tensor_tensor(tmps[5], tmps[4], tmps[4], ALU.mult))
            link(v.tensor_scalar(tmps[6], tmps[5], 1.0 / 17, None, ALU.mult))
            for k in range(7, 0, -1):
                link(v.scalar_tensor_tensor(tmps[6], tmps[6], 1.0 / (2 * k + 1), tmps[5], ALU.add, ALU.mult))
            done(v.tensor_scalar(tmps[7], dtp, 0.0, None, ALU.max))
            link(v.scalar_tensor_tensor(tmps[6], tmps[6], 1.0, tmps[4], ALU.add, ALU.mult))
            link(v.scalar_tensor_tensor(tmps[2], tmps[6], 2.0, tmps[7], ALU.mult, ALU.add))
            dt = tmps[2]
            v.tensor_tensor(tmps[3], dt, xs, ALU.mult).then_inc(p_dtx, 1)

            def rest(t, k, val, hi):
                dve.wait_ge(split_hi[t], k + 1)
                v.scalar_tensor_tensor(val, hi, not_first[:, :], val, ALU.mult, ALU.add).then_inc(split_rest[t], 1)

            def to_table(t, k, val, hi, dst):
                dve.wait_ge(split_mid[t], k + 1)
                v.scalar_tensor_tensor(dst, hi, last_copy[:, :], val, ALU.mult, ALU.add).then_inc(table_ready[t], 1)

            def decay_argument(k):
                wait(dve, table_ready["a"], k - 1)
                d_of = slice(k * QN // STATE, (k + 1) * QN // STATE)
                grid = "p (d n) -> p d n"
                v.tensor_tensor(a_val[k % 2].rearrange(grid, n=STATE), expA[:, k * QN:(k + 1) * QN].rearrange(grid, n=STATE),
                                dt[:, d_of].unsqueeze(2).to_broadcast([COPIES, QN // STATE, STATE]),
                                ALU.mult).then_inc(p_arg, 1)

            def a_table(k):
                return a_val[k % 2], a_hi, table[:, TA + k * QN:TA + (k + 1) * QN]

            def b_table(k):
                return b_val[:, k * QN:(k + 1) * QN], b_hi, table[:, TB + k * QN:TB + (k + 1) * QN]

            def s_table(k):
                cols = slice(0, SMALL_1) if k == 0 else slice(SMALL_1, SMALL)
                return small[:, cols], small_h[:, cols], table[:, TC:NTAB][:, cols]

            def table_op(q):
                k = (q + 2) // QG + 1
                if (q + 2) % QG == 0 and k < QUARTERS:
                    decay_argument(k)
                k = q // QG + 1
                if k < QUARTERS:
                    if q % QG == 2:
                        rest("a", k, *a_table(k)[0:2])
                    if q % QG == 3:
                        rest("b", k, *b_table(k)[0:2])
                    if q % QG == 5:
                        to_table("a", k, *a_table(k))
                    if q % QG == 6:
                        to_table("b", k, *b_table(k))
                if q == 0:
                    dve.wait_ge(p_ez, 1)
                    done(v.tensor_scalar(tmps[8], tmps[8], 1.0, None, ALU.add))
                if q == 1:
                    after()
                    done(v.reciprocal(tmps[9], tmps[8]))
                if q == 4:
                    after()
                    v.tensor_tensor(small[:, TZ - TC:TZ - TC + HID], zz, tmps[9], ALU.mult).then_inc(split_val["s"], 1)
                if q == 9:
                    dve.wait_ge(small_pool, 4)
                    rest("s", 1, *s_table(1)[0:2])
                if q == 13:
                    to_table("s", 1, *s_table(1))
                if q == 18:
                    v.tensor_scalar(onehot[:, CHUNK:], lev_all[:, CHUNK:], lvl_id[:, :], None,
                                    ALU.is_equal).then_inc(onehot_ready, 1)

            dve.wait_ge(p_eA, 1)
            dve.wait_ge(consts2, 1)
            decay_argument(0)
            dve.wait_ge(small_pool, 2)
            v.tensor_copy(small[:, 0:P].rearrange("p (e n) -> p e n", n=STATE),
                          Cl.unsqueeze(1).to_broadcast([COPIES, GCH, STATE])).then_inc(split_val["s"], 1)
            decay_argument(1)
            rest("s", 0, *s_table(0)[0:2])
            rest("a", 0, *a_table(0)[0:2])
            rest("b", 0, *b_table(0)[0:2])
            dve.wait_ge(lev_back, 16)
            v.tensor_scalar(onehot[:, 0:CHUNK], lev_all[:, 0:CHUNK], lvl_id[:, :], None,
                            ALU.is_equal).then_inc(onehot_ready, 1)
            to_table("s", 0, *s_table(0))
            to_table("a", 0, *a_table(0))
            to_table("b", 0, *b_table(0))
            dve.wait_ge(ld_g, 48)

            def scan(c, q):
                dve.wait_ge(x_copied, XPER * c + xpos(q) + 1)
                dve.wait_ge(b_ready, GROUPS * c + q + 1)
                if q % 4 == 0:
                    wait(dve, sum_done, 8 * c + q // 4 - HRING // 4 + 1)
                v.tensor_tensor_scan(hslot(q), aslot(q), bbank[q % 3][:, :], 0.0, ALU.mult, ALU.add).then_inc(scan_done, 1)

            def mul(c, q):
                dve.wait_ge(scan_done, GROUPS * c + q + 1)
                dve.wait_ge(x_copied, XPER * c + C_POS + 2)
                v.tensor_tensor(hslot(q), hslot(q), c_sb, ALU.mult).then_inc(mul_v, 1)

            def gate_z(c, half):
                dve.wait_ge(sum_done, 8 * c + 4 * half + 4)
                dve.wait_ge(x_copied, XPER * c + Z_POS[half] + 1)
                wait(dve, pre_ready, 4 * c)
                v.tensor_tensor(v_sb[:, half * CHUNK:(half + 1) * CHUNK], ybank[:, :],
                                z_sb, ALU.mult).then_inc(v_done, 1)

            def weight_lo(c, k):
                dve.wait_ge(w_hi, PIECES * c + k + 1)
                hi, lo, at = (W1H, W1L, k * PIECE) if k < 4 else (W2H, W2L, (k - 4) * PIECE)
                v.scalar_tensor_tensor(wsec(c, lo, at, PIECE), stage[:, (k % 2) * PIECE:(k % 2 + 1) * PIECE], W_UP,
                                       wsec(c, hi, at, PIECE), ALU.mult, ALU.subtract).then_inc(w_lo, 1)

            def stats(src, j):
                done(v.bn_stats(bn6[:, j, :], src))

            def aggregate():
                after()
                done(v.tensor_copy(carried[:, :], bn6[:, 0, 0:1]))
                for j in range(TILES):
                    done(v.bn_aggr(mv[:, j, :], bn6[:, j, :]))

            def variance(ready):
                after()
                v.tensor_scalar(nrm[:, 0, :], mv[:, :, 1], EPS, None, ALU.add).then_inc(ready, 1)

            def end_op(cp, q):
                for j in range(TILES):
                    if q == S_STATS1[j]:
                        dve.wait_ge(pre_ready, TILES * cp + 2 * (j // 2) + 2)
                        stats(pre[:, j * HID:(j + 1) * HID], j)
                if q == S_GAMMA:
                    aggregate()
                if q in (S_GAMMA, S_GAMMA + 1):
                    if q == S_GAMMA:
                        wait(dve, xT_ready, 2 * cp)
                        after()
                    for j in range(2 * (q - S_GAMMA), 2 * (q - S_GAMMA) + 2):
                        v.scalar_tensor_tensor(rows4[:, j, :], pre[:, j * HID:(j + 1) * HID], mv[:, j, 0:1],
                                               gamma_b[:, :], ALU.subtract, ALU.mult).then_inc(t1_ready, 1)
                    if q == S_GAMMA:
                        variance(var1)
                if q == S_H - 1:
                    dve.wait_ge(std1, cp + 1)
                    done(v.reciprocal(nrm[:, 2, :], nrm[:, 1, :]))
                if q in (S_H, S_H + 1):
                    if q == S_H:
                        after()
                        dve.wait_ge(t1_ready, TILES * cp + TILES)
                        dve.wait_ge(hb_ready, cp + 1)
                    for j in range(2 * (q - S_H), 2 * (q - S_H) + 2):
                        v.scalar_tensor_tensor(rows4[:, j, :], rows4[:, j, :], nrm[:, 2, j:j + 1],
                                               pre[:, j * HID:(j + 1) * HID], ALU.mult, ALU.add).then_inc(h_ready, 1)
                if q in (S_STATS2, S_STATS2 + 1):
                    if q == S_STATS2:
                        dve.wait_ge(h_ready, TILES * cp + TILES)
                    for j in range(2 * (q - S_STATS2), 2 * (q - S_STATS2) + 2):
                        stats(rows4[:, j, :], j)
                if q == S_STATS2 + 2:
                    aggregate()
                    variance(var2)
                if q == S_NORM2:
                    dve.wait_ge(std2, cp + 1)
                    done(v.reciprocal(nrm[:, 2, :], nrm[:, 1, :]))
                if q == S_NORM2 + 1:
                    after()
                    v.scalar_tensor_tensor(nrm[:, 3, :], mv[:, :, 0], -1.0, nrm[:, 2, :], ALU.mult,
                                           ALU.mult).then_inc(nrm2, 1)
                if q == S_LOW:
                    dve.wait_ge(hi_ready, cp + 1)
                    v.scalar_tensor_tensor(x_lo, rows4[:, :, :], X_UP, x_hi, ALU.mult, ALU.subtract)

            def first_max(src, k, i):
                m = top[:, k, :]
                if i == 0:
                    done(v.tensor_reduce(m, src, AX.X, ALU.max))
                elif i == 1:
                    done(v.tensor_tensor(eq[:, :, :], src, m.unsqueeze(2).to_broadcast([P, TILES, NE]), ALU.is_ge))
                elif i == 2:
                    done(v.tensor_tensor_scan(cs[:, :], segmask[:, :], eq[:, :, :].rearrange("p j e -> p (j e)"), 0.0,
                                              ALU.mult, ALU.add))
                else:
                    return v.scalar_tensor_tensor(hot[:, :, k, :], cs[:, :].rearrange("p (j e) -> p j e", e=NE), 1.0,
                                                  eq[:, :, :], ALU.is_equal, ALU.mult)

            def choose(cp, i):
                if i == 0:
                    dve.wait_ge(logit_ready, 2 * cp + 2)
                    done(v.tensor_copy(lg[:, :, :], logit_ps))
                    return
                after()
                if i < 4:
                    first_max(lg[:, :, :], 0, i - 1)
                elif i == 4:
                    done(first_max(lg[:, :, :], 0, 3))
                elif i == 5:
                    done(v.scalar_tensor_tensor(lg2[:, :, :], hot[:, :, 0, :], -1.0e30, lg[:, :, :], ALU.mult, ALU.add))
                elif i < 9:
                    first_max(lg2[:, :, :], 1, i - 6)
                elif i == 9:
                    first_max(lg2[:, :, :], 1, 3).then_inc(hot_ready, 1)
                elif i == 10:
                    dve.wait_ge(hot_ready, cp + 1)
                    done(v.tensor_tensor(top[:, 2, :], top[:, 0, :], top[:, 1, :], ALU.subtract))
                    done(v.tensor_tensor(dif[:, :, :], hot[:, :, 0, :], hot[:, :, 1, :], ALU.subtract))
                elif i == 11:
                    done(v.tensor_tensor(payload[:, :, HID:HID + NE], dif[:, :, :],
                                         top[:, 2, :].unsqueeze(2).to_broadcast([P, TILES, NE]), ALU.mult))
                    done(v.tensor_scalar(tok_f[:, :], tok_f[:, :], float(CHUNK), None, ALU.add))
                else:
                    done(v.tensor_copy(payload[:, :, XW - 1:XW].bitcast(i32), tok_f[:, :].unsqueeze(2)))

            CHOOSE_STEPS, PLACE_STEPS = 13, 12

            def place(cp, i):
                flat = "p j k e -> p j (k e)"
                if i == 0:
                    dve.wait_ge(cnt_ready, cp + 1)
                    v.tensor_copy(counts[:, :, :], cnt_ps).then_inc(cnt_taken, 1)
                    return
                if i == 1:
                    dve.wait_ge(cnt_taken, cp + 1)
                after()
                if i < 5:
                    done(v.tensor_tensor(seen[:, i, :], counts[:, 1, (i - 1) * 2 * NE:i * 2 * NE], seen[:, i - 1, :],
                                         ALU.add))
                elif i == 5:
                    done(v.tensor_tensor(pos[:, :, :, :].rearrange(flat),
                                         counts[:, 0, :].rearrange("p (j f) -> p j f", j=TILES), seen[:, 0:TILES, :], ALU.add))
                elif i == 6:
                    done(v.tensor_copy(seen[:, 0, :], seen[:, TILES, :]))
                    done(v.tensor_scalar(kept[:, :, :, :].rearrange(flat), pos[:, :, :, :].rearrange(flat), float(CAP),
                                         None, ALU.min))
                    done(v.tensor_tensor(mul2[:, :, :, :].rearrange(flat), hot[:, :, :, :].rearrange(flat),
                                         pos[:, :, :, :].rearrange(flat), ALU.mult))
                elif i == 7:
                    done(v.tensor_tensor(slot[:, :, :], kept[:, :, 0, :], kept[:, :, 1, :], ALU.add))
                    done(v.tensor_reduce(red2[:, :, :], mul2[:, :, :, :], AX.X, ALU.add))
                elif i == 8:
                    done(v.tensor_tensor(slot[:, :, :], slot[:, :, :],
                                         row_base[:, :].unsqueeze(1).to_broadcast([P, TILES, NE]), ALU.add))
                    done(v.tensor_scalar(drop[:, :, :], red2[:, :, :], float(CAP), DROP, ALU.is_gt, ALU.mult))
                elif i == 9:
                    for k in range(2):
                        done(v.tensor_tensor(mul1[:, :, k, :], hot[:, :, k, :], slot[:, :, :], ALU.mult))
                elif i == 10:
                    done(v.tensor_reduce(red1[:, :, :], mul1[:, :, :, :], AX.X, ALU.add))
                else:
                    v.tensor_tensor(slot_i[:, :, :], red1[:, :, :], drop[:, :, :], ALU.add).then_inc(route_done, 1)
                    dve.wait_ge(route_done, cp + 1)

            def routing(cp, q, odd):
                i = 2 * (q - S_CHOOSE) + odd
                if 0 <= i < CHOOSE_STEPS:
                    choose(cp, i)
                i = 2 * (q - S_PLACE) + odd
                if 0 <= i < PLACE_STEPS:
                    place(cp, i)

            def body(c, main, prev, prev2):
                for q in range(GROUPS):
                    if main:
                        scan(c, q)
                    if prev:
                        routing(c - 1, q, 0)
                    if prev2:
                        routing(c - 2, q + GROUPS, 0)
                    if prev and q == 0:
                        mul(c - 1, VEC_MULS[-1])
                    if main:
                        for k in VEC_MULS:
                            if q == k + 1:
                                mul(c, k)
                        if q == S_GATE[0]:
                            gate_z(c, 0)
                        if not prev:
                            table_op(q)
                    if prev:
                        for k in range(PIECES):
                            if main and q == piece_slot(k):
                                weight_lo(c - 1, k)
                        if q == S_GATE[1]:
                            gate_z(c - 1, 1)
                        end_op(c - 1, q)
                        routing(c - 1, q, 1)
                    if prev2:
                        routing(c - 2, q + GROUPS, 1)

            LN_STEPS, CHOOSE_COUNT, PLACE_COUNT = TILES + (1 + TILES) + 1, 14, 15
            PER_BODY = 2 * LN_STEPS + CHOOSE_COUNT + PLACE_COUNT
            body(0, True, False, False)
            body(1, True, True, False)
            before = n[0]
            with dve.Fori(2, NCHUNK) as c:
                base[0] = (c - 2) * PER_BODY + before
                n[0] = 0
                body(c, True, True, True)
                assert n[0] == PER_BODY, n[0]
            n[0] = before + PER_BODY * (NCHUNK - 2)
            base[0] = 0
            body(NCHUNK, False, True, True)
            body(NCHUNK + 1, False, False, True)

            link(v.tensor_scalar(cnt[:, :], seen[0:1, TILES, :], float(CAP), None, ALU.min))
            link(v.tensor_tensor(n8[:, :], cnt[:, 0:NE], cnt[:, NE:2 * NE], ALU.add))
            link(v.tensor_tensor(gt[:, :, :], n8[:, :].unsqueeze(2).to_broadcast([1, NE, REGION_TILES]),
                                 thr[:, :].unsqueeze(1).to_broadcast([1, NE, REGION_TILES]), ALU.is_gt))
            link(v.tensor_reduce(nt[:, :], gt[:, :, :], AX.X, ALU.add))
            link(v.tensor_tensor_scan(ntc[:, :], one8[:, :], nt[:, :], 0.0, ALU.mult, ALU.add))
            link(v.tensor_tensor(le[:, :, :], tile_no[:, :].unsqueeze(2).to_broadcast([1, FT, NE]),
                                 ntc[:, :].unsqueeze(1).to_broadcast([1, FT, NE]), ALU.is_ge))
            link(v.tensor_tensor(le2[:, :, :], le[:, :, :], nt[:, :].unsqueeze(1).to_broadcast([1, FT, NE]), ALU.mult))
            link(v.tensor_reduce(ex[:, :], le[:, :, :], AX.X, ALU.add))
            link(v.tensor_reduce(bel[:, :], le2[:, :, :], AX.X, ALU.add))
            link(v.tensor_tensor(rw1[:, :], tile_no[:, :], bel[:, :], ALU.subtract))
            link(v.tensor_scalar(rw2[:, :], ex[:, :], float(REGION), None, ALU.mult))
            link(v.scalar_tensor_tensor(bel[:, :], rw1[:, :], float(TT), rw2[:, :], ALU.mult, ALU.add))
            link(v.tensor_scalar(tile_row[:, :], bel[:, :], float(DUMMY_ROW), None, ALU.min))
            link(v.tensor_copy(tile_count[:, :], ntc[:, NE - 1:NE]))
            v.tensor_scalar(tile_expert[:, :], ex[:, :], float(NE - 1), None, ALU.min).then_inc(tiles_ready, 1)
            for k in range(2):
                weight_lo(EXPERTS - 1, k)
            dve.drain().then_inc(scan_phase_over, 1)
            dve.wait_ge(scan_phase_over, 3)

            def low_half(i, s):
                for b in range(4):
                    dve.wait_ge(f_hi, 4 * i + b + 1)
                    if b == 0:
                        wait(dve, f_y, i - FR + 1)
                    pair = "p (j t) -> p j t"
                    v.scalar_tensor_tensor(h_lo[s][:, 2 * b:2 * b + 2, :], g_sb[b].rearrange(pair, j=2), H_UP,
                                           h_hi[s][:, 2 * b:2 * b + 2, :], ALU.mult, ALU.subtract).then_inc(f_lo, 1)

            def meta(i, s, m):
                back = 0.5 / (H_UP * W_UP)
                dve.wait_ge(f_tg, i + 1)
                wait(dve, f_ys, i - FR + 1)
                v.tensor_scalar(gate[s][:, :], tgate[s][:, :], back, back, ALU.mult, ALU.add).then_inc(f_gate, 1)
                dve.wait_ge(f_in[s], 16 * (m + 1))
                wait(dve, f_out, 32 * (i - FR + 1))
                v.tensor_copy(tok_i[s][:, :].unsqueeze(2), x_in[s][:, :, XW - 1:XW].bitcast(i32)).then_inc(f_meta, 1)

            def evacuate(i, s):
                dve.wait_ge(f_y, i + 1)
                dve.wait_ge(f_gate, i + 1)
                wait(dve, f_out, 32 * (i - FR + 1))
                last = None
                for k in range(2):
                    last = v.tensor_scalar(y_sb[s][:, k, :], yb[s][:, k * HID:(k + 1) * HID], gate[s][:, k:k + 1], None,
                                           ALU.mult)
                last.then_inc(f_ys, 1)

            meta(0, 0, 0)
            low_half(0, 0)
            meta(1, 1, 0)

            def next_tiles(m, u):
                i1, s1, _ = ahead(m, u, 1)
                i2, s2, m2 = ahead(m, u, 2)
                low_half(i1, s1)
                meta(i2, s2, m2)

            def this_tile(m, u):
                i, s, _ = ahead(m, u, 0)
                evacuate(i, s)
                if isinstance(m, int):
                    for k in (2 * u + 2, 2 * u + 3):
                        weight_lo(EXPERTS - 1, k)

            tile_steps(dve, (next_tiles, 1), (this_tile, 0))

        @block.tensor
        def _(pe):
            mm = nc.tensor.matmul
            pe.wait_ge(consts2, 1)
            pe.wait_ge(p_x0, 1)
            for k in range(2):
                last = nc.tensor.transpose(misc[:, k * COPIES:(k + 1) * COPIES], x0[:, k * P:(k + 1) * P],
                                           ident[0:COPIES, 0:COPIES])
            last.then_inc(p_x0T, 1)
            pe.wait_ge(p_x0Ts, 1)
            pe.wait_ge(ld_w, 48)
            for k in range(2):
                last = mm(ybank[0:COPIES, 0:HID], rowsT[:, k, :], pro_w[:, k, 0:HID], start=(k == 0), stop=(k == 1))
            last.then_inc(p_xs, 1)
            for k in range(2):
                last = mm(zbank[0:COPIES, 0:HID], rowsT[:, k, :], pro_w[:, k, HID:], start=(k == 0), stop=(k == 1))
            last.then_inc(p_z, 1)
            pe.wait_ge(p_x, 1)
            for k in range(2):
                last = nc.tensor.transpose(misc[:, k * COPIES:(k + 1) * COPIES], xz[:, k * P:(k + 1) * P],
                                           ident[0:COPIES, 0:COPIES])
            last.then_inc(p_xsT, 1)
            pe.wait_ge(p_xsTs, 1)
            pe.wait_ge(ld_p, 96)
            for k in range(2):
                last = mm(ybank[0:COPIES, 0:NP], rowsT[:, k, :], pro_p[:, k, :], start=(k == 0), stop=(k == 1))
            last.then_inc(p_dbc, 1)

            def first_chunk(c):
                return isinstance(c, int) and c == 0

            def hot_cols(c, at, n):
                return onehot[:, bass.ds(c * CHUNK + at, n)]

            def expand(c, pos_, lhsT, at=0, n=CHUNK):
                wait(pe, x_copied, XPER * c + pos_ - 1)
                mm(xbank[pos_ % 2][:, 0:n], lhsT, hot_cols(c, at, n), start=True, stop=True).then_inc(x_ready, 1)

            def expand_decay(c, q):
                if first_chunk(c) and q % QG == 0:
                    pe.wait_ge(table_ready["a"], q // QG + 1)
                expand(c, xpos(q), table[:, TA + q * P:TA + (q + 1) * P])
                if first_chunk(c) and q == 3:
                    pe.wait_ge(table_ready["s"], 1)
                if first_chunk(c) and q == 17:
                    pe.wait_ge(table_ready["s"], 2)
                if q == 3:
                    for k in range(2):
                        expand(c, C_POS + k, table[:, TC:TC + P], k * TT, TT)
                if q == 17:
                    expand(c, Z_POS[0], table[:, TZ:TZ + P])
                if q == 31:
                    expand(c, Z_POS[1], table[:, TZ + P:TZ + 2 * P])

            def expand_input(c, q):
                if first_chunk(c) and q % QG == 0:
                    pe.wait_ge(table_ready["b"], q // QG + 1)
                wait(pe, scan_done, GROUPS * c + (q - 2 if q > 2 else (-1, 0, -2)[q]))
                mm(bbank[q % 3][:, :], table[:, TB + q * P:TB + (q + 1) * P], hot_cols(c, 0, CHUNK),
                   start=True, stop=True).then_inc(b_ready, 1)

            def sum_states(c, b):
                half, blk = b // 4, b % 4
                if blk == 0:
                    wait(pe, v_done, 2 * c + half)
                    mm(ybank[:, :], table[:, TDX + half * P:TDX + (half + 1) * P], hot_cols(c, 0, CHUNK), start=True,
                       stop=False)
                q1 = 4 * b + 4
                pe.wait_ge(mul_v, len(VEC_MULS) * c + muls_before(VEC_MULS, q1))
                pe.wait_ge(mul_p, len(POOL_MULS) * c + muls_before(POOL_MULS, q1))
                for m in range(4):
                    last = mm(ybank[32 * m:32 * m + 32, :], sel[:, blk, :], hslot(4 * b + m), start=False, stop=(blk == 3))
                last.then_inc(sum_done, 1)

            def project_out(cp, j):
                if j == 0:
                    pe.wait_ge(v_done, 2 * cp + 2)
                    wait(pe, cnt_taken, cp)
                o = pre[:, j * HID:(j + 1) * HID]
                for half in range(2):
                    at = half * CHUNK + j * P
                    mm(o, v_sb[:, at:at + P], wo[:, half, :], start=(half == 0), stop=False)
                mm(o, hot_cols(cp, j * P, P), table[:, TRB:TRB + HID], start=False, stop=True).then_inc(pre_ready, 1)

            def row_base_terms(cp):
                pe.wait_ge(t1_ready, TILES * cp + TILES)
                for j in range(TILES):
                    last = mm(pre[:, j * HID:(j + 1) * HID], hot_cols(cp, j * P, P), table[:, THB:THB + HID],
                              start=True, stop=True)
                last.then_inc(hb_ready, 1)

            def turn_x2(cp, part_):
                pe.wait_ge(x2_ready, TILES * cp + 2 * part_ + 2)
                for j in (2 * part_, 2 * part_ + 1):
                    for k in range(2):
                        at = j * HID + k * P
                        last = nc.tensor.transpose(pre[:, at:at + P], rows4[:, j, k * P:(k + 1) * P], ident[:, :])
                last.then_inc(xT_ready, 1)

            def logits(cp, part_):
                pe.wait_ge(xT_copied, 2 * cp + part_ + 1)
                for j in range(2):
                    for k in range(2):
                        last = mm(logit_ps[:, 2 * part_ + j, :], x2T[:, j, k, :], rw[:, k, :], start=(k == 0), stop=(k == 1))
                last.then_inc(logit_ready, 1)

            def count_pairs(cp):
                pe.wait_ge(hot_ready, cp + 1)
                oh = hot[:, :, :, :].rearrange("p j k e -> p (j k e)")
                mm(cnt_ps[:, 0, :], tri[:, :], oh, start=True, stop=True)
                mm(cnt_ps[:, 1, :], ones[:, :], oh, start=True, stop=True).then_inc(cnt_ready, 1)

            def body(c, main, prev, prev2):
                if main and not prev2:
                    pe.wait_ge(onehot_ready, c + 1)
                if prev and not prev2:
                    pe.wait_ge(ld_g, 48)
                for q in range(GROUPS):
                    if main:
                        for k in ((0, 1) if q == 0 else (q + 1,)):
                            if k < GROUPS:
                                expand_decay(c, k)
                        expand_input(c, q)
                        if q >= T_SUM and (q - T_SUM) % 4 == 0:
                            sum_states(c, (q - T_SUM) // 4)
                    if prev:
                        if q < T_SUM and q % 4 == 0:
                            sum_states(c - 1, (q + GROUPS - T_SUM) // 4)
                        for j in range(TILES):
                            if q == T_PROJECT[j]:
                                project_out(c - 1, j)
                        if q == T_BASE:
                            row_base_terms(c - 1)
                        for k in range(2):
                            if q == T_TURN[k]:
                                turn_x2(c - 1, k)
                            if q == T_LOGITS[k]:
                                logits(c - 1, k)
                    if prev2 and q + GROUPS == T_COUNT:
                        count_pairs(c - 2)

            chunks(pe, body)
            pe.drain().then_inc(scan_phase_over, 1)
            pe.wait_ge(scan_phase_over, 3)
            pe.wait_ge(tiles_ready, 1)
            pe.wait_ge(w_lo, PIECES * (EXPERTS - 1))

            def expert_of(i):
                return pe.value_load(tile_expert[0:1, bass.ds(i, 1)], min_val=0, max_val=NE - 1)

            def turn_rows(i, s, m):
                pe.wait_ge(f_in[s], 16 * (m + 1))
                wait(pe, f_xT, i)
                for k in range(2):
                    halves = x_in[s][:, k, 0:HID].bitcast(f16)
                    for l in range(2):
                        for c in range(2):
                            last = nc.tensor.transpose(xTp16[:, l, c, k * P:(k + 1) * P],
                                                       halves[:, l * HID + c * P:l * HID + (c + 1) * P], ident16[:, :])
                last.then_inc(f_tp, 1)

            def first_product(i, s):
                e = expert_of(i)
                pe.wait_ge(f_xT, i + 1)
                for j in range(8):
                    b = j // 2
                    if j % 2 == 0:
                        wait(pe, f_g, 4 * (i - 1) + b + 1)
                    o = bank[b][:, (j % 2) * TT:(j % 2 + 1) * TT]
                    for c in range(2):
                        at = c * FFN + j * P
                        wh, wl = wsec(e, W1H, at, P), wsec(e, W1L, at, P)
                        mm(o, wh, x_T[s][:, 0, c, :], start=(c == 0), stop=False)
                        mm(o, wh, x_T[s][:, 1, c, :], start=False, stop=False)
                        last = mm(o, wl, x_T[s][:, 0, c, :], start=False, stop=(c == 1))
                    if j % 2 == 1:
                        last.then_inc(f_h, 1)

            def second_product(i, s):
                e = expert_of(i)
                pe.wait_ge(f_lo, 4 * i + 4)
                wait(pe, f_ys, i - FR + 1)
                for k in range(2):
                    o = yb[s][:, k * HID:(k + 1) * HID]
                    for j in range(8):
                        hh, hl = h_hi[s][:, j, k * P:(k + 1) * P], h_lo[s][:, j, k * P:(k + 1) * P]
                        wh, wl = wsec(e, W2H, j * HID, HID), wsec(e, W2L, j * HID, HID)
                        mm(o, hh, wh, start=(j == 0), stop=False)
                        mm(o, hh, wl, start=False, stop=False)
                        last = mm(o, hl, wh, start=False, stop=(j == 7))
                last.then_inc(f_y, 1)

            turn_rows(0, 0, 0)
            first_product(0, 0)
            turn_rows(1, 1, 0)

            def next_tiles(m, u):
                i1, s1, _ = ahead(m, u, 1)
                i2, s2, m2 = ahead(m, u, 2)
                if not isinstance(m, int):
                    pe.wait_ge(w_lo, PIECES * EXPERTS)
                first_product(i1, s1)
                turn_rows(i2, s2, m2)

            def this_tile(m, u):
                i, s, _ = ahead(m, u, 0)
                second_product(i, s)

            tile_steps(pe, (next_tiles, 1), (this_tile, 0))


def kernel(**inputs):
    import numpy as np
    import concourse.bacc as bacc
    from concourse.bass_utils import run_bass_kernel_spmd

    order = np.array(channel_order())
    a = {k: np.asarray(v) for k, v in inputs.items()}
    z_rows = HID + order
    w_in = np.concatenate([a["L0_attn_w_in"][:HID], a["L0_attn_w_in"][z_rows]], axis=0)
    b_in = np.concatenate([a["L0_attn_b_in"][:HID], a["L0_attn_b_in"][z_rows]], axis=0)
    laid = {
        "x_tok": a["x"], "level_emb": a["L0_tok_level_emb"], "w_inT": w_in.T, "b_in": b_in,
        "w_dtT": a["L0_attn_w_dt"].T, "b_dt": a["L0_attn_b_dt"], "a_log": a["L0_attn_A_log"],
        "w_BT": a["L0_attn_w_B"].T, "b_B": a["L0_attn_b_B"], "w_CT": a["L0_attn_w_C"].T, "b_C": a["L0_attn_b_C"],
        "d_skip": a["L0_attn_D"], "w_outT": a["L0_attn_w_out"].T[order], "b_out": a["L0_attn_b_out"],
        "gamma": a["L0_attn_gamma"], "beta": a["L0_attn_beta"], "router_wT": a["L0_ffn_router_w"].T,
        "w1": a["L0_ffn_w1"], "w2": a["L0_ffn_w2"],
    }
    nc = bacc.Bacc("TRN2", target_bir_lowering=False, num_devices=1)
    arrays, args = {}, []
    for name, value in laid.items():
        value = np.ascontiguousarray(value)
        arrays[f"in_{name}"] = value
        args.append(nc.dram_tensor(f"in_{name}", value.shape, mybir.dt.from_np(value.dtype), kind="ExternalInput").ap())
    out = nc.dram_tensor("out_0", (NTOK + TT, HID), mybir.dt.float32, kind="ExternalOutput").ap()
    program(nc, *args, out)
    r = run_bass_kernel_spmd(nc, [arrays], core_ids=[0])
    return r.results[0]["out_0"][:NTOK].reshape(BATCH, SEQ, HID)
```
